# Optimizing a Trainium2 kernel written in Bass

```python
import numpy as np
import jax
import jax.numpy as jnp

def _softmax(x, axis=-1):
    return jax.nn.softmax(x, axis=axis)

def _gelu(x):
    return jax.nn.gelu(x, approximate=True)

def _silu(x):
    return jax.nn.silu(x)

def _sigmoid(x):
    return jax.nn.sigmoid(x)

def _layernorm(x, axis=-1, eps=1e-05):
    m = jnp.mean(x, axis=axis, keepdims=True)
    v = jnp.var(x, axis=axis, keepdims=True)
    return (x - m) / jnp.sqrt(v + eps)

def _scatter_add(tgt, idx, src, axis=0):
    return tgt.at[idx].add(src)

def _segment_sum(src, seg, n):
    return jax.ops.segment_sum(src, seg, n)
kernel_name = 'mk_xattn_ffn_d2_seqx_r8_ffd60a'

def setup_inputs(seed: int=0):
    np.random.seed(seed)
    _w = jnp.asarray

    def _rec_inputs():
        import jax
        import jax.numpy as jnp
        _rk = jax.random.key(seed)
        x = -0.0003929 + 0.9999 * jax.random.normal(jax.random.fold_in(_rk, 1), (8, 56, 256), jnp.float32)
        _lenS = 56 - jax.random.randint(jax.random.fold_in(_rk, 7), (8,), 0, max(1, 56 // 4) + 1, jnp.int32)
        _lenS2 = 1500 - jax.random.randint(jax.random.fold_in(_rk, 8), (8,), 0, max(1, 1500 // 4) + 1, jnp.int32)
        _ctx_2048P = jax.random.normal(jax.random.fold_in(_rk, 11), (8, 16, 256), jnp.float32)
        _ctx_2048c = jax.random.dirichlet(jax.random.fold_in(_rk, 511), 0.3 * jnp.ones((16,), jnp.float32), (8, 1500))
        _ctx_2048t = jnp.einsum('bsk,bkd->bsd', _ctx_2048c, _ctx_2048P)
        _ctx_2048t = _ctx_2048t * jax.lax.rsqrt(jnp.mean(jnp.square(_ctx_2048t)) + 1e-12) * 0.953939
        ctx_2048 = 4.13588e-05 + 0.999923 * (_ctx_2048t + 0.3 * jax.random.normal(jax.random.fold_in(_rk, 611), (8, 1500, 256), jnp.float32))
        _validS = jnp.arange(56)[None, :] < _lenS[:, None]
        _validS2 = jnp.arange(1500)[None, :] < _lenS2[:, None]
        _causal = jnp.tril(jnp.ones((56, 56), dtype=bool))
        mask_BxS2_ff1 = jnp.where(jnp.ones((8, 1500), dtype=bool), 1.0, 0.0).astype(jnp.float32)
        return (x, ctx_2048, mask_BxS2_ff1)
    x, ctx_2048, mask_BxS2_ff1 = _rec_inputs()

    def _L0_xattn_setup():
        import jax, jax.numpy as jnp
        import numpy as np
        HIDDEN = 256
        N_HEADS = 16
        N_KV_HEADS = 4
        HEAD_DIM = 128
        EPS = 1e-06

        def rms_norm(x, w, eps=EPS):
            xf = x.astype(jnp.float32)
            var = jnp.mean(xf * xf, axis=-1, keepdims=True)
            return w * (xf * jax.lax.rsqrt(var + eps)).astype(x.dtype)
        key = jax.random.key(seed)
        ks = jax.random.split(key, 8)
        B, S, S_ENC = (4, 256, 128)
        inner = N_HEADS * HEAD_DIM
        kv_dim = N_KV_HEADS * HEAD_DIM
        s = 0.02
        return {'hidden_states': jax.random.normal(ks[0], (B, S, HIDDEN), jnp.float32), 'encoder_hidden_states': jax.random.normal(ks[1], (B, S_ENC, HIDDEN), jnp.float32), 'Wq': jax.random.normal(ks[2], (HIDDEN, inner), jnp.float32) * s, 'Wk': jax.random.normal(ks[3], (HIDDEN, kv_dim), jnp.float32) * s, 'Wv': jax.random.normal(ks[4], (HIDDEN, kv_dim), jnp.float32) * s, 'Wo': jax.random.normal(ks[5], (inner, HIDDEN), jnp.float32) * s, 'q_norm_w': jnp.ones((HEAD_DIM,), jnp.float32), 'k_norm_w': jnp.ones((HEAD_DIM,), jnp.float32)}
    _L0_xattn_all = _L0_xattn_setup()
    _L0_xattn_in = {k: v for k, v in _L0_xattn_all.items() if k in ('Wq', 'Wk', 'Wv', 'Wo', 'q_norm_w', 'k_norm_w')}
    del _L0_xattn_all

    def _L0_ffn_setup():
        import jax, jax.numpy as jnp
        import numpy as np
        B, S, D = (4, 64, 256)
        E, K, H = (8, 2, 176)
        HS = 2 * 176
        ALPHA = 0.001
        W_SCALE = 0.02

        def _moe_forward(hidden_states, gate_w, w_gate, w_up, w_down, sw_gate, sw_up, sw_down):
            b, s, d = hidden_states.shape
            x = hidden_states.reshape(-1, d)
            T = x.shape[0]
            logits = x @ gate_w
            scores = jax.nn.softmax(logits, axis=-1)
            topk_w, topk_idx = jax.lax.top_k(scores, K)
            mask = jax.nn.one_hot(topk_idx, E, dtype=scores.dtype).sum(axis=1)
            ce = mask.mean(axis=0)
            Pi = scores.mean(axis=0)
            aux_loss = (Pi * ce * E).sum() * ALPHA
            comb = jnp.zeros((T, E), dtype=x.dtype)
            comb = comb.at[jnp.arange(T)[:, None], topk_idx].add(topk_w)
            g = jax.nn.silu(jnp.einsum('td,edh->teh', x, w_gate)) * jnp.einsum('td,edh->teh', x, w_up)
            routed = jnp.einsum('teh,ehd,te->td', g, w_down, comb)
            shared = jax.nn.silu(x @ sw_gate) * (x @ sw_up) @ sw_down
            out = (routed + shared).reshape(b, s, d)
            return (out, aux_loss)
        key = jax.random.key(seed)
        ks = jax.random.split(key, 8)
        rn = lambda k, sh: jax.random.normal(k, sh, dtype=jnp.float32)
        return {'hidden_states': rn(ks[0], (B, S, D)), 'gate_w': rn(ks[1], (D, E)) * W_SCALE, 'w_gate': rn(ks[2], (E, D, H)) * W_SCALE, 'w_up': rn(ks[3], (E, D, H)) * W_SCALE, 'w_down': rn(ks[4], (E, H, D)) * W_SCALE, 'sw_gate': rn(ks[5], (D, HS)) * W_SCALE, 'sw_up': rn(ks[6], (D, HS)) * W_SCALE, 'sw_down': rn(ks[7], (HS, D)) * W_SCALE}
    _L0_ffn_all = _L0_ffn_setup()
    _L0_ffn_in = {k: v for k, v in _L0_ffn_all.items() if k in ('gate_w', 'w_gate', 'w_up', 'w_down', 'sw_gate', 'sw_up', 'sw_down')}
    del _L0_ffn_all

    def _L1_xattn_setup():
        import jax, jax.numpy as jnp
        import numpy as np
        H = 256
        NH = 16
        HD = H // NH
        FD = 64
        key = jax.random.key(seed)
        ks = jax.random.split(key, 12)
        B, S = (4, 512)
        s = 1.0 / np.sqrt(H)
        sf = 1.0 / np.sqrt(HD)
        return {'query': jax.random.normal(ks[0], (B, S, H), jnp.float32), 'key': jax.random.normal(ks[1], (B, S, H), jnp.float32), 'value': jax.random.normal(ks[2], (B, S, H), jnp.float32), 'attention_mask': jnp.ones((B, S), jnp.float32), 'Wq': jax.random.normal(ks[3], (H, H), jnp.float32) * s, 'bq': jnp.zeros((H,), jnp.float32), 'Wk': jax.random.normal(ks[4], (H, H), jnp.float32) * s, 'bk': jnp.zeros((H,), jnp.float32), 'Wv': jax.random.normal(ks[5], (H, H), jnp.float32) * s, 'bv': jnp.zeros((H,), jnp.float32), 'Wqf': jax.random.normal(ks[6], (FD, HD), jnp.float32) * sf, 'Wkf': jax.random.normal(ks[7], (FD, HD), jnp.float32) * sf, 'Wo': jax.random.normal(ks[8], (H, H), jnp.float32) * s, 'bo': jnp.zeros((H,), jnp.float32)}
    _L1_xattn_all = _L1_xattn_setup()
    _L1_xattn_in = {k: v for k, v in _L1_xattn_all.items() if k in ('Wq', 'bq', 'Wk', 'bk', 'Wv', 'bv', 'Wqf', 'Wkf', 'Wo', 'bo')}
    del _L1_xattn_all

    def _L1_ffn_setup():
        import jax, jax.numpy as jnp
        import numpy as np
        E = 8
        TOP_K = 2
        H = 256
        I_MOE = 176
        I_SH = 704
        B, S = (2, 256)

        def _moe_forward(hidden_states, router_weight, gate_up_proj, down_proj, sh_gate_w, sh_up_w, sh_down_w, shared_gate_w):
            b, s, h = hidden_states.shape
            x = hidden_states.reshape(-1, h)
            shared = jnp.einsum('ti,hi->th', jax.nn.silu(x @ sh_gate_w.T) * (x @ sh_up_w.T), sh_down_w)
            logits = x @ router_weight.T
            probs = jax.nn.softmax(logits.astype(jnp.float32), axis=-1)
            top_v, top_i = jax.lax.top_k(probs, TOP_K)
            top_v = top_v / top_v.sum(axis=-1, keepdims=True)
            combine = (jax.nn.one_hot(top_i, E, dtype=top_v.dtype) * top_v[..., None]).sum(axis=1)
            out = jnp.zeros_like(x)
            for e in range(E):
                gu = x @ gate_up_proj[e].T
                gate, up = (gu[:, :I_MOE], gu[:, I_MOE:])
                cur = jax.nn.silu(gate) * up @ down_proj[e].T
                out = out + cur * combine[:, e:e + 1]
            out = out + jax.nn.sigmoid(x @ shared_gate_w.T) * shared
            return out.reshape(b, s, h)
        key = jax.random.key(seed)
        ks = jax.random.split(key, 8)
        scale = 0.02
        return {'hidden_states': jax.random.normal(ks[0], (B, S, H), dtype=jnp.float32), 'router_weight': jax.random.normal(ks[1], (E, H), dtype=jnp.float32) * scale, 'gate_up_proj': jax.random.normal(ks[2], (E, 2 * I_MOE, H), dtype=jnp.float32) * scale, 'down_proj': jax.random.normal(ks[3], (E, H, I_MOE), dtype=jnp.float32) * scale, 'sh_gate_w': jax.random.normal(ks[4], (I_SH, H), dtype=jnp.float32) * scale, 'sh_up_w': jax.random.normal(ks[5], (I_SH, H), dtype=jnp.float32) * scale, 'sh_down_w': jax.random.normal(ks[6], (H, I_SH), dtype=jnp.float32) * scale, 'shared_gate_w': jax.random.normal(ks[7], (1, H), dtype=jnp.float32) * scale}
    _L1_ffn_all = _L1_ffn_setup()
    _L1_ffn_in = {k: v for k, v in _L1_ffn_all.items() if k in ('router_weight', 'gate_up_proj', 'down_proj', 'sh_gate_w', 'sh_up_w', 'sh_down_w', 'shared_gate_w')}
    del _L1_ffn_all
    return {'x': x, 'ctx_2048': ctx_2048, 'mask_BxS2_ff1': mask_BxS2_ff1, 'L0_xattn_Wq': _L0_xattn_in['Wq'], 'L0_xattn_Wk': _L0_xattn_in['Wk'], 'L0_xattn_Wv': _L0_xattn_in['Wv'], 'L0_xattn_Wo': _L0_xattn_in['Wo'], 'L0_xattn_q_norm_w': _L0_xattn_in['q_norm_w'], 'L0_xattn_k_norm_w': _L0_xattn_in['k_norm_w'], 'L0_ffn_gate_w': _L0_ffn_in['gate_w'], 'L0_ffn_w_gate': _L0_ffn_in['w_gate'], 'L0_ffn_w_up': _L0_ffn_in['w_up'], 'L0_ffn_w_down': _L0_ffn_in['w_down'], 'L0_ffn_sw_gate': _L0_ffn_in['sw_gate'], 'L0_ffn_sw_up': _L0_ffn_in['sw_up'], 'L0_ffn_sw_down': _L0_ffn_in['sw_down'], 'L1_xattn_Wq': _L1_xattn_in['Wq'], 'L1_xattn_bq': _L1_xattn_in['bq'], 'L1_xattn_Wk': _L1_xattn_in['Wk'], 'L1_xattn_bk': _L1_xattn_in['bk'], 'L1_xattn_Wv': _L1_xattn_in['Wv'], 'L1_xattn_bv': _L1_xattn_in['bv'], 'L1_xattn_Wqf': _L1_xattn_in['Wqf'], 'L1_xattn_Wkf': _L1_xattn_in['Wkf'], 'L1_xattn_Wo': _L1_xattn_in['Wo'], 'L1_xattn_bo': _L1_xattn_in['bo'], 'L1_ffn_router_weight': _L1_ffn_in['router_weight'], 'L1_ffn_gate_up_proj': _L1_ffn_in['gate_up_proj'], 'L1_ffn_down_proj': _L1_ffn_in['down_proj'], 'L1_ffn_sh_gate_w': _L1_ffn_in['sh_gate_w'], 'L1_ffn_sh_up_w': _L1_ffn_in['sh_up_w'], 'L1_ffn_sh_down_w': _L1_ffn_in['sh_down_w'], 'L1_ffn_shared_gate_w': _L1_ffn_in['shared_gate_w']}

def reference(x, ctx_2048, mask_BxS2_ff1, L0_xattn_Wq, L0_xattn_Wk, L0_xattn_Wv, L0_xattn_Wo, L0_xattn_q_norm_w, L0_xattn_k_norm_w, L0_ffn_gate_w, L0_ffn_w_gate, L0_ffn_w_up, L0_ffn_w_down, L0_ffn_sw_gate, L0_ffn_sw_up, L0_ffn_sw_down, L1_xattn_Wq, L1_xattn_bq, L1_xattn_Wk, L1_xattn_bk, L1_xattn_Wv, L1_xattn_bv, L1_xattn_Wqf, L1_xattn_Wkf, L1_xattn_Wo, L1_xattn_bo, L1_ffn_router_weight, L1_ffn_gate_up_proj, L1_ffn_down_proj, L1_ffn_sh_gate_w, L1_ffn_sh_up_w, L1_ffn_sh_down_w, L1_ffn_shared_gate_w):
    import jax
    import jax.numpy as jnp

    def _L0_xattn_ref(hidden_states, encoder_hidden_states, Wq, Wk, Wv, Wo, q_norm_w, k_norm_w):
        import jax, jax.numpy as jnp
        import numpy as np
        HIDDEN = 256
        N_HEADS = 16
        N_KV_HEADS = 4
        HEAD_DIM = 128
        EPS = 1e-06

        def rms_norm(x, w, eps=EPS):
            xf = x.astype(jnp.float32)
            var = jnp.mean(xf * xf, axis=-1, keepdims=True)
            return w * (xf * jax.lax.rsqrt(var + eps)).astype(x.dtype)
        B, S, _ = hidden_states.shape
        S_enc = encoder_hidden_states.shape[1]
        groups = N_HEADS // N_KV_HEADS
        scale = 1.0 / HEAD_DIM ** 0.5
        q = (hidden_states @ Wq).reshape(B, S, N_HEADS, HEAD_DIM)
        k = (encoder_hidden_states @ Wk).reshape(B, S_enc, N_KV_HEADS, HEAD_DIM)
        v = (encoder_hidden_states @ Wv).reshape(B, S_enc, N_KV_HEADS, HEAD_DIM)
        q = rms_norm(q, q_norm_w)
        k = rms_norm(k, k_norm_w)
        k = jnp.repeat(k, groups, axis=2)
        v = jnp.repeat(v, groups, axis=2)
        scores = jnp.einsum('bqhd,bkhd->bhqk', q, k) * scale
        probs = jax.nn.softmax(scores, axis=-1)
        out = jnp.einsum('bhqk,bkhd->bqhd', probs, v)
        out = out.reshape(B, S, N_HEADS * HEAD_DIM)
        return out @ Wo

    def _L0_ffn_ref(hidden_states, gate_w, w_gate, w_up, w_down, sw_gate, sw_up, sw_down):
        import jax, jax.numpy as jnp
        import numpy as np
        B, S, D = (4, 64, 256)
        E, K, H = (8, 2, 176)
        HS = 2 * 176
        ALPHA = 0.001
        W_SCALE = 0.02

        def _moe_forward(hidden_states, gate_w, w_gate, w_up, w_down, sw_gate, sw_up, sw_down):
            b, s, d = hidden_states.shape
            x = hidden_states.reshape(-1, d)
            T = x.shape[0]
            logits = x @ gate_w
            scores = jax.nn.softmax(logits, axis=-1)
            topk_w, topk_idx = jax.lax.top_k(scores, K)
            mask = jax.nn.one_hot(topk_idx, E, dtype=scores.dtype).sum(axis=1)
            ce = mask.mean(axis=0)
            Pi = scores.mean(axis=0)
            aux_loss = (Pi * ce * E).sum() * ALPHA
            comb = jnp.zeros((T, E), dtype=x.dtype)
            comb = comb.at[jnp.arange(T)[:, None], topk_idx].add(topk_w)
            g = jax.nn.silu(jnp.einsum('td,edh->teh', x, w_gate)) * jnp.einsum('td,edh->teh', x, w_up)
            routed = jnp.einsum('teh,ehd,te->td', g, w_down, comb)
            shared = jax.nn.silu(x @ sw_gate) * (x @ sw_up) @ sw_down
            out = (routed + shared).reshape(b, s, d)
            return (out, aux_loss)
        out, _aux = _moe_forward(hidden_states, gate_w, w_gate, w_up, w_down, sw_gate, sw_up, sw_down)
        return out

    def _L1_xattn_ref(query, key, value, attention_mask, Wq, bq, Wk, bk, Wv, bv, Wqf, Wkf, Wo, bo):
        import jax, jax.numpy as jnp
        import numpy as np
        H = 256
        NH = 16
        HD = H // NH
        FD = 64
        B, Sq, _ = query.shape
        Sk = key.shape[1]

        def heads(x, W, b, S):
            return (x @ W.T + b).reshape(B, S, NH, HD).transpose(0, 2, 1, 3)
        q = heads(query, Wq, bq, Sq)
        k = heads(key, Wk, bk, Sk)
        v = heads(value, Wv, bv, Sk)
        q_prime = jax.nn.relu(jnp.einsum('bhnd,fd->bhnf', q, Wqf))
        k_prime = jax.nn.relu(jnp.einsum('bhnd,fd->bhnf', k, Wkf))
        k_prime = k_prime * attention_mask[:, None, :, None]
        kv = jnp.einsum('bhnf,bhne->bhfe', k_prime, v)
        qkv = jnp.einsum('bhmf,bhfe->bhme', q_prime, kv)
        k_sum = jnp.sum(k_prime, axis=2)
        qk_sum = jnp.einsum('bhmf,bhf->bhm', q_prime, k_sum)[..., None]
        out = qkv / (qk_sum + 1e-08)
        out = out.transpose(0, 2, 1, 3).reshape(B, Sq, H)
        return out @ Wo.T + bo

    def _L1_ffn_ref(hidden_states, router_weight, gate_up_proj, down_proj, sh_gate_w, sh_up_w, sh_down_w, shared_gate_w):
        import jax, jax.numpy as jnp
        import numpy as np
        E = 8
        TOP_K = 2
        H = 256
        I_MOE = 176
        I_SH = 704
        B, S = (2, 256)

        def _moe_forward(hidden_states, router_weight, gate_up_proj, down_proj, sh_gate_w, sh_up_w, sh_down_w, shared_gate_w):
            b, s, h = hidden_states.shape
            x = hidden_states.reshape(-1, h)
            shared = jnp.einsum('ti,hi->th', jax.nn.silu(x @ sh_gate_w.T) * (x @ sh_up_w.T), sh_down_w)
            logits = x @ router_weight.T
            probs = jax.nn.softmax(logits.astype(jnp.float32), axis=-1)
            top_v, top_i = jax.lax.top_k(probs, TOP_K)
            top_v = top_v / top_v.sum(axis=-1, keepdims=True)
            combine = (jax.nn.one_hot(top_i, E, dtype=top_v.dtype) * top_v[..., None]).sum(axis=1)
            out = jnp.zeros_like(x)
            for e in range(E):
                gu = x @ gate_up_proj[e].T
                gate, up = (gu[:, :I_MOE], gu[:, I_MOE:])
                cur = jax.nn.silu(gate) * up @ down_proj[e].T
                out = out + cur * combine[:, e:e + 1]
            out = out + jax.nn.sigmoid(x @ shared_gate_w.T) * shared
            return out.reshape(b, s, h)
        return _moe_forward(hidden_states, router_weight, gate_up_proj, down_proj, sh_gate_w, sh_up_w, sh_down_w, shared_gate_w)
    x = x + _L0_xattn_ref(_layernorm(x, axis=-1), ctx_2048, L0_xattn_Wq, L0_xattn_Wk, L0_xattn_Wv, L0_xattn_Wo, L0_xattn_q_norm_w, L0_xattn_k_norm_w)
    x = x + _L0_ffn_ref(_layernorm(x, axis=-1), L0_ffn_gate_w, L0_ffn_w_gate, L0_ffn_w_up, L0_ffn_w_down, L0_ffn_sw_gate, L0_ffn_sw_up, L0_ffn_sw_down)
    x = x + _L1_xattn_ref(_layernorm(x, axis=-1), ctx_2048, ctx_2048, mask_BxS2_ff1, L1_xattn_Wq, L1_xattn_bq, L1_xattn_Wk, L1_xattn_bk, L1_xattn_Wv, L1_xattn_bv, L1_xattn_Wqf, L1_xattn_Wkf, L1_xattn_Wo, L1_xattn_bo)
    x = x + _L1_ffn_ref(_layernorm(x, axis=-1), L1_ffn_router_weight, L1_ffn_gate_up_proj, L1_ffn_down_proj, L1_ffn_sh_gate_w, L1_ffn_sh_up_w, L1_ffn_sh_down_w, L1_ffn_shared_gate_w)
    return x

_drawn_inputs = setup_inputs


def setup_inputs(seed=0):
    import zlib

    import numpy as np

    out = dict(_drawn_inputs(seed))
    spreads = {'L0_xattn_q_norm_w': (1.0, 0.6),
     'L0_xattn_k_norm_w': (1.0, 0.6),
     'L1_xattn_bq': (0.0, 2.0),
     'L1_xattn_bk': (0.0, 2.0),
     'L1_xattn_bv': (0.0, 0.1),
     'L1_xattn_bo': (0.0, 0.1)}
    factors = {'L0_ffn_gate_w': 8.0,
     'L0_ffn_w_gate': 8.0,
     'L0_ffn_w_up': 8.0,
     'L0_ffn_w_down': 8.0,
     'L0_ffn_sw_gate': 3.277,
     'L0_ffn_sw_up': 3.237,
     'L0_ffn_sw_down': 3.26,
     'L1_ffn_router_weight': 7.38,
     'L1_ffn_gate_up_proj': 6.356,
     'L1_ffn_down_proj': 6.375,
     'L1_ffn_sh_gate_w': 4.53,
     'L1_ffn_sh_up_w': 4.507,
     'L1_ffn_sh_down_w': 4.497,
     'L1_ffn_shared_gate_w': 8.0,
     'L1_xattn_Wq': 9.134,
     'L1_xattn_Wk': 11.04,
     'L1_xattn_Wqf': 9.24,
     'L1_xattn_Wkf': 13.601}
    for name, (base, spread) in spreads.items():
        noise = np.random.default_rng([zlib.crc32(name.encode()), seed]).standard_normal(out[name].shape)
        drawn = base * np.exp(spread * noise) if base else spread * noise
        out[name] = jnp.asarray(drawn.astype(out[name].dtype))
    for name, factor in factors.items():
        out[name] = (out[name] * factor).astype(out[name].dtype)
    return out
```

```python
from contextlib import ExitStack

import concourse.bass as bass
from concourse import mybir

F32 = mybir.dt.float32
F32R = mybir.dt.float32r
ALU = mybir.AluOpType
ACT = mybir.ActivationFunctionType
AX = mybir.AxisListType.X

B = 8
S = 56
D = 256
DC = D // 128
NTOK = B * S
TT = 4
TP = NTOK // TT
SK = 1500
KC = 3
CH = SK // KC
KT = 12
KP = SK // KT
TPC = KT // KC

NH = 16
HD = 128
G = 4
HG = NH // G
QG = HG * S
U = 2
QU = 2 * QG
NJ = NH * S // TP

HE = 16
FD = 64
FEAT = NH * FD
KG = 6
GH = 3
GF = GH * FD
GV = GH * HE
VW = 2 * GV + 2
SUMS = [(i * 2 * GF, min((i + 1) * 2 * GF, FEAT)) for i in range(KG // 2)]
RV = HE + 1

E = 8
HB = 88
EB = 2

SHARED0 = 4
SHARED1 = 8

LN_EXP = "natural_log_exp_and_others"

LN_EPS = 1e-5
RMS_EPS = 1e-6


def wait(eng, sem, value):
    if isinstance(value, int) and value <= 0:
        return
    eng.wait_ge(sem, value)


def identity(nc, pool, tile, n, memset_done, ident_done):
    nc.gpsimd.memset(tile, 0.0).then_inc(memset_done, 1)
    pool.wait_ge(memset_done, 1)
    nc.gpsimd.affine_select(out=tile, in_=tile, compare_op=ALU.not_equal, fill=1.0, base=0,
                            pattern=[[-1, n]], channel_multiplier=1).then_inc(ident_done, 1)


class Phase:

    def __init__(self, nc, ctx, name):
        self.nc, self.ctx, self.name, self.sems = nc, ctx, name, []
        ctx.callback(self.clear)

    def clear(self):
        if self.sems:
            self.nc.clear_and_free_semaphores(self.sems)
            self.nc.all_engine_barrier()

    def sb(self, name, shape, dt=F32):
        return self.ctx.enter_context(self.nc.sbuf_tensor(f"{self.name}_{name}", shape, dt))

    def ps(self, name, shape):
        return self.ctx.enter_context(self.nc.psum_tensor(f"{self.name}_{name}", shape, F32))

    def sem(self, name):
        self.sems.append(self.nc.alloc_semaphore(f"{self.name}_{name}"))
        return self.sems[-1]


def mm3(nc, out, w_hi, w_lo, x_hi, x_lo, start, stop):
    nc.tensor.matmul(out, w_lo, x_hi, start=start, stop=False, skip_group_check=True)
    nc.tensor.matmul(out, w_hi, x_lo, start=False, stop=False, skip_group_check=True)
    return nc.tensor.matmul(out, w_hi, x_hi, start=False, stop=stop, skip_group_check=True)


def layernorm_transposed(nc, name, x, xnT, ident, load=None):
    with ExitStack() as ctx:
        p = Phase(nc, ctx, name)
        stats = p.sb("stats", [TP, TT, 6])
        mv = p.sb("mv", [TP, TT, 2])
        var = p.sb("var", [TP, TT])
        rstd = p.sb("rstd", [TP, TT])
        tmp = p.sb("tmp", [TP, TT])
        xn = p.sb("xn", [TP, TT, D])
        eps = p.sb("eps", [128, 1])
        turned = p.ps("turned", [128, 2, 512])
        x_here, stats_done, mv_done, var_done, guess_done = (p.sem(s) for s in (
            "x_here", "stats_done", "mv_done", "var_done", "guess_done"))
        newton, xn_done, turned_done, copied = (p.sem(s) for s in ("newton", "xn_done", "turned_done", "copied"))
        block = ctx.enter_context(nc.Block())

        if load is not None:
            @block.sync
            def _(sp):
                for src, dst in load:
                    sp.dma_start(dst, src).then_inc(x_here, 16)

        @block.vector
        def _(dve):
            nc.vector.memset(eps[:], 0.0).then_inc(var_done, 1)
            if load is not None:
                dve.wait_ge(x_here, 16 * len(load))
            for t in range(TT):
                nc.vector.bn_stats(stats[:, t, :], x[:, t, :]).then_inc(stats_done, 1)
            for t in range(TT):
                dve.wait_ge(stats_done, t + 1)
                nc.vector.bn_aggr(mv[:, t, :], stats[:, t, :]).then_inc(mv_done, 1)
            dve.wait_ge(mv_done, TT)
            nc.vector.tensor_scalar(var[:], mv[:, :, 1], LN_EPS, None, ALU.add).then_inc(var_done, 1)
            dve.wait_ge(guess_done, 2)
            nc.vector.tensor_tensor(tmp[:], rstd[:], rstd[:], ALU.mult).then_inc(newton, 1)
            dve.wait_ge(newton, 1)
            nc.vector.tensor_tensor(tmp[:], tmp[:], var[:], ALU.mult).then_inc(newton, 1)
            dve.wait_ge(newton, 2)
            nc.vector.tensor_scalar(tmp[:], tmp[:], -0.5, 1.5, ALU.mult, ALU.add).then_inc(newton, 1)
            dve.wait_ge(newton, 3)
            nc.vector.tensor_tensor(rstd[:], rstd[:], tmp[:], ALU.mult).then_inc(newton, 1)
            dve.wait_ge(newton, 4)
            for t in range(TT):
                nc.vector.tensor_scalar(xn[:, t, :], x[:, t, :], mv[:, t, 0:1], rstd[:, t:t + 1],
                                        ALU.subtract, ALU.mult).then_inc(xn_done, 1)
            for c in range(DC):
                dve.wait_ge(turned_done, c + 1)
                nc.vector.tensor_copy(xnT[:, c, :], turned[:, c, 0:NTOK]).then_inc(copied, 1)
            dve.wait_ge(copied, DC)

        @block.scalar
        def _(act):
            nc.scalar.preload_act_table_set(LN_EXP)
            act.wait_ge(var_done, 2)
            nc.scalar.activation(rstd[:], var[:], ACT.Ln, bias=eps[0:TP, 0:1]).then_inc(guess_done, 1)
            act.wait_ge(guess_done, 1)
            nc.scalar.activation(rstd[:], rstd[:], ACT.Exp, scale=-0.5, bias=eps[0:TP, 0:1]).then_inc(guess_done, 1)

        @block.tensor
        def _(pe):
            for c in range(DC):
                for t in range(TT):
                    if c == 0:
                        pe.wait_ge(xn_done, t + 1)
                    last = nc.tensor.transpose(turned[:, c, t * TP:(t + 1) * TP],
                                               xn[:, t, c * 128:(c + 1) * 128], ident[0:TP, 0:TP])
                last.then_inc(turned_done, 1)


def queries(nc, xnT, qT, wq_dram, qw_dram, kw_dram, mean_mat):
    with ExitStack() as ctx:
        p = Phase(nc, ctx, "qry")
        wq = p.sb("wq", [128, DC, NH * HD])
        nw = p.sb("nw", [128, 4])
        eps = p.sb("eps", [128, 2])
        sq = p.sb("sq", [128, 2, NTOK])
        rs = p.sb("rs", [128, 2, NTOK])
        proj = p.ps("proj", [128, 3, 512])
        mean = p.ps("mean", [128, 2, 512])
        loaded, eps_set, w_done, proj_done, sq_done, mean_done = (p.sem(s) for s in (
            "loaded", "eps_set", "w_done", "proj_done", "sq_done", "mean_done"))
        ln_done, rs_done, q_done = (p.sem(s) for s in ("ln_done", "rs_done", "q_done"))
        block = ctx.enter_context(nc.Block())

        @block.sync
        def _(sp):
            sp.dma_start(wq[:], wq_dram.rearrange("(c p) n -> p c n", p=128)).then_inc(loaded, 16)
            sp.dma_start(nw[:, 0:1], qw_dram).then_inc(loaded, 16)
            sp.dma_start(nw[:, 1:2], kw_dram).then_inc(loaded, 16)

        @block.tensor
        def _(pe):
            pe.wait_ge(loaded, 48)

            def mean_square(h):
                pe.wait_ge(sq_done, h + 1)
                wait(pe, ln_done, h - 1)
                nc.tensor.matmul(mean[:, h % 2, 0:NTOK], mean_mat[:], sq[:, h % 2, :],
                                 start=True, stop=True).then_inc(mean_done, 1)

            for h in range(NH):
                wait(pe, q_done, h - 2)
                for c in range(DC):
                    last = nc.tensor.matmul(proj[:, h % 3, 0:NTOK], wq[:, c, h * HD:(h + 1) * HD],
                                            xnT[:, c, :], start=(c == 0), stop=(c == DC - 1))
                last.then_inc(proj_done, 1)
                if h >= 1:
                    mean_square(h - 1)
            mean_square(NH - 1)

        @block.scalar
        def _(act):
            nc.scalar.preload_act_table_set(LN_EXP)
            act.wait_ge(eps_set, 2)

            def rstd(h):
                act.wait_ge(mean_done, h + 1)
                wait(act, q_done, h - 1)
                nc.scalar.activation(rs[:, h % 2, :], mean[:, h % 2, 0:NTOK], ACT.Ln,
                                     bias=eps[:, 0:1]).then_inc(ln_done, 1)
                act.wait_ge(ln_done, h + 1)
                nc.scalar.activation(rs[:, h % 2, :], rs[:, h % 2, :], ACT.Exp, scale=-0.5,
                                     bias=eps[:, 1:2]).then_inc(rs_done, 1)

            for h in range(NH):
                act.wait_ge(proj_done, h + 1)
                wait(act, mean_done, h - 1)
                nc.scalar.activation(sq[:, h % 2, :], proj[:, h % 3, 0:NTOK], ACT.Square,
                                     bias=eps[:, 1:2]).then_inc(sq_done, 1)
                if h >= 1:
                    rstd(h - 1)
            rstd(NH - 1)

        @block.vector
        def _(dve):
            nc.vector.memset(eps[:, 0:1], RMS_EPS).then_inc(eps_set, 1)
            nc.vector.memset(eps[:, 1:2], 0.0).then_inc(eps_set, 1)
            dve.wait_ge(loaded, 48)
            nc.vector.scalar_tensor_tensor(nw[:, 2:3], nw[:, 0:1], HD ** -0.5, nw[:, 1:2],
                                           ALU.mult, ALU.mult).then_inc(w_done, 1)
            dve.wait_ge(w_done, 1)
            for h in range(NH):
                dve.wait_ge(rs_done, h + 1)
                nc.vector.scalar_tensor_tensor(qT[:, h, :], proj[:, h % 3, 0:NTOK], nw[:, 2:3],
                                               rs[:, h % 2, :], ALU.mult, ALU.mult).then_inc(q_done, 1)



def split_weights(nc, name, pairs):
    with ExitStack() as ctx:
        p = Phase(nc, ctx, name)
        raw = [p.sb(f"raw{i}", list(hi.shape)) for i, (_, hi, _) in enumerate(pairs)]
        loaded = [p.sem(f"loaded{i}") for i in range(len(pairs))]
        hi_done, lo_done = p.sem("hi_done"), p.sem("lo_done")
        block = ctx.enter_context(nc.Block())

        @block.sync
        def _(sp):
            for i, (src, _, _) in enumerate(pairs):
                sp.dma_start(raw[i][:], src).then_inc(loaded[i], 16)

        @block.scalar
        def _(act):
            for i, (_, hi, _) in enumerate(pairs):
                act.wait_ge(loaded[i], 16)
                nc.scalar.activation(hi[:], raw[i][:], ACT.Copy).then_inc(hi_done, 1)

        @block.vector
        def _(dve):
            for i, (_, hi, lo) in enumerate(pairs):
                dve.wait_ge(hi_done, i + 1)
                nc.vector.tensor_tensor(lo[:], raw[i][:], hi[:].bitcast(F32), ALU.subtract).then_inc(lo_done, 1)
            dve.wait_ge(lo_done, len(pairs))


def softmax_attention(nc, qT, rz, ctx_dram, ctxT_dram, wk_dram, wv_dram, mean_mat, ident):
    with ExitStack() as ctx:
        p = Phase(nc, ctx, "att")
        wk = [p.sb(f"wk{i}", [128, DC, G * HD], F32R) for i in range(2)]
        wv = [p.sb(f"wv{i}", [128, DC, G * HD], F32R) for i in range(2)]
        split_weights(nc, "attw", [(w.rearrange("(c p) n -> p c n", p=128), *halves)
                                   for w, halves in ((wk_dram, wk), (wv_dram, wv))])
        raw_t = p.sb("raw_t", [128, DC, SK])
        raw_n = p.sb("raw_n", [KP, 2, KT // 2, D])
        ct = [p.sb(f"ct{i}", [128, DC, SK], F32R) for i in range(2)]
        cn = [p.sb(f"cn{i}", [KP, KT, D], F32R) for i in range(2)]
        q = [p.sb(f"q{i}", [128, NH, S], F32R) for i in range(2)]
        kf = p.sb("kf", [128, 2, CH])
        k = [p.sb(f"k{i}", [128, 2, SK], F32R) for i in range(2)]
        sq = p.sb("sq", [128, 3, CH])
        rs = p.sb("rs", [128, 2, CH])
        pr = p.sb("pr", [TP, 4, SK])
        mx = p.sb("mx", [TP, 4, KC])
        nmx = p.sb("nmx", [TP, 4, 2])
        z = p.sb("z", [TP, NJ])
        pT = [p.sb(f"pT{i}", [KP, 2, QU], F32R) for i in range(2)]
        cs = [p.sb(f"cs{i}", [128, DC, QU], F32R) for i in range(2)]
        eps = p.sb("eps", [128, 2])
        proj = p.ps("proj", [128, 3, 512])
        mean = p.ps("mean", [128, 512])
        ring = p.ps("ring", [128, 2, 512])
        csum = p.ps("csum", [128, 2, 512])

        zeros = p.sb("zeros", [KP, D])
        eps_set, zeros_set = p.sem("eps_set"), p.sem("zeros_set")
        t_loaded = p.sem("t_loaded")
        n_loaded = [p.sem(f"n_loaded{i}") for i in range(2)]
        t_hi, t_lo, n_hi, n_lo, q_hi, q_lo = (p.sem(s) for s in ("t_hi", "t_lo", "n_hi", "n_lo", "q_hi", "q_lo"))
        proj_done, sq_done, mean_done, ln_done, rs_done = (p.sem(s) for s in (
            "proj_done", "sq_done", "mean_done", "ln_done", "rs_done"))
        k_full, k_hi, k_lo = (p.sem(s) for s in ("k_full", "k_hi", "k_lo"))
        ring_full, ring_free = p.sem("ring_full"), p.sem("ring_free")
        max_done, nmx_done, exp_done, rz_done = (p.sem(s) for s in ("max_done", "nmx_done", "exp_done", "rz_done"))
        pT_hi, pv_done, cs_hi, cs_lo = (p.sem(s) for s in ("pT_hi", "pv_done", "cs_hi", "cs_lo"))
        block = ctx.enter_context(nc.Block())

        NKC = G * KC
        NSC = 2 * KC
        PIECES = DC * KC
        SC = [0, NSC, 2 * NSC + KT, 3 * NSC + KT]
        TU = [2 * NSC, 4 * NSC + KT + 1]
        OU = [4 * NSC + KT, 4 * NSC + 2 * KT + 1]
        NR = 4 * NSC + 2 * KT + 2

        @block.sync
        def _(sp):
            def load_t(b):
                wait(sp, t_lo, b * PIECES)
                src = ctxT_dram[bass.ds(b, 1), :, :] if not isinstance(b, int) else ctxT_dram[b:b + 1, :, :]
                sp.dma_start(raw_t[:], src.rearrange("a (c p) n -> p (a c) n", p=128)).then_inc(t_loaded, 16)

            def load_n(b):
                for half in range(2):
                    wait(sp, n_lo, (b - 1) * KT + (half + 1) * (KT // 2))
                    rows = slice(half * (SK // 2), (half + 1) * (SK // 2))
                    src = ctx_dram[bass.ds(b, 1), rows, :] if not isinstance(b, int) else ctx_dram[b:b + 1, rows, :]
                    sp.dma_start(raw_n[:, half], src.rearrange("a (j p) c -> p (a j) c", p=KP))\
                        .then_inc(n_loaded[half], 16)

            for b in range(2):
                load_t(b)
                load_n(b)
            with sp.Fori(2, B) as b:
                load_t(b)
                load_n(b)

        @block.tensor
        def _(pe):
            def project(b, g):
                for c in range(KC):
                    n = b * NKC + g * KC + c
                    if g == 0:
                        for i in range(DC):
                            wait(pe, t_lo, b * PIECES + i * KC + c + 1)
                    wait(pe, k_full, n - 2)
                    for i in range(DC):
                        last = mm3(nc, proj[:, c, 0:CH], wk[0][:, i, g * HD:(g + 1) * HD],
                                   wk[1][:, i, g * HD:(g + 1) * HD], ct[0][:, i, c * CH:(c + 1) * CH],
                                   ct[1][:, i, c * CH:(c + 1) * CH], i == 0, i == DC - 1)
                    last.then_inc(proj_done, 1)

            def mean_squares(b, g):
                for c in range(KC):
                    n = b * NKC + g * KC + c
                    wait(pe, sq_done, n + 1)
                    wait(pe, ln_done, n)
                    nc.tensor.matmul(mean[:, 0:CH], mean_mat[:], sq[:, c, :], start=True, stop=True)\
                        .then_inc(mean_done, 1)
                    yield

            def scores(b, g, between):
                for j in range(2):
                    for c in range(KC):
                        r = b * NR + SC[g] + j * KC + c
                        if j == 0:
                            wait(pe, k_lo, b * NKC + g * KC + c + 1)
                        if g == 0 and j == 0 and c == 0:
                            wait(pe, q_lo, b + 1)
                        wait(pe, ring_free, r - 1)
                        h = 4 * g + 2 * j
                        mm3(nc, ring[0:TP, (SC[g] + j * KC + c) % 2, 0:CH], q[0][:, h:h + 2, :], q[1][:, h:h + 2, :],
                            k[0][:, g % 2, c * CH:(c + 1) * CH], k[1][:, g % 2, c * CH:(c + 1) * CH],
                            True, True).then_inc(ring_full, 1)
                        next(between, None)

            def unit(b, u, between):
                def turn(t):
                    if t == 0:
                        wait(pe, exp_done, b * NJ + 4 * (u + 1))
                    wait(pe, ring_free, b * NR + TU[u] + t - 1)
                    for j in range(4):
                        last = nc.tensor.transpose(ring[0:KP, (TU[u] + t) % 2, j * TP:(j + 1) * TP],
                                                   pr[:, j, t * KP:(t + 1) * KP], ident[0:TP, 0:TP])
                    last.then_inc(ring_full, 1)

                turn(0)
                for t in range(KT):
                    if t + 1 < KT:
                        turn(t + 1)
                    wait(pe, ring_free, b * NR + TU[u] + t + 1)
                    if u == 0:
                        wait(pe, n_lo, b * KT + t + 1)
                    if t == 0:
                        wait(pe, cs_lo, (b * U + u) * DC)
                    for i in range(DC):
                        last = mm3(nc, csum[:, i, 0:QU], cn[0][:, t, i * 128:(i + 1) * 128],
                                   cn[1][:, t, i * 128:(i + 1) * 128], pT[0][:, t % 2, :], pT[1][:, t % 2, :],
                                   t == 0, t == KT - 1)
                    last.then_inc(pv_done, 1)
                    next(between, None)

            def output(b, u):
                wait(pe, cs_lo, (b * U + u + 1) * DC)
                wait(pe, ring_free, b * NR + OU[u] - 1)
                for gi in range(2):
                    w = slice((2 * u + gi) * HD, (2 * u + gi + 1) * HD)
                    x = slice(gi * QG, (gi + 1) * QG)
                    for i in range(DC):
                        last = mm3(nc, ring[:, OU[u] % 2, x], wv[0][:, i, w], wv[1][:, i, w],
                                   cs[0][:, i, x], cs[1][:, i, x], i == 0, i == DC - 1)
                last.then_inc(ring_full, 1)

            def batch(b, first, last):
                project(b, 1)
                if not first:
                    output(b - 1, 1)
                scores(b, 0, mean_squares(b, 1))
                project(b, 2)
                scores(b, 1, mean_squares(b, 2))
                project(b, 3)
                unit(b, 0, mean_squares(b, 3))
                scores(b, 2, iter(()))
                scores(b, 3, iter(()))
                output(b, 0)
                if last:
                    unit(b, 1, iter(()))
                    output(b, 1)
                else:
                    project(b + 1, 0)
                    unit(b, 1, mean_squares(b + 1, 0))

            pe.wait_ge(eps_set, 2)
            project(0, 0)
            for _ in mean_squares(0, 0):
                pass
            batch(0, True, False)
            with pe.Fori(1, B - 1) as b:
                batch(b, False, False)
            batch(B - 1, False, True)

        @block.scalar
        def _(act):
            def split_t(b, n):
                wait(act, t_loaded, 16 * (b + 1))
                wait(act, proj_done, b * NKC)
                i, c = n // KC, n % KC
                nc.scalar.activation(ct[0][:, i, c * CH:(c + 1) * CH], raw_t[:, i, c * CH:(c + 1) * CH],
                                     ACT.Copy).then_inc(t_hi, 1)

            def squares(b, g):
                for c in range(KC):
                    n = b * NKC + g * KC + c
                    wait(act, proj_done, n + 1)
                    wait(act, mean_done, n - 2)
                    nc.scalar.activation(sq[:, c, :], proj[:, c, 0:CH], ACT.Square,
                                         bias=eps[:, 1:2]).then_inc(sq_done, 1)

            def rms(b, g):
                for c in range(KC):
                    n = b * NKC + g * KC + c
                    r = (g * KC + c) % 2
                    wait(act, mean_done, n + 1)
                    wait(act, k_full, n - 1)
                    nc.scalar.activation(rs[:, r, :], mean[:, 0:CH], ACT.Ln, bias=eps[:, 0:1]).then_inc(ln_done, 1)
                    wait(act, ln_done, n + 1)
                    nc.scalar.activation(rs[:, r, :], rs[:, r, :], ACT.Exp, scale=-0.5,
                                         bias=eps[:, 1:2]).then_inc(rs_done, 1)
                    yield

            def keys(b, g):
                squares(b, g)
                for _ in rms(b, g):
                    pass

            def exponentials(b, g):
                for j in (2 * g, 2 * g + 1):
                    wait(act, nmx_done, b * NJ + j + 1)
                    wait(act, rz_done, b)
                    nc.scalar.activation(pr[:, j % 4, :], pr[:, j % 4, :], ACT.Exp, bias=nmx[:, j % 4, 1:2],
                                         accum_out=z[:, j:j + 1]).then_inc(exp_done, 1)

            def unit(b, u, pieces, between):
                for t in range(KT):
                    wait(act, ring_full, b * NR + TU[u] + t + 1)
                    wait(act, pv_done, (b * U + u) * KT + t - 1)
                    nc.scalar.activation(pT[0][:, t % 2, :], ring[0:KP, (TU[u] + t) % 2, 0:QU], ACT.Copy)\
                        .then_inc(pT_hi, 1)
                    if t >= 1:
                        next(between, None)
                    if pieces is not None and 2 <= t < 2 + PIECES:
                        split_t(pieces, t - 2)
                wait(act, pv_done, (b * U + u + 1) * KT)
                if u == 1:
                    wait(act, ring_full, b * NR + OU[0] + 1)
                else:
                    wait(act, ring_full, (b - 1) * NR + OU[1] + 1)
                for i in range(DC):
                    nc.scalar.activation(cs[0][:, i, :], csum[:, i, 0:QU], ACT.Copy).then_inc(cs_hi, 1)

            def batch(b, last):
                keys(b, 1)
                exponentials(b, 0)
                keys(b, 2)
                exponentials(b, 1)
                squares(b, 3)
                unit(b, 0, None if last else b + 1, rms(b, 3))
                exponentials(b, 2)
                exponentials(b, 3)
                if last:
                    unit(b, 1, None, iter(()))
                else:
                    squares(b + 1, 0)
                    unit(b, 1, None, rms(b + 1, 0))

            nc.scalar.preload_act_table_set(LN_EXP)
            act.wait_ge(eps_set, 2)
            for n in range(PIECES):
                split_t(0, n)
            keys(0, 0)
            batch(0, False)
            with act.Fori(1, B - 1) as b:
                batch(b, False)
            batch(B - 1, True)

        @block.vector
        def _(dve):
            def split_t(b, n):
                wait(dve, t_hi, b * PIECES + n + 1)
                x = (slice(None), n // KC, slice(n % KC * CH, (n % KC + 1) * CH))
                nc.vector.tensor_tensor(ct[1][x], raw_t[x], ct[0][x].bitcast(F32), ALU.subtract).then_inc(t_lo, 1)

            def split_q(b):
                src = qT[:, :, bass.ds(b * S, S)] if not isinstance(b, int) else qT[:, :, b * S:(b + 1) * S]
                wait(dve, ring_full, (b - 1) * NR + SC[3] + NSC)
                nc.vector.tensor_scalar(q[0][:], src, 1.0, None, ALU.mult).then_inc(q_hi, 1)
                wait(dve, q_hi, b + 1)
                nc.vector.tensor_tensor(q[1][:], src, q[0][:].bitcast(F32), ALU.subtract).then_inc(q_lo, 1)

            def keys(b, g):
                for c in range(KC):
                    n = b * NKC + g * KC + c
                    r = (g * KC + c) % 2
                    wait(dve, rs_done, n + 1)
                    wait(dve, k_lo, n - 1)
                    nc.vector.tensor_tensor(kf[:, r, :], proj[:, c, 0:CH], rs[:, r, :], ALU.mult).then_inc(k_full, 1)
                    wait(dve, k_full, n + 1)
                    if c == 0:
                        wait(dve, ring_full, (b if g >= 2 else b - 1) * NR + SC[(g + 2) % 4] + NSC)
                    nc.vector.tensor_copy(k[0][:, g % 2, c * CH:(c + 1) * CH], kf[:, r, :]).then_inc(k_hi, 1)
                    yield

            def scores(b, g, between):
                for jj in range(2):
                    j = 2 * g + jj
                    for c in range(KC):
                        r = b * NR + SC[g] + jj * KC + c
                        wait(dve, ring_full, r + 1)
                        if c == 0:
                            if g >= 2:
                                wait(dve, ring_full, b * NR + TU[0] + KT)
                            else:
                                wait(dve, ring_full, (b - 1) * NR + TU[1] + KT)
                            wait(dve, exp_done, b * NJ + j - 3)
                        nc.vector.tensor_scalar(pr[:, j % 4, c * CH:(c + 1) * CH],
                                                ring[0:TP, (SC[g] + jj * KC + c) % 2, 0:CH], 1.0, -3.0e38,
                                                ALU.mult, ALU.max, accum_out=mx[:, j % 4, c:c + 1])\
                            .then_inc(ring_free, 1)
                        if jj * KC + c >= 2:
                            next(between, None)
                    wait(dve, ring_free, b * NR + SC[g] + (jj + 1) * KC)
                    nc.vector.tensor_reduce(nmx[:, j % 4, 0:1], mx[:, j % 4, :], AX, ALU.max).then_inc(max_done, 1)
                    wait(dve, max_done, b * NJ + j + 1)
                    nc.vector.tensor_scalar(nmx[:, j % 4, 1:2], nmx[:, j % 4, 0:1], -1.0, None, ALU.mult)\
                        .then_inc(nmx_done, 1)

            def unit(b, u, pieces, between):
                for t in range(KT):
                    wait(dve, pT_hi, (b * U + u) * KT + t + 1)
                    nc.vector.tensor_tensor(pT[1][:, t % 2, :], ring[0:KP, (TU[u] + t) % 2, 0:QU],
                                            pT[0][:, t % 2, :].bitcast(F32), ALU.subtract).then_inc(ring_free, 1)
                    if t >= 2:
                        next(between, None)
                    if pieces is not None and 2 <= t < 2 + PIECES:
                        split_t(pieces, t - 2)
                for i in range(DC):
                    wait(dve, cs_hi, (b * U + u) * DC + i + 1)
                    nc.vector.tensor_tensor(cs[1][:, i, :], csum[:, i, 0:QU], cs[0][:, i, :].bitcast(F32),
                                            ALU.subtract).then_inc(cs_lo, 1)

            def output(b, u):
                wait(dve, ring_full, b * NR + OU[u] + 1)
                x = bass.ds(b * S, S) if not isinstance(b, int) else slice(b * S, (b + 1) * S)
                nc.vector.tensor_scalar(qT[:, 8 * u:8 * u + 8, x],
                                        ring[:, OU[u] % 2, 0:QU].rearrange("p (h t) -> p h t", t=S), 1.0, None,
                                        ALU.mult).then_inc(ring_free, 1)

            def sums(b):
                wait(dve, exp_done, (b + 1) * NJ)
                x = bass.ds(b * NJ, NJ) if not isinstance(b, int) else slice(b * NJ, (b + 1) * NJ)
                nc.vector.reciprocal(rz[:, x], z[:]).then_inc(rz_done, 1)

            def batch(b, first, last):
                split_q(b)
                if not first:
                    output(b - 1, 1)
                scores(b, 0, keys(b, 1))
                scores(b, 1, keys(b, 2))
                unit(b, 0, None if last else b + 1, keys(b, 3))
                scores(b, 2, iter(()))
                scores(b, 3, iter(()))
                output(b, 0)
                unit(b, 1, None, iter(()) if last else keys(b + 1, 0))
                sums(b)

            nc.vector.memset(eps[:, 0:1], RMS_EPS).then_inc(eps_set, 1)
            nc.vector.memset(eps[:, 1:2], 0.0).then_inc(eps_set, 1)
            for n in range(PIECES):
                split_t(0, n)
            for _ in keys(0, 0):
                pass
            batch(0, True, False)
            with dve.Fori(1, B - 1) as b:
                batch(b, False, False)
            batch(B - 1, False, True)
            output(B - 1, 1)
            dve.wait_ge(ring_free, B * NR)
            dve.wait_ge(rz_done, B)

        @block.gpsimd
        def _(pool):
            def keys(b, g):
                for c in range(KC):
                    n = b * NKC + g * KC + c
                    wait(pool, k_hi, n + 1)
                    x = (slice(None), g % 2, slice(c * CH, (c + 1) * CH))
                    nc.gpsimd.tensor_tensor(k[1][x], kf[:, (g * KC + c) % 2, :], k[0][x].bitcast(F32),
                                            ALU.subtract).then_inc(k_lo, 1)

            def split_n(b, tiles):
                for t in tiles:
                    half, j = divmod(t, KT // 2)
                    wait(pool, n_loaded[half], 16 * (b + 1))
                    wait(pool, pv_done, (b * U - 1) * KT + t + 1)
                    nc.gpsimd.tensor_tensor(cn[0][:, t, :], raw_n[:, half, j, :], zeros[:], ALU.add).then_inc(n_hi, 1)
                    wait(pool, n_hi, b * KT + t + 1)
                    nc.gpsimd.tensor_tensor(cn[1][:, t, :], raw_n[:, half, j, :], cn[0][:, t, :].bitcast(F32),
                                            ALU.subtract).then_inc(n_lo, 1)

            def batch(b, last):
                keys(b, 1)
                split_n(b, range(0, 4))
                keys(b, 2)
                split_n(b, range(4, 8))
                keys(b, 3)
                split_n(b, range(8, KT))
                if not last:
                    keys(b + 1, 0)

            nc.gpsimd.memset(zeros[:], 0.0).then_inc(zeros_set, 1)
            pool.wait_ge(zeros_set, 1)
            keys(0, 0)
            batch(0, False)
            with pool.Fori(1, B - 1) as b:
                batch(b, False)
            batch(B - 1, True)


def attention_output(nc, x, oT, rz, wo_dram, ident, ones_mat):
    with ExitStack() as ctx:
        p = Phase(nc, ctx, "wo")
        wo = p.sb("wo", [128, NH, D])
        diag = p.sb("diag", [TP, 2, NJ, TP])
        spread = p.ps("spread", [128, 2, 2, 512])
        out = p.ps("out", [128, 2, 512])
        loaded, diag_done, spread_done, scaled, out_done, added = (p.sem(s) for s in (
            "loaded", "diag_done", "spread_done", "scaled", "out_done", "added"))
        block = ctx.enter_context(nc.Block())

        @block.sync
        def _(sp):
            sp.dma_start(wo[:], wo_dram.rearrange("(h p) n -> p h n", p=128)).then_inc(loaded, 16)

        @block.vector
        def _(dve):
            def scale(b):
                for i in range(2):
                    dve.wait_ge(spread_done, b + 1)
                    y = oT[:, 8 * i:8 * i + 8, b * S:(b + 1) * S]
                    nc.vector.tensor_tensor(y, y, spread[:, b % 2, i, 0:QU].rearrange("p (h t) -> p h t", t=S),
                                            ALU.mult).then_inc(scaled, 1)

            for b in range(B):
                wait(dve, spread_done, b - 1)
                nc.vector.tensor_tensor(diag[:, b % 2], ident[0:TP, None, 0:TP].to_broadcast([TP, NJ, TP]),
                                        rz[:, b * NJ:(b + 1) * NJ].unsqueeze(2).to_broadcast([TP, NJ, TP]),
                                        ALU.mult).then_inc(diag_done, 1)
                if b >= 1:
                    scale(b - 1)
            scale(B - 1)
            for t in range(TT):
                dve.wait_ge(out_done, t + 1)
                nc.vector.tensor_tensor(x[:, t, :], x[:, t, :], out[0:TP, t % 2, 0:D], ALU.add).then_inc(added, 1)
            dve.wait_ge(added, TT)

        @block.tensor
        def _(pe):
            for b in range(B):
                pe.wait_ge(diag_done, b + 1)
                wait(pe, scaled, 2 * (b - 1))
                for i in range(2):
                    last = nc.tensor.matmul(spread[:, b % 2, i, 0:QU], ones_mat[0:TP, :],
                                            diag[:, b % 2, 4 * i:4 * i + 4, :], start=True, stop=True)
                last.then_inc(spread_done, 1)
            pe.wait_ge(loaded, 16)
            for t in range(TT):
                pe.wait_ge(scaled, 2 * (2 * t + 2))
                wait(pe, added, t - 1)
                for h in range(NH):
                    last = nc.tensor.matmul(out[0:TP, t % 2, 0:D], oT[:, h, t * TP:(t + 1) * TP], wo[:, h, :],
                                            start=(h == 0), stop=(h == NH - 1))
                last.then_inc(out_done, 1)


def mixture(nc, name, x, xnT, gate_dram, up_dram, down_dram, router_dram, shared_blocks, before,
            normalise, shared_gate=False):
    rows = (E * EB + shared_blocks) * HB
    with ExitStack() as ctx:
        p = Phase(nc, ctx, name)
        wg = p.sb("wg", [128, DC, rows])
        wu = p.sb("wu", [128, DC, rows])
        wd = p.sb("wd", [HB, rows // HB, D])
        wr = p.sb("wr", [128, DC, E + 1])
        silu = p.sb("silu", [HB, 2, NTOK])
        hid = p.sb("hid", [HB, 4, NTOK])
        logit = p.sb("logit", [TP, TT, E + 1])
        mx = p.sb("mx", [TP, TT])
        prob = p.sb("prob", [TP, TT, E])
        tot = p.sb("tot", [TP, TT])
        rank = p.sb("rank", [TP, TT, E, E])
        same = p.sb("same", [TP, TT, E, E])
        place = p.sb("place", [TP, TT, E])
        share = p.sb("share", [TP, TT])
        comb = p.sb("comb", [TP, TT, E + 1])
        zero = p.sb("zero", [128, 1])
        gate = p.ps("gate", [128, 2, 512])
        up = p.ps("up", [128, 2, 512])
        down = p.ps("down", [128, 2, 512])
        lg = p.ps("lg", [128, 512])

        loaded, wd_loaded, wr_loaded = p.sem("loaded"), p.sem("wd_loaded"), p.sem("wr_loaded")
        lg_done, r, gates_done, silu_done, hid_done, down_done, added, act_r = (p.sem(s) for s in (
            "lg_done", "route_step", "gates_done", "silu_done", "hid_done", "down_done", "added", "act_step"))
        block = ctx.enter_context(nc.Block())

        units = [(e, [e * EB + i for i in range(EB)]) for e in range(E)]
        units.append((E, [E * EB + i for i in range(shared_blocks)]))
        blocks = [m for _, ms in units for m in ms]
        nblk = len(blocks)
        nl = E + shared_gate

        @block.sync
        def _(sp):
            sp.dma_start(wr[:, :, 0:nl], router_dram.rearrange("(c p) n -> p c n", p=128)).then_inc(wr_loaded, 16)
            sp.dma_start(wg[:], gate_dram.rearrange("(c p) n -> p c n", p=128)).then_inc(loaded, 16)
            sp.dma_start(wu[:], up_dram.rearrange("(c p) n -> p c n", p=128)).then_inc(loaded, 16)
            sp.dma_start(wd[:], down_dram.rearrange("(m p) n -> p m n", p=HB)).then_inc(wd_loaded, 16)

        @block.tensor
        def _(pe):
            pe.wait_ge(wr_loaded, 16)
            for t in range(TT):
                for c in range(DC):
                    last = nc.tensor.matmul(lg[0:TP, t * 16:t * 16 + nl], xnT[:, c, t * TP:(t + 1) * TP],
                                            wr[:, c, 0:nl], start=(c == 0), stop=(c == DC - 1))
            last.then_inc(lg_done, 1)
            pe.wait_ge(loaded, 32)

            def widen(n):
                m = blocks[n]
                wait(pe, hid_done, n - 1)
                for out, w in ((gate, wg), (up, wu)):
                    for c in range(DC):
                        last = nc.tensor.matmul(out[0:HB, n % 2, 0:NTOK], w[:, c, m * HB:(m + 1) * HB],
                                                xnT[:, c, :], start=(c == 0), stop=(c == DC - 1))
                last.then_inc(gates_done, 1)

            pe.wait_ge(wd_loaded, 16)
            pairs = [(blocks[2 * i], blocks[2 * i + 1]) for i in range(nblk // 2)]
            for i in range(nblk // 2 + 1):
                if i < nblk // 2:
                    widen(2 * i)
                    widen(2 * i + 1)
                if i >= 1:
                    n = i - 1
                    for half in range(2):
                        wait(pe, added, 4 * n + 2 * half - 2)
                        for t in (2 * half, 2 * half + 1):
                            for ii, m in enumerate(pairs[n]):
                                wait(pe, hid_done, m + 1)
                                last = nc.tensor.matmul(down[0:TP, half, (t % 2) * D:(t % 2 + 1) * D],
                                                        hid[:, m % 4, t * TP:(t + 1) * TP], wd[:, m, :],
                                                        start=(ii == 0), stop=(ii == 1))
                        last.then_inc(down_done, 1)

        @block.scalar
        def _(act):
            act.wait_ge(r, 1)
            act.wait_ge(r, 4)
            nc.scalar.activation(prob[:], prob[:], ACT.Exp, bias=zero[0:TP, 0:1]).then_inc(act_r, 1)
            if shared_gate:
                nc.scalar.activation(share[:], logit[:, :, E], ACT.Exp, scale=-1.0, bias=zero[0:TP, 0:1]).then_inc(act_r, 1)
            for n in range(nblk):
                act.wait_ge(gates_done, n + 1)
                wait(act, hid_done, n - 1)
                nc.scalar.activation(silu[:, n % 2, :], gate[0:HB, n % 2, 0:NTOK], ACT.Silu,
                                     bias=zero[0:HB, 0:1]).then_inc(silu_done, 1)

        @block.vector
        def _(dve):
            step = [0]

            def then(ins):
                step[0] += 1
                ins.then_inc(r, 1)
                dve.wait_ge(r, step[0])

            then(nc.vector.memset(zero[:], 0.0))
            dve.wait_ge(lg_done, 1)
            then(nc.vector.tensor_copy(logit[:, :, 0:nl], lg[0:TP, 0:TT * 16].rearrange("p (t n) -> p t n", n=16)[:, :, 0:nl]))
            then(nc.vector.tensor_reduce(mx[:], logit[:, :, 0:E], AX, ALU.max))
            then(nc.vector.tensor_tensor(prob[:], logit[:, :, 0:E], mx[:].unsqueeze(2).to_broadcast([TP, TT, E]),
                                         ALU.subtract))
            dve.wait_ge(act_r, 1)
            then(nc.vector.tensor_reduce(tot[:], prob[:], AX, ALU.add))
            then(nc.vector.reciprocal(tot[:], tot[:]))
            then(nc.vector.tensor_tensor(prob[:], prob[:], tot[:].unsqueeze(2).to_broadcast([TP, TT, E]), ALU.mult))
            for t in range(TT):
                mine = prob[:, t, :].unsqueeze(2).to_broadcast([TP, E, E])
                other = prob[:, t, :].unsqueeze(1).to_broadcast([TP, E, E])
                then(nc.vector.tensor_tensor(rank[:, t], other, mine, ALU.is_gt))
                then(nc.vector.tensor_tensor(same[:, t], other, mine, ALU.is_equal))
                then(nc.vector.tensor_tensor(same[:, t], same[:, t], before[0:TP], ALU.mult))
            then(nc.vector.tensor_tensor(rank[:], rank[:], same[:], ALU.add))
            then(nc.vector.tensor_reduce(place[:], rank[:], AX, ALU.add))
            then(nc.vector.tensor_scalar(place[:], place[:], 1.5, None, ALU.is_lt))
            then(nc.vector.tensor_tensor(comb[:, :, 0:E], place[:], prob[:], ALU.mult))
            if normalise:
                then(nc.vector.tensor_reduce(tot[:], comb[:, :, 0:E], AX, ALU.add))
                then(nc.vector.reciprocal(tot[:], tot[:]))
                then(nc.vector.tensor_tensor(comb[:, :, 0:E], comb[:, :, 0:E],
                                             tot[:].unsqueeze(2).to_broadcast([TP, TT, E]), ALU.mult))
            if shared_gate:
                dve.wait_ge(act_r, 2)
                then(nc.vector.tensor_scalar(share[:], share[:], 1.0, None, ALU.add))
                then(nc.vector.reciprocal(comb[:, :, E], share[:]))
            else:
                then(nc.vector.memset(comb[:, :, E:E + 1], 1.0))

            def hidden(n):
                dve.wait_ge(silu_done, n + 1)
                if n >= 4:
                    dve.wait_ge(down_done, 2 * ((n - 4) // 2 + 1))
                nc.vector.tensor_tensor(hid[:, n % 4, :], silu[:, n % 2, :], up[0:HB, n % 2, 0:NTOK],
                                        ALU.mult).then_inc(hid_done, 1)

            def add(n):
                e = min(n, E)
                for t in range(TT):
                    dve.wait_ge(down_done, 2 * n + t // 2 + 1)
                    wait(dve, added, 4 * (n - 1) + t + 1)
                    nc.vector.scalar_tensor_tensor(x[:, t, :], down[0:TP, t // 2, (t % 2) * D:(t % 2 + 1) * D],
                                                   comb[:, t, e:e + 1], x[:, t, :], ALU.mult, ALU.add)\
                        .then_inc(added, 1)

            for i in range(nblk // 2):
                hidden(2 * i)
                hidden(2 * i + 1)
                if i >= 1:
                    add(i - 1)
            add(nblk // 2 - 1)
            dve.wait_ge(added, 4 * (nblk // 2))


def key_value_sums(nc, kv, ctxT_dram, mask_dram, wk_dram, bk_dram, wv_dram, bv_dram, wf_dram):
    with ExitStack() as ctx:
        p = Phase(nc, ctx, "kvs")
        wk = [p.sb(f"wk{i}", [128, DC, D], F32R) for i in range(2)]
        wv = [p.sb(f"wv{i}", [128, DC, D], F32R) for i in range(2)]
        split_weights(nc, "kvsw", [(w.rearrange("(c p) n -> p c n", p=128), *halves)
                                   for w, halves in ((wk_dram, wk), (wv_dram, wv))])
        fmap = p.sb("fmap", [128, D])
        f2 = p.sb("f2", [128, 2, D], F32R)
        bk = p.sb("bk", [128, DC])
        bv = p.sb("bv", [KP, D])
        zero = p.sb("zero", [128, 1])
        masks = p.sb("masks", [KP, B * KT])
        mask2 = p.sb("mask2", [KP, B * KT, 2], F32R)
        raw = p.sb("raw", [128, KC, DC, CH])
        ct = [p.sb(f"ct{i}", [128, KC, DC, CH], F32R) for i in range(2)]
        ks = p.sb("ks", [128, KC, 4, CH], F32R)
        vb = p.sb("vb", [KP, 2, KG * GV])
        vs = p.sb("vs", [KP, 2, KG, VW], F32R)
        kp = [p.sb(f"kp{i}", [KP, 2, FEAT], F32R) for i in range(2)]
        keys_ps = p.ps("keys_ps", [128, DC, 512])
        vals_ps = p.ps("vals_ps", [128, 512])
        feat = p.ps("feat", [128, 2, 512])
        sums = p.ps("sums", [128, 3, 512])

        const_loaded, fmap_set, f_loaded, f_hi_done, f_split, m_loaded, m_hi, m_lo, vb_set = (p.sem(s) for s in (
            "const_loaded", "fmap_set", "f_loaded", "f_hi_done", "f_split", "m_loaded", "m_hi", "m_lo", "vb_set"))
        loaded = [p.sem(f"loaded{c}") for c in range(KC)]
        t_hi, t_lo, k_done, ks_hi, ks_lo = (p.sem(s) for s in ("t_hi", "t_lo", "k_done", "ks_hi", "ks_lo"))
        v_done, vb_done, v_hi, v_lo, v_mask = (p.sem(s) for s in ("v_done", "vb_done", "v_hi", "v_lo", "v_mask"))
        feat_done, f_hi, f_lo, sums_done, kv_done = (p.sem(s) for s in ("feat_done", "f_hi", "f_lo", "sums_done", "kv_done"))
        block = ctx.enter_context(nc.Block())
        NB = len(SUMS)

        def at_batch(b, t):
            return slice(b * KT + t, b * KT + t + 1) if isinstance(b, int) else bass.ds(b * KT + t, 1)

        def chunk_after(b, t):
            if t % TPC != 1:
                return None
            c = t // TPC + 1
            return (b, c) if c < KC else (b + 1, 0)

        def chunk_to_split(b, t):
            if t % TPC != TPC - 1:
                return None
            c = t // TPC + 2
            return (b, c) if c < KC else (b + 1, c - KC)

        def passes(b, last):
            for t in range(KT):
                project, split = chunk_after(b, t), chunk_to_split(b, t)
                wraps = t // TPC + 1 >= KC, t // TPC + 2 >= KC
                yield (t, None if last and wraps[0] else project, None if last and wraps[1] else split)

        def run_peeled(eng, batch):
            batch(0, False)
            with eng.Fori(1, B - 1) as b:
                batch(b, False)
            batch(B - 1, True)

        @block.sync
        def _(sp):
            sp.dma_start(bk[:], bk_dram).then_inc(const_loaded, 16)
            sp.dma_start(bv[:], bv_dram.partition_broadcast(KP)).then_inc(const_loaded, 16)
            sp.dma_start(masks[:], mask_dram).then_inc(m_loaded, 16)
            sp.wait_ge(fmap_set, 1)
            for h in range(8):
                i = h % 4
                sp.dma_start(fmap[16 * h:16 * h + 16, FD * i:FD * (i + 1)], wf_dram).then_inc(f_loaded, 16)

            def load(b, c):
                wait(sp, t_lo, (b - 1) * KC + c + 1)
                src = ctxT_dram[bass.ds(b, 1), :, c * CH:(c + 1) * CH] if not isinstance(b, int) else \
                    ctxT_dram[b:b + 1, :, c * CH:(c + 1) * CH]
                sp.dma_start(raw[:, c], src.rearrange("a (k p) n -> p (a k) n", p=128)).then_inc(loaded[c], 16)

            for c in range(KC):
                load(0, c)
            with sp.Fori(1, B) as b:
                for c in range(KC):
                    load(b, c)

        @block.tensor
        def _(pe):
            def keys(b, c):
                wait(pe, t_lo, b * KC + c + 1)
                for m in range(DC):
                    wait(pe, ks_lo, 4 * (b * KC + c - 1) + 2 * (m + 1))
                    for i in range(DC):
                        last = mm3(nc, keys_ps[:, m, 0:CH], wk[0][:, i, m * 128:(m + 1) * 128],
                                   wk[1][:, i, m * 128:(m + 1) * 128], ct[0][:, c, i, :], ct[1][:, c, i, :],
                                   i == 0, i == DC - 1)
                    last.then_inc(k_done, 1)

            def values(b, t):
                c, i = divmod(t, TPC)
                x = slice(i * KP, (i + 1) * KP)
                wait(pe, vb_done, b * KT + t)
                for k in range(DC):
                    last = mm3(nc, vals_ps[0:KP, 0:D], ct[0][:, c, k, x], ct[1][:, c, k, x],
                               wv[0][:, k, :], wv[1][:, k, :], k == 0, k == DC - 1)
                last.then_inc(v_done, 1)

            def features(b, t):
                c, i = divmod(t, TPC)
                x = slice(i * KP, (i + 1) * KP)
                wait(pe, ks_lo, 4 * (b * KC + c + 1))
                for half in range(2):
                    wait(pe, f_lo, 2 * (b * KT + t - 1) + half + 1)
                    for g in range(2):
                        y = slice(g * D, (g + 1) * D)
                        for w in (1, 0):
                            last = nc.tensor.matmul(feat[0:KP, half, y], ks[:, c, 2 * half + g, x], f2[:, w, :],
                                                    start=(w == 1), stop=(w == 0), skip_group_check=True)
                    last.then_inc(feat_done, 1)

            def add(b, t):
                n = b * KT + t
                wait(pe, v_lo, n + 1)
                wait(pe, v_mask, n + 1)
                wait(pe, f_lo, 2 * n + 2)
                if t == 0:
                    wait(pe, kv_done, NB * b)
                for g in range(KG):
                    w = min(GF, FEAT - g * GF)
                    for half in (1, 0):
                        last = nc.tensor.matmul(sums[0:VW, g // 2, (g % 2) * GF:(g % 2) * GF + w],
                                                vs[:, t % 2, g, :], kp[half][:, t % 2, g * GF:g * GF + w],
                                                start=(t == 0 and g % 2 == 0 and half == 1),
                                                stop=(t == KT - 1 and g % 2 == 1 and half == 0),
                                                skip_group_check=True)
                last.then_inc(sums_done, 1)

            def batch(b, last):
                for t, project, _ in passes(b, last):
                    values(b, t)
                    features(b, t)
                    if t >= 1:
                        add(b, t - 1)
                    if project is not None:
                        keys(*project)
                add(b, KT - 1)

            pe.wait_ge(f_split, 2)
            keys(0, 0)
            run_peeled(pe, batch)

        @block.scalar
        def _(act):
            def split(b, c):
                wait(act, loaded[c], 16 * (b + 1))
                wait(act, v_done, (b - 1) * KT + TPC * (c + 1))
                nc.scalar.activation(ct[0][:, c], raw[:, c], ACT.Copy).then_inc(t_hi, 1)

            def keys(b, c):
                for m in range(DC):
                    wait(act, k_done, 2 * (b * KC + c) + m + 1)
                    wait(act, feat_done, 2 * ((b - 1) * KT + TPC * (c + 1)))
                    for h in range(2):
                        x = slice(64 * h, 64 * (h + 1))
                        nc.scalar.activation(ks[0:64, c, 2 * m + h, :], keys_ps[x, m, 0:CH], ACT.Identity,
                                             bias=bk[x, m:m + 1]).then_inc(ks_hi, 1)

            def batch(b, last):
                for t, project, to_split in passes(b, last):
                    n = b * KT + t
                    wait(act, sums_done, n - 1)
                    for half in range(2):
                        wait(act, feat_done, 2 * n + half + 1)
                        nc.scalar.activation(kp[0][:, t % 2, half * 512:(half + 1) * 512], feat[0:KP, half, :],
                                             ACT.Relu, bias=zero[0:KP, 0:1]).then_inc(f_hi, 1)
                    wait(act, vb_done, n + 1)
                    nc.scalar.activation(vs[:, t % 2, :, 0:GV], vb[:, t % 2, :].rearrange("p (g v) -> p g v", v=GV),
                                         ACT.Copy, scale=masks[:, at_batch(b, t)]).then_inc(v_hi, 1)
                    if project is not None:
                        keys(*project)
                    if to_split is not None:
                        split(*to_split)
                wait(act, sums_done, (b + 1) * KT)
                for i, (lo, hi) in enumerate(SUMS):
                    dst = kv[:, b, lo:hi] if isinstance(b, int) else kv[:, bass.ds(b, 1), lo:hi]
                    src = sums[0:VW, i, 0:hi - lo] if isinstance(b, int) else sums[0:VW, i:i + 1, 0:hi - lo]
                    nc.scalar.activation(dst, src, ACT.Copy).then_inc(kv_done, 1)

            act.wait_ge(m_loaded, 16)
            act.wait_ge(const_loaded, 32)
            act.wait_ge(vb_set, 2)
            act.wait_ge(f_loaded, 16 * 8)
            nc.scalar.activation(f2[:, 0, :], fmap[:], ACT.Copy).then_inc(f_hi_done, 1)
            split(0, 0)
            split(0, 1)
            keys(0, 0)
            run_peeled(act, batch)
            act.wait_ge(kv_done, NB * B)

        @block.vector
        def _(dve):
            def split(b, c):
                wait(dve, t_hi, b * KC + c + 1)
                nc.vector.tensor_tensor(ct[1][:, c], raw[:, c], ct[0][:, c].bitcast(F32), ALU.subtract).then_inc(t_lo, 1)

            def keys(b, c):
                for m in range(DC):
                    for h in range(2):
                        x = slice(64 * h, 64 * (h + 1))
                        wait(dve, ks_hi, 4 * (b * KC + c) + 2 * m + h + 1)
                        nc.vector.scalar_tensor_tensor(ks[64:128, c, 2 * m + h, :], keys_ps[x, m, 0:CH],
                                                       bk[x, m:m + 1], ks[0:64, c, 2 * m + h, :].bitcast(F32),
                                                       ALU.add, ALU.subtract).then_inc(ks_lo, 1)

            def batch(b, last):
                for t, project, to_split in passes(b, last):
                    n = b * KT + t
                    wait(dve, v_done, n + 1)
                    wait(dve, v_lo, n - 1)
                    nc.vector.tensor_tensor(vb[:, t % 2, 0:D], vals_ps[0:KP, 0:D], bv[:], ALU.add).then_inc(vb_done, 1)
                    for half in range(2):
                        wait(dve, f_hi, 2 * n + half + 1)
                        y = slice(half * 512, (half + 1) * 512)
                        nc.vector.scalar_tensor_tensor(kp[1][:, t % 2, y], feat[0:KP, half, :], 0.0,
                                                       kp[0][:, t % 2, y].bitcast(F32), ALU.max,
                                                       ALU.subtract).then_inc(f_lo, 1)
                    wait(dve, v_hi, n + 1)
                    nc.vector.scalar_tensor_tensor(vs[:, t % 2, :, GV:2 * GV],
                                                   vb[:, t % 2, :].rearrange("p (g v) -> p g v", v=GV),
                                                   masks[:, at_batch(b, t)], vs[:, t % 2, :, 0:GV].bitcast(F32),
                                                   ALU.mult, ALU.subtract).then_inc(v_lo, 1)
                    nc.vector.tensor_scalar(vs[:, t % 2, :, 2 * GV:VW],
                                            mask2[:, at_batch(b, t), :].bitcast(F32).to_broadcast([KP, KG, 2]),
                                            1.0, None, ALU.mult).then_inc(v_mask, 1)
                    if project is not None:
                        keys(*project)
                    if to_split is not None:
                        split(*to_split)

            dve.wait_ge(m_lo, 1)
            nc.vector.memset(vb[:], 0.0).then_inc(vb_set, 1)
            nc.vector.memset(zero[:], 0.0).then_inc(vb_set, 1)
            dve.wait_ge(vb_set, 2)
            nc.vector.memset(f2[64:128, 1, :].bitcast(F32), 0.0).then_inc(f_split, 1)
            dve.wait_ge(f_hi_done, 1)
            nc.vector.tensor_tensor(f2[0:64, 1, :], fmap[0:64, :], f2[0:64, 0, :].bitcast(F32),
                                    ALU.subtract).then_inc(f_split, 1)
            split(0, 0)
            split(0, 1)
            keys(0, 0)
            run_peeled(dve, batch)

        @block.gpsimd
        def _(pool):
            nc.gpsimd.memset(fmap[:], 0.0).then_inc(fmap_set, 1)
            pool.wait_ge(m_loaded, 16)
            nc.gpsimd.tensor_copy(mask2[:, :, 0], masks[:]).then_inc(m_hi, 1)
            pool.wait_ge(m_hi, 1)
            nc.gpsimd.tensor_tensor(mask2[:, :, 1], masks[:], mask2[:, :, 0].bitcast(F32), ALU.subtract).then_inc(m_lo, 1)
            pool.wait_ge(m_lo, 1)


def linear_readout(nc, x, xnT, kv, wq_dram, bq_dram, wf_dram, wo_dram, bo_dram, ident):
    with ExitStack() as ctx:
        p = Phase(nc, ctx, "lin")
        wq = p.sb("wq", [128, DC, D])
        wo = p.sb("wo", [128, DC, D])
        fmap = p.sb("fmap", [128, 4, 128])
        bq = p.sb("bq", [128, DC])
        bo = p.sb("bo", [TP, D])
        qT = p.sb("qT", [128, DC, NTOK])
        qf = p.sb("qf", [128, NH // 2, NTOK])
        sel = p.sb("sel", [VW, GH, RV])
        kvd = p.sb("kvd", [128, 2, NH // 2, 2 * RV])
        den = p.sb("den", [S, B, NH])
        att = p.sb("att", [S, B, D])
        attT = p.sb("attT", [128, DC, NTOK])
        zero = p.sb("zero", [128, 1])
        q_ps = p.ps("q_ps", [128, 2, 512])
        kv_ps = p.ps("kv_ps", [128, 2, 512])
        out_ps = p.ps("out_ps", [128, 2, 512])
        t_ps = p.ps("t_ps", [128, 2, 512])

        set0, loaded, f_loaded, sel_done = p.sem("set0"), p.sem("loaded"), p.sem("f_loaded"), p.sem("sel_done")
        q_done, qT_done, qf_ps, qf_done, kv_full, kvd_done = (p.sem(s) for s in (
            "q_done", "qT_done", "qf_ps", "qf_done", "kv_full", "kvd_done"))
        read_done, den_done, att_done, t_done, attT_done, y_done, added = (p.sem(s) for s in (
            "read_done", "den_done", "att_done", "t_done", "attT_done", "y_done", "added"))
        block = ctx.enter_context(nc.Block())

        @block.sync
        def _(sp):
            sp.dma_start(wq[:], wq_dram.rearrange("(c p) n -> p c n", p=128)).then_inc(loaded, 16)
            sp.dma_start(wo[:], wo_dram.rearrange("(c p) n -> p c n", p=128)).then_inc(loaded, 16)
            sp.dma_start(bq[:], bq_dram).then_inc(loaded, 16)
            sp.dma_start(bo[:], bo_dram.partition_broadcast(TP)).then_inc(loaded, 16)
            sp.wait_ge(set0, 3)
            for h in range(8):
                sp.dma_start(fmap[16 * h:16 * h + 16, h // 2, FD * (h % 2):FD * (h % 2 + 1)], wf_dram)\
                    .then_inc(f_loaded, 16)

        @block.gpsimd
        def _(pool):
            nc.gpsimd.memset(fmap[:], 0.0).then_inc(set0, 1)
            nc.gpsimd.memset(kvd[:], 0.0).then_inc(set0, 1)
            nc.gpsimd.memset(zero[:], 0.0).then_inc(set0, 1)
            for i in range(GH):
                x = slice(HE * i, HE * (i + 1))
                y = slice(GV + HE * i, GV + HE * (i + 1))
                nc.gpsimd.tensor_tensor(sel[:, i, 0:HE], ident[0:VW, x], ident[0:VW, y], ALU.add).then_inc(sel_done, 1)
                nc.gpsimd.tensor_tensor(sel[:, i, HE:RV], ident[0:VW, 2 * GV:2 * GV + 1],
                                        ident[0:VW, 2 * GV + 1:2 * GV + 2], ALU.add).then_inc(sel_done, 1)

        @block.tensor
        def _(pe):
            pe.wait_ge(loaded, 64)
            for m in range(DC):
                for c in range(DC):
                    last = nc.tensor.matmul(q_ps[:, m, 0:NTOK], wq[:, c, m * 128:(m + 1) * 128], xnT[:, c, :],
                                            start=(c == 0), stop=(c == DC - 1))
                last.then_inc(q_done, 1)
            pe.wait_ge(f_loaded, 16 * 8)
            pe.wait_ge(qT_done, DC)
            for j in range(NH // 2):
                wait(pe, qf_done, j - 1)
                nc.tensor.matmul(q_ps[:, j % 2, 0:NTOK], fmap[:, j % 4, :], qT[:, j // 4, :],
                                 start=True, stop=True).then_inc(qf_ps, 1)
            pe.wait_ge(sel_done, 2 * GH)

            def gather(b):
                wait(pe, kvd_done, 2 * (b - 1))
                for h in range(NH):
                    r = slice(64 * (h % 2), 64 * (h % 2 + 1))
                    c0 = h // 2 * 2 * RV + (h % 2) * RV
                    last = nc.tensor.matmul(kv_ps[r, b % 2, c0:c0 + RV], kv[:, b, h * FD:(h + 1) * FD],
                                            sel[:, h % GH, :], start=True, stop=True, skip_group_check=True)
                last.then_inc(kv_full, 1)

            def read(b):
                wait(pe, kvd_done, 2 * (b + 1))
                wait(pe, qf_done, NH // 2)
                wait(pe, att_done, b - 1)
                for j in range(NH // 2):
                    last = nc.tensor.matmul(out_ps[0:S, b % 2, j * 2 * RV:(j + 1) * 2 * RV],
                                            qf[:, j, b * S:(b + 1) * S], kvd[:, b % 2, j, :], start=True, stop=True)
                last.then_inc(read_done, 1)

            def turn(b):
                wait(pe, att_done, b + 1)
                for c in range(DC):
                    last = nc.tensor.transpose(t_ps[:, c, b * S:(b + 1) * S], att[:, b, c * 128:(c + 1) * 128],
                                               ident[0:S, 0:S])
                last.then_inc(t_done, 1)

            for b in range(B + 2):
                if b < B:
                    gather(b)
                if 1 <= b <= B:
                    read(b - 1)
                if b >= 2:
                    turn(b - 2)
            pe.wait_ge(attT_done, DC)
            for t in range(TT):
                wait(pe, added, 2 * (t - 1))
                for c in range(DC):
                    last = nc.tensor.matmul(q_ps[0:TP, t % 2, 0:D], attT[:, c, t * TP:(t + 1) * TP], wo[:, c, :],
                                            start=(c == 0), stop=(c == DC - 1))
                last.then_inc(y_done, 1)

        @block.scalar
        def _(act):
            act.wait_ge(set0, 3)
            act.wait_ge(loaded, 64)
            for m in range(DC):
                act.wait_ge(q_done, m + 1)
                nc.scalar.activation(qT[:, m, :], q_ps[:, m, 0:NTOK], ACT.Identity, bias=bq[:, m:m + 1]).then_inc(qT_done, 1)
            for j in range(NH // 2):
                act.wait_ge(qf_ps, j + 1)
                nc.scalar.activation(qf[:, j, :], q_ps[:, j % 2, 0:NTOK], ACT.Relu, bias=zero[:, 0:1]).then_inc(qf_done, 1)

        @block.vector
        def _(dve):
            dve.wait_ge(set0, 3)

            def diagonal(b):
                dve.wait_ge(kv_full, b + 1)
                wait(dve, read_done, b - 1)
                src = kv_ps[:, b % 2, 0:NH * RV].rearrange("p (j n) -> p j n", n=2 * RV)
                for i in range(2):
                    r, c = slice(64 * i, 64 * (i + 1)), slice(RV * i, RV * (i + 1))
                    nc.vector.tensor_copy(kvd[r, b % 2, :, c], src[r, :, c]).then_inc(kvd_done, 1)

            def divide(b):
                dve.wait_ge(read_done, b + 1)
                o = out_ps[0:S, b % 2, 0:NH * RV].rearrange("p (h n) -> p h n", n=RV)
                nc.vector.tensor_scalar(den[:, b, :], o[:, :, HE], 1e-8, None, ALU.add).then_inc(den_done, 1)
                dve.wait_ge(den_done, 2 * b + 1)
                nc.vector.reciprocal(den[:, b, :], den[:, b, :]).then_inc(den_done, 1)
                dve.wait_ge(den_done, 2 * b + 2)
                nc.vector.tensor_tensor(att[:, b, :].rearrange("p (h n) -> p h n", n=HE), o[:, :, 0:HE],
                                        den[:, b, :].unsqueeze(2).to_broadcast([S, NH, HE]), ALU.mult).then_inc(att_done, 1)

            for b in range(B + 1):
                if b < B:
                    diagonal(b)
                if b >= 1:
                    divide(b - 1)
            dve.wait_ge(t_done, B)
            for c in range(DC):
                nc.vector.tensor_copy(attT[:, c, :], t_ps[:, c, 0:NTOK]).then_inc(attT_done, 1)
            dve.wait_ge(loaded, 64)
            for t in range(TT):
                dve.wait_ge(y_done, t + 1)
                nc.vector.tensor_tensor(x[:, t, :], x[:, t, :], q_ps[0:TP, t % 2, 0:D], ALU.add).then_inc(added, 1)
                dve.wait_ge(added, 2 * t + 1)
                nc.vector.tensor_tensor(x[:, t, :], x[:, t, :], bo[:], ALU.add).then_inc(added, 1)
            dve.wait_ge(added, 2 * TT)


def build(nc, a, out):
    with ExitStack() as ctx:
        p = Phase(nc, ctx, "all")
        x = p.sb("x", [TP, TT, D])
        xnT = p.sb("xnT", [128, DC, NTOK])
        ident = p.sb("ident", [128, 128])
        mean_mat = p.sb("mean_mat", [128, 128])
        ones_mat = p.sb("ones_mat", [128, 128])
        before = p.sb("before", [128, E, E])
        x_loaded, zeroed, consts, stored = p.sem("x_loaded"), p.sem("zeroed"), p.sem("consts"), p.sem("stored")

        with nc.Block() as block:
            @block.gpsimd
            def _(pool):
                identity(nc, pool, ident[:], 128, zeroed, consts)
                nc.gpsimd.memset(mean_mat[:], 1.0 / HD).then_inc(consts, 1)
                nc.gpsimd.memset(ones_mat[:], 1.0).then_inc(consts, 1)
                nc.gpsimd.memset(before[:], 1.0).then_inc(zeroed, 1)
                pool.wait_ge(zeroed, 2)
                nc.gpsimd.affine_select(out=before[:], in_=before[:], compare_op=ALU.is_gt, fill=0.0, base=0,
                                        pattern=[[1, E], [-1, E]], channel_multiplier=0).then_inc(consts, 1)
                pool.wait_ge(consts, 4)

            @block.sync
            def _(sp):
                sp.dma_start(x[:], a["x"].rearrange("(t p) d -> p t d", p=TP)).then_inc(x_loaded, 16)
                sp.wait_ge(x_loaded, 16)

        with ExitStack() as heads:
            h = Phase(nc, heads, "heads")
            qT = h.sb("qT", [128, NH, NTOK])
            rz = h.sb("rz", [TP, B * NJ])
            layernorm_transposed(nc, "ln0", x, xnT, ident)
            queries(nc, xnT, qT, a["wq0"], a["qnorm"], a["knorm"], mean_mat)
            softmax_attention(nc, qT, rz, a["ctx"], a["ctxT"], a["wk0"], a["wv0"], mean_mat, ident)
            attention_output(nc, x, qT, rz, a["wo0"], ident, ones_mat)

        layernorm_transposed(nc, "ln1", x, xnT, ident)
        mixture(nc, "moe0", x, xnT, a["gate0"], a["up0"], a["down0"], a["router0"], SHARED0, before, False)

        with ExitStack() as linear:
            h = Phase(nc, linear, "linear")
            kv = h.sb("kv", [VW, B, FEAT])
            key_value_sums(nc, kv, a["ctxT"], a["mask"], a["wk1"], a["bk1"], a["wv1"], a["bv1"], a["wkf"])
            layernorm_transposed(nc, "ln2", x, xnT, ident)
            linear_readout(nc, x, xnT, kv, a["wq1"], a["bq1"], a["wqf"], a["wo1"], a["bo1"], ident)

        layernorm_transposed(nc, "ln3", x, xnT, ident)
        mixture(nc, "moe1", x, xnT, a["gate1"], a["up1"], a["down1"], a["router1"], SHARED1, before, True,
                shared_gate=True)

        with nc.Block() as block:
            @block.sync
            def _(sp):
                sp.dma_start(out.rearrange("(t p) d -> p t d", p=TP), x[:]).then_inc(stored, 16)
                sp.wait_ge(stored, 16)


def kernel(**inputs):
    import numpy as np
    from concourse import bacc
    from concourse.bass_utils import run_bass_kernel_spmd

    g = {k: np.asarray(v) for k, v in inputs.items()}
    moe1 = g["L1_ffn_gate_up_proj"].transpose(0, 2, 1)
    hidden = moe1.shape[2] // 2

    def columns(w, shared):
        return np.concatenate([w.transpose(1, 0, 2).reshape(D, -1), shared], axis=1)

    arrays = {
        "x": g["x"].reshape(NTOK, D),
        "ctx": g["ctx_2048"],
        "ctxT": g["ctx_2048"].transpose(0, 2, 1),
        "mask": g["mask_BxS2_ff1"].reshape(B, KT, KP).transpose(2, 0, 1).reshape(KP, B * KT),
        "wq0": g["L0_xattn_Wq"], "wk0": g["L0_xattn_Wk"], "wv0": g["L0_xattn_Wv"], "wo0": g["L0_xattn_Wo"],
        "qnorm": g["L0_xattn_q_norm_w"].reshape(HD, 1), "knorm": g["L0_xattn_k_norm_w"].reshape(HD, 1),
        "router0": g["L0_ffn_gate_w"],
        "gate0": columns(g["L0_ffn_w_gate"], g["L0_ffn_sw_gate"]),
        "up0": columns(g["L0_ffn_w_up"], g["L0_ffn_sw_up"]),
        "down0": np.concatenate([g["L0_ffn_w_down"].reshape(-1, D), g["L0_ffn_sw_down"]]),
        "wq1": g["L1_xattn_Wq"].T, "wk1": g["L1_xattn_Wk"].T, "wv1": g["L1_xattn_Wv"].T, "wo1": g["L1_xattn_Wo"].T,
        "bq1": g["L1_xattn_bq"].reshape(DC, 128).T, "bk1": g["L1_xattn_bk"].reshape(DC, 128).T,
        "bv1": g["L1_xattn_bv"].reshape(1, D), "bo1": g["L1_xattn_bo"].reshape(1, D),
        "wqf": g["L1_xattn_Wqf"].T, "wkf": g["L1_xattn_Wkf"].T,
        "router1": np.concatenate([g["L1_ffn_router_weight"], g["L1_ffn_shared_gate_w"]]).T,
        "gate1": columns(moe1[:, :, :hidden], g["L1_ffn_sh_gate_w"].T),
        "up1": columns(moe1[:, :, hidden:], g["L1_ffn_sh_up_w"].T),
        "down1": np.concatenate([g["L1_ffn_down_proj"].transpose(0, 2, 1).reshape(-1, D), g["L1_ffn_sh_down_w"].T]),
    }
    nc = bacc.Bacc("TRN2", target_bir_lowering=False, num_devices=1)
    drams, feed = {}, {}
    for name, value in arrays.items():
        value = np.ascontiguousarray(value)
        feed[f"in_{name}"] = value
        drams[name] = nc.dram_tensor(f"in_{name}", value.shape, mybir.dt.from_np(value.dtype), kind="ExternalInput").ap()
    out = nc.dram_tensor("out", (NTOK, D), F32, kind="ExternalOutput").ap()
    build(nc, drams, out)
    got = run_bass_kernel_spmd(nc, [feed], core_ids=[0]).results[0]["out"]
    return got.reshape(B, S, D)
```

```python
from contextlib import ExitStack

import concourse.bass as bass
from concourse import mybir

F32 = mybir.dt.float32
F32R = mybir.dt.float32r
ALU = mybir.AluOpType
ACT = mybir.ActivationFunctionType
AX = mybir.AxisListType.X

B = 8
S = 56
D = 256
DC = D // 128
NTOK = B * S
TT = 4
TP = NTOK // TT
SK = 1500
KC = 3
CH = SK // KC
KT = 12
KP = SK // KT
TPC = KT // KC

NH = 16
HD = 128
G = 4
HG = NH // G
QG = HG * S
U = 2
QU = 2 * QG
NJ = NH * S // TP

HE = 16
FD = 64
FEAT = NH * FD
KG = 6
GH = 3
GF = GH * FD
GV = GH * HE
VW = 2 * GV + 2
SUMS = [(i * 2 * GF, min((i + 1) * 2 * GF, FEAT)) for i in range(KG // 2)]
RV = HE + 1

E = 8
HB = 88
EB = 2

SHARED0 = 4
SHARED1 = 8

LN_EXP = "natural_log_exp_and_others"

LN_EPS = 1e-5
RMS_EPS = 1e-6


def wait(eng, sem, value):
    if isinstance(value, int) and value <= 0:
        return
    eng.wait_ge(sem, value)


def identity(nc, pool, tile, n, memset_done, ident_done):
    nc.gpsimd.memset(tile, 0.0).then_inc(memset_done, 1)
    pool.wait_ge(memset_done, 1)
    nc.gpsimd.affine_select(out=tile, in_=tile, compare_op=ALU.not_equal, fill=1.0, base=0,
                            pattern=[[-1, n]], channel_multiplier=1).then_inc(ident_done, 1)


class Phase:

    def __init__(self, nc, ctx, name):
        self.nc, self.ctx, self.name, self.sems = nc, ctx, name, []
        ctx.callback(self.clear)

    def clear(self):
        if self.sems:
            self.nc.clear_and_free_semaphores(self.sems)
            self.nc.all_engine_barrier()

    def sb(self, name, shape, dt=F32):
        return self.ctx.enter_context(self.nc.sbuf_tensor(f"{self.name}_{name}", shape, dt))

    def ps(self, name, shape):
        return self.ctx.enter_context(self.nc.psum_tensor(f"{self.name}_{name}", shape, F32))

    def sem(self, name):
        self.sems.append(self.nc.alloc_semaphore(f"{self.name}_{name}"))
        return self.sems[-1]


def mm3(nc, out, w_hi, w_lo, x_hi, x_lo, start, stop):
    nc.tensor.matmul(out, w_lo, x_hi, start=start, stop=False, skip_group_check=True)
    nc.tensor.matmul(out, w_hi, x_lo, start=False, stop=False, skip_group_check=True)
    return nc.tensor.matmul(out, w_hi, x_hi, start=False, stop=stop, skip_group_check=True)


def layernorm_transposed(nc, name, x, xnT, ident, halves=None):
    with ExitStack() as ctx:
        p = Phase(nc, ctx, name)
        stats = p.sb("stats", [TP, TT, 6])
        mv = p.sb("mv", [TP, TT, 2])
        var = p.sb("var", [TP, TT])
        rstd = p.sb("rstd", [TP, TT])
        tmp = p.sb("tmp", [TP, TT])
        xn = p.sb("xn", [TP, TT, D])
        eps = p.sb("eps", [128, 1])
        turned = p.ps("turned", [128, 2, 512])
        stats_done, mv_done, var_done, guess_done = (p.sem(s) for s in (
            "stats_done", "mv_done", "var_done", "guess_done"))
        newton, xn_done, turned_done, copied = (p.sem(s) for s in ("newton", "xn_done", "turned_done", "copied"))
        hi_done = p.sem("hi_done")
        block = ctx.enter_context(nc.Block())

        @block.vector
        def _(dve):
            nc.vector.memset(eps[:], 0.0).then_inc(var_done, 1)
            for t in range(TT):
                nc.vector.bn_stats(stats[:, t, :], x[:, t, :]).then_inc(stats_done, 1)
            for t in range(TT):
                dve.wait_ge(stats_done, t + 1)
                nc.vector.bn_aggr(mv[:, t, :], stats[:, t, :]).then_inc(mv_done, 1)
            dve.wait_ge(mv_done, TT)
            nc.vector.tensor_scalar(var[:], mv[:, :, 1], LN_EPS, None, ALU.add).then_inc(var_done, 1)
            dve.wait_ge(guess_done, 2)
            nc.vector.tensor_tensor(tmp[:], rstd[:], rstd[:], ALU.mult).then_inc(newton, 1)
            dve.wait_ge(newton, 1)
            nc.vector.tensor_tensor(tmp[:], tmp[:], var[:], ALU.mult).then_inc(newton, 1)
            dve.wait_ge(newton, 2)
            nc.vector.tensor_scalar(tmp[:], tmp[:], -0.5, 1.5, ALU.mult, ALU.add).then_inc(newton, 1)
            dve.wait_ge(newton, 3)
            nc.vector.tensor_tensor(rstd[:], rstd[:], tmp[:], ALU.mult).then_inc(newton, 1)
            dve.wait_ge(newton, 4)
            for t in range(TT):
                nc.vector.tensor_scalar(xn[:, t, :], x[:, t, :], mv[:, t, 0:1], rstd[:, t:t + 1],
                                        ALU.subtract, ALU.mult).then_inc(xn_done, 1)
            for c in range(DC):
                dve.wait_ge(turned_done, c + 1)
                nc.vector.tensor_copy(xnT[:, c, :], turned[:, c, 0:NTOK]).then_inc(copied, 1)
            if halves:
                for c in range(DC):
                    dve.wait_ge(hi_done, c + 1)
                    nc.vector.tensor_tensor(halves[1][:, c, :], xnT[:, c, :], halves[0][:, c, :].bitcast(F32),
                                            ALU.subtract).then_inc(copied, 1)
            dve.wait_ge(copied, 2 * DC if halves else DC)

        @block.scalar
        def _(act):
            nc.scalar.preload_act_table_set(LN_EXP)
            act.wait_ge(var_done, 2)
            nc.scalar.activation(rstd[:], var[:], ACT.Ln, bias=eps[0:TP, 0:1]).then_inc(guess_done, 1)
            act.wait_ge(guess_done, 1)
            nc.scalar.activation(rstd[:], rstd[:], ACT.Exp, scale=-0.5, bias=eps[0:TP, 0:1]).then_inc(guess_done, 1)
            if halves:
                for c in range(DC):
                    act.wait_ge(copied, c + 1)
                    nc.scalar.activation(halves[0][:, c, :], xnT[:, c, :], ACT.Copy).then_inc(hi_done, 1)

        @block.tensor
        def _(pe):
            for c in range(DC):
                for t in range(TT):
                    if c == 0:
                        pe.wait_ge(xn_done, t + 1)
                    last = nc.tensor.transpose(turned[:, c, t * TP:(t + 1) * TP],
                                               xn[:, t, c * 128:(c + 1) * 128], ident[0:TP, 0:TP])
                last.then_inc(turned_done, 1)


def queries(nc, xnT, qT, wq_dram, qw_dram, kw_dram):
    with ExitStack() as ctx:
        p = Phase(nc, ctx, "qry")
        wq = p.sb("wq", [128, DC, NH * HD])
        nw = p.sb("nw", [128, 4])
        eps = p.sb("eps", [128, 2])
        mean_mat = p.sb("mean_mat", [128, 128])
        sq = p.sb("sq", [128, 2, NTOK])
        rs = p.sb("rs", [128, 2, NTOK])
        proj = p.ps("proj", [128, 3, 512])
        mean = p.ps("mean", [128, 2, 512])
        loaded, eps_set, w_done, proj_done, sq_done, mean_done = (p.sem(s) for s in (
            "loaded", "eps_set", "w_done", "proj_done", "sq_done", "mean_done"))
        ln_done, rs_done, q_done = (p.sem(s) for s in ("ln_done", "rs_done", "q_done"))
        block = ctx.enter_context(nc.Block())

        @block.sync
        def _(sp):
            sp.dma_start(wq[:], wq_dram.rearrange("(c p) n -> p c n", p=128)).then_inc(loaded, 16)
            sp.dma_start(nw[:, 0:1], qw_dram).then_inc(loaded, 16)
            sp.dma_start(nw[:, 1:2], kw_dram).then_inc(loaded, 16)

        @block.tensor
        def _(pe):
            pe.wait_ge(loaded, 48)
            pe.wait_ge(eps_set, 3)

            def mean_square(h):
                pe.wait_ge(sq_done, h + 1)
                wait(pe, ln_done, h - 1)
                nc.tensor.matmul(mean[:, h % 2, 0:NTOK], mean_mat[:], sq[:, h % 2, :],
                                 start=True, stop=True).then_inc(mean_done, 1)

            for h in range(NH):
                wait(pe, q_done, h - 2)
                for c in range(DC):
                    last = nc.tensor.matmul(proj[:, h % 3, 0:NTOK], wq[:, c, h * HD:(h + 1) * HD],
                                            xnT[:, c, :], start=(c == 0), stop=(c == DC - 1))
                last.then_inc(proj_done, 1)
                if h >= 1:
                    mean_square(h - 1)
            mean_square(NH - 1)

        @block.scalar
        def _(act):
            nc.scalar.preload_act_table_set(LN_EXP)
            act.wait_ge(eps_set, 3)

            def rstd(h):
                act.wait_ge(mean_done, h + 1)
                wait(act, q_done, h - 1)
                nc.scalar.activation(rs[:, h % 2, :], mean[:, h % 2, 0:NTOK], ACT.Ln,
                                     bias=eps[:, 0:1]).then_inc(ln_done, 1)
                act.wait_ge(ln_done, h + 1)
                nc.scalar.activation(rs[:, h % 2, :], rs[:, h % 2, :], ACT.Exp, scale=-0.5,
                                     bias=eps[:, 1:2]).then_inc(rs_done, 1)

            for h in range(NH):
                act.wait_ge(proj_done, h + 1)
                wait(act, mean_done, h - 1)
                nc.scalar.activation(sq[:, h % 2, :], proj[:, h % 3, 0:NTOK], ACT.Square,
                                     bias=eps[:, 1:2]).then_inc(sq_done, 1)
                if h >= 1:
                    rstd(h - 1)
            rstd(NH - 1)

        @block.vector
        def _(dve):
            nc.vector.memset(eps[:, 0:1], RMS_EPS).then_inc(eps_set, 1)
            nc.vector.memset(eps[:, 1:2], 0.0).then_inc(eps_set, 1)
            nc.vector.memset(mean_mat[:], 1.0 / HD).then_inc(eps_set, 1)
            dve.wait_ge(loaded, 48)
            nc.vector.scalar_tensor_tensor(nw[:, 2:3], nw[:, 0:1], HD ** -0.5, nw[:, 1:2],
                                           ALU.mult, ALU.mult).then_inc(w_done, 1)
            dve.wait_ge(w_done, 1)
            for h in range(NH):
                dve.wait_ge(rs_done, h + 1)
                nc.vector.scalar_tensor_tensor(qT[:, h, :], proj[:, h % 3, 0:NTOK], nw[:, 2:3],
                                               rs[:, h % 2, :], ALU.mult, ALU.mult).then_inc(q_done, 1)



def split_weights(nc, name, pairs):
    with ExitStack() as ctx:
        p = Phase(nc, ctx, name)
        raw = [p.sb(f"raw{i}", list(hi.shape)) for i, (_, hi, _) in enumerate(pairs)]
        loaded = [p.sem(f"loaded{i}") for i in range(len(pairs))]
        hi_done, lo_done = p.sem("hi_done"), p.sem("lo_done")
        block = ctx.enter_context(nc.Block())

        @block.sync
        def _(sp):
            for i, (src, _, _) in enumerate(pairs):
                sp.dma_start(raw[i][:], src).then_inc(loaded[i], 16)

        @block.scalar
        def _(act):
            for i, (_, hi, _) in enumerate(pairs):
                act.wait_ge(loaded[i], 16)
                nc.scalar.activation(hi[:], raw[i][:], ACT.Copy).then_inc(hi_done, 1)

        @block.vector
        def _(dve):
            for i, (_, hi, lo) in enumerate(pairs):
                dve.wait_ge(hi_done, i + 1)
                nc.vector.tensor_tensor(lo[:], raw[i][:], hi[:].bitcast(F32), ALU.subtract).then_inc(lo_done, 1)
            dve.wait_ge(lo_done, len(pairs))


def softmax_attention(nc, qT, rz, ctx_dram, ctxT_dram, wk_dram, wv_dram, ident):
    with ExitStack() as ctx:
        p = Phase(nc, ctx, "att")
        wk = [p.sb(f"wk{i}", [128, DC, G * HD], F32R) for i in range(2)]
        wv = [p.sb(f"wv{i}", [128, DC, G * HD], F32R) for i in range(2)]
        split_weights(nc, "attw", [(w.rearrange("(c p) n -> p c n", p=128), *halves)
                                   for w, halves in ((wk_dram, wk), (wv_dram, wv))])
        raw_t = p.sb("raw_t", [128, DC, SK])
        raw_n = p.sb("raw_n", [KP, 2, KT // 2, D])
        ct = [p.sb(f"ct{i}", [128, DC, SK], F32R) for i in range(2)]
        cn = [p.sb(f"cn{i}", [KP, KT, D], F32R) for i in range(2)]
        q = [p.sb(f"q{i}", [128, NH, S], F32R) for i in range(2)]
        work = p.sb("work", [128, 2, CH])
        sq = [p.sb(f"sq{i}", [128, 2, CH], F32R) for i in range(2)]
        mean_mat = p.sb("mean_mat", [128, 128], F32R)
        k = [p.sb(f"k{i}", [128, 2, SK], F32R) for i in range(2)]
        pr = p.sb("pr", [TP, 4, SK])
        mn = p.sb("mn", [TP, 4, KC])
        nmx = p.sb("nmx", [TP, 4])
        z = p.sb("z", [TP, NJ, KC])
        zsum = p.sb("zsum", [TP, NJ])
        pT = [p.sb(f"pT{i}", [KP, 3, QU], F32R) for i in range(2)]
        cs = [p.sb(f"cs{i}", [128, DC, QU], F32R) for i in range(2)]
        eps = p.sb("eps", [128, 2])
        proj = p.ps("proj", [128, 2, 512])
        mean = p.ps("mean", [128, 512])
        ring = p.ps("ring", [128, 3, 512])
        csum = p.ps("csum", [128, 2, 512])

        eps_set = p.sem("eps_set")
        t_loaded = p.sem("t_loaded")
        n_loaded = [p.sem(f"n_loaded{i}") for i in range(2)]
        t_hi, t_lo, n_hi, n_lo, q_hi, q_lo = (p.sem(s) for s in ("t_hi", "t_lo", "n_hi", "n_lo", "q_hi", "q_lo"))
        proj_done, sq_done, sq_hi, sq_lo, mean_done, ln_done, rs_done = (p.sem(s) for s in (
            "proj_done", "sq_done", "sq_hi", "sq_lo", "mean_done", "ln_done", "rs_done"))
        k_full, k_hi, k_lo = (p.sem(s) for s in ("k_full", "k_hi", "k_lo"))
        ring_full, ring_free = p.sem("ring_full"), p.sem("ring_free")
        nmx_done, exp_done, rz_done = (p.sem(s) for s in ("nmx_done", "exp_done", "rz_done"))
        pT_hi, pv_done, cs_hi, cs_lo = (p.sem(s) for s in ("pT_hi", "pv_done", "cs_hi", "cs_lo"))
        out_full, out_free, zsum_done = p.sem("out_full"), p.sem("out_free"), p.sem("zsum_done")
        block = ctx.enter_context(nc.Block())

        NE = 3 + KC
        NS = 2 * KC
        NSC = 4 * KC
        NR = NSC + KT
        PIECES = DC * KC
        SEQ = [(0, 0), (0, 1), (1, 0), (1, 1), (0, 2), (0, 3), (1, 2), (1, 3), (0, 4), (0, 5), (1, 4), (1, 5)]
        SPLIT_AT = {2: 0, 5: 1, 6: 2, 8: 3, 9: 4, 10: 5}

        @block.sync
        def _(sp):
            def load_t(b):
                wait(sp, t_lo, b * PIECES)
                src = ctxT_dram[bass.ds(b, 1), :, :] if not isinstance(b, int) else ctxT_dram[b:b + 1, :, :]
                sp.dma_start(raw_t[:], src.rearrange("a (c p) n -> p (a c) n", p=128)).then_inc(t_loaded, 16)

            def load_n(b):
                for half in range(2):
                    wait(sp, n_lo, (b - 1) * KT + (half + 1) * (KT // 2))
                    rows = slice(half * (SK // 2), (half + 1) * (SK // 2))
                    src = ctx_dram[bass.ds(b, 1), rows, :] if not isinstance(b, int) else ctx_dram[b:b + 1, rows, :]
                    sp.dma_start(raw_n[:, half], src.rearrange("a (j p) c -> p (a j) c", p=KP))\
                        .then_inc(n_loaded[half], 16)

            for b in range(2):
                load_t(b)
                load_n(b)
            with sp.Fori(2, B) as b:
                load_t(b)
                load_n(b)

        @block.tensor
        def _(pe):
            def key_step(b, u, part, i):
                n = (2 * b + u) * NS + i
                c, g = i // 2, 2 * u + i % 2
                if part == 0:
                    if u == 0 and i % 2 == 0:
                        wait(pe, t_lo, b * PIECES + DC * (c + 1))
                    wait(pe, k_full, n - 1)
                    for d in range(DC):
                        last = mm3(nc, proj[:, i % 2, 0:CH], wk[0][:, d, g * HD:(g + 1) * HD],
                                   wk[1][:, d, g * HD:(g + 1) * HD], ct[0][:, d, c * CH:(c + 1) * CH],
                                   ct[1][:, d, c * CH:(c + 1) * CH], d == 0, d == DC - 1)
                    last.then_inc(proj_done, 1)
                else:
                    wait(pe, sq_lo, n + 1)
                    wait(pe, ln_done, n)
                    if i == 0:
                        wait(pe, out_free, 2 * b + u - 1)
                    for half in (1, 0):
                        last = nc.tensor.matmul(mean[:, 0:CH], mean_mat[:], sq[half][:, i % 2, :],
                                                start=(half == 1), stop=(half == 0))
                    last.then_inc(mean_done, 1)

            def output(b, u, ahead=NS):
                wait(pe, cs_lo, (2 * b + u + 1) * DC)
                wait(pe, ln_done, (2 * b + u + 1) * NS + ahead)
                wait(pe, out_free, 2 * b + u)
                for gi in range(2):
                    w = slice((2 * u + gi) * HD, (2 * u + gi + 1) * HD)
                    x = slice(gi * QG, (gi + 1) * QG)
                    for i in range(DC):
                        last = mm3(nc, mean[:, x], wv[0][:, i, w], wv[1][:, i, w],
                                   cs[0][:, i, x], cs[1][:, i, x], i == 0, i == DC - 1)
                last.then_inc(out_full, 1)

            def scores(b, u):
                for j in range(4):
                    gi = j // 2
                    for c in range(KC):
                        r = (2 * b + u) * NR + j * KC + c
                        if j % 2 == 0:
                            wait(pe, k_lo, (2 * b + u) * NS + 2 * c + gi + 1)
                        if u == 0 and j == 0 and c == 0:
                            wait(pe, q_lo, 2 * (b + 1))
                        wait(pe, ring_free, r - 2)
                        h = 8 * u + 2 * j
                        mm3(nc, ring[0:TP, c, 0:CH], q[0][:, h:h + 2, :], q[1][:, h:h + 2, :],
                            k[0][:, gi, c * CH:(c + 1) * CH], k[1][:, gi, c * CH:(c + 1) * CH],
                            True, True).then_inc(ring_full, 1)

            def unit(b, u, keys, before):
                def turn(t):
                    if t % TPC == 0:
                        wait(pe, exp_done, (2 * b + u) * NE + 3 + t // TPC + 1)
                    wait(pe, ring_free, (2 * b + u) * NR + NSC + t - 2)
                    for j in range(4):
                        last = nc.tensor.transpose(ring[0:KP, t % 3, j * TP:(j + 1) * TP],
                                                   pr[:, j, t * KP:(t + 1) * KP], ident[0:TP, 0:TP])
                    last.then_inc(ring_full, 1)

                if keys:
                    key_step(*keys, *SEQ[0])
                    key_step(*keys, *SEQ[1])
                turn(0)
                turn(1)
                if before:
                    output(*before)
                for t in range(KT):
                    if t + 2 < KT:
                        turn(t + 2)
                    wait(pe, ring_free, (2 * b + u) * NR + NSC + t + 1)
                    if u == 0:
                        wait(pe, n_lo, b * KT + t + 1)
                    if t == 0:
                        wait(pe, cs_lo, (2 * b + u) * DC)
                    for i in range(DC):
                        last = mm3(nc, csum[:, i, 0:QU], cn[0][:, t, i * 128:(i + 1) * 128],
                                   cn[1][:, t, i * 128:(i + 1) * 128], pT[0][:, t % 3, :], pT[1][:, t % 3, :],
                                   t == 0, t == KT - 1)
                    last.then_inc(pv_done, 1)
                    if keys and t + 2 < len(SEQ):
                        key_step(*keys, *SEQ[t + 2])

            def batch(b, first, last):
                scores(b, 0)
                unit(b, 0, (b, 1), None if first else (b - 1, 1))
                scores(b, 1)
                unit(b, 1, None if last else (b + 1, 0), (b, 0))

            pe.wait_ge(eps_set, 4)
            for part, i in SEQ:
                key_step(0, 0, part, i)
            batch(0, True, False)
            with pe.Fori(1, B - 1) as b:
                batch(b, False, False)
            batch(B - 1, False, True)
            output(B - 1, 1, 0)

        @block.scalar
        def _(act):
            def split_t(b, n):
                c, d = n // DC, n % DC
                wait(act, t_loaded, 16 * (b + 1))
                wait(act, proj_done, (2 * b - 1) * NS + 2 * (c + 1))
                nc.scalar.activation(ct[0][:, d, c * CH:(c + 1) * CH], raw_t[:, d, c * CH:(c + 1) * CH],
                                     ACT.Copy).then_inc(t_hi, 1)

            def key_step(b, u, part, i):
                n = (2 * b + u) * NS + i
                if part == 0:
                    wait(act, proj_done, n + 1)
                    wait(act, k_lo, n - 1)
                    nc.scalar.activation(work[:, i % 2, :], proj[:, i % 2, 0:CH], ACT.Square,
                                         bias=eps[:, 1:2]).then_inc(sq_done, 1)
                else:
                    wait(act, mean_done, n + 1)
                    nc.scalar.activation(work[:, i % 2, :], mean[:, 0:CH], ACT.Ln, bias=eps[:, 0:1]).then_inc(ln_done, 1)
                    wait(act, ln_done, n + 1)
                    nc.scalar.activation(work[:, i % 2, :], work[:, i % 2, :], ACT.Exp, scale=-0.5,
                                         bias=eps[:, 1:2]).then_inc(rs_done, 1)

            def exponential(u, j, c, keys):
                nc.scalar.activation(pr[:, j, keys], pr[:, j, keys], ACT.Exp, scale=-1.0, bias=nmx[:, j:j + 1],
                                     accum_out=z[:, 4 * u + j, c:c + 1]).then_inc(exp_done, 1)

            def exponentials(b, u):
                for j in range(4):
                    wait(act, nmx_done, b * NJ + 4 * u + j + 1)
                    if u == 0 and j == 0:
                        wait(act, rz_done, b)
                    exponential(u, j, 0, slice(0, CH if j == 3 else SK))

            def unit(b, u, keys, pieces):
                if keys:
                    key_step(*keys, *SEQ[0])
                for t in range(KT):
                    wait(act, ring_full, (2 * b + u) * NR + NSC + t + 1)
                    wait(act, pv_done, (2 * b + u) * KT + t - 2)
                    nc.scalar.activation(pT[0][:, t % 3, :], ring[0:KP, t % 3, 0:QU], ACT.Copy).then_inc(pT_hi, 1)
                    if t + 1 < KC:
                        exponential(u, 3, t + 1, slice((t + 1) * CH, (t + 2) * CH))
                    if keys and t >= 1:
                        key_step(*keys, *SEQ[t])
                    if pieces is not None and t in SPLIT_AT:
                        split_t(pieces, SPLIT_AT[t])
                wait(act, pv_done, (2 * b + u + 1) * KT)
                wait(act, out_full, 2 * b + u)
                for i in range(DC):
                    nc.scalar.activation(cs[0][:, i, :], csum[:, i, 0:QU], ACT.Copy).then_inc(cs_hi, 1)

            def batch(b, last):
                exponentials(b, 0)
                unit(b, 0, (b, 1), None if last else b + 1)
                exponentials(b, 1)
                unit(b, 1, None if last else (b + 1, 0), None)

            nc.scalar.preload_act_table_set(LN_EXP)
            act.wait_ge(eps_set, 4)
            for n in range(PIECES):
                split_t(0, n)
            for part, i in SEQ:
                key_step(0, 0, part, i)
            batch(0, False)
            with act.Fori(1, B - 1) as b:
                batch(b, False)
            batch(B - 1, True)

        @block.vector
        def _(dve):
            def split_t(b, n):
                wait(dve, t_hi, b * PIECES + n + 1)
                x = (slice(None), n % DC, slice(n // DC * CH, (n // DC + 1) * CH))
                nc.vector.tensor_tensor(ct[1][x], raw_t[x], ct[0][x].bitcast(F32), ALU.subtract).then_inc(t_lo, 1)

            def split_n(b, t):
                half, j = divmod(t, KT // 2)
                wait(dve, n_loaded[half], 16 * (b + 1))
                wait(dve, pv_done, (2 * b - 1) * KT + t + 1)
                nc.vector.tensor_copy(cn[0][:, t, :], raw_n[:, half, j, :]).then_inc(n_hi, 1)

            def split_q(b, half):
                wait(dve, ring_full, (2 * b - 1) * NR + NSC)
                for y in (slice(0, NH // 2), slice(NH // 2, NH)):
                    src = qT[:, y, bass.ds(b * S, S)] if not isinstance(b, int) else qT[:, y, b * S:(b + 1) * S]
                    if half == 0:
                        nc.vector.tensor_scalar(q[0][:, y], src, 1.0, None, ALU.mult).then_inc(q_hi, 1)
                    else:
                        wait(dve, q_hi, 2 * (b + 1))
                        nc.vector.tensor_tensor(q[1][:, y], src, q[0][:, y].bitcast(F32), ALU.subtract).then_inc(q_lo, 1)

            def key_step(b, u, part, i):
                n = (2 * b + u) * NS + i
                c, gi = i // 2, i % 2
                if part == 0:
                    wait(dve, sq_done, n + 1)
                    wait(dve, mean_done, n - 1)
                    nc.vector.tensor_copy(sq[0][:, i % 2, :], work[:, i % 2, :]).then_inc(sq_hi, 1)
                else:
                    wait(dve, rs_done, n + 1)
                    nc.vector.tensor_tensor(work[:, i % 2, :], proj[:, i % 2, 0:CH], work[:, i % 2, :],
                                            ALU.mult).then_inc(k_full, 1)
                    wait(dve, k_full, n + 1)
                    if i == 0:
                        wait(dve, ring_full, (2 * b + u - 1) * NR + NSC)
                    nc.vector.tensor_copy(k[0][:, gi, c * CH:(c + 1) * CH], work[:, i % 2, :]).then_inc(k_hi, 1)

            def split_sums(b, u):
                for i in range(DC):
                    wait(dve, cs_hi, (2 * b + u) * DC + i + 1)
                    nc.vector.tensor_tensor(cs[1][:, i, :], csum[:, i, 0:QU], cs[0][:, i, :].bitcast(F32),
                                            ALU.subtract).then_inc(cs_lo, 1)

            def output(b, u):
                wait(dve, out_full, 2 * b + u + 1)
                x = bass.ds(b * S, S) if not isinstance(b, int) else slice(b * S, (b + 1) * S)
                nc.vector.tensor_scalar(qT[:, 8 * u:8 * u + 8, x],
                                        mean[:, 0:QU].rearrange("p (h t) -> p h t", t=S), 1.0, None,
                                        ALU.mult).then_inc(out_free, 1)

            def scores(b, u, before):
                for j in range(4):
                    for c in range(KC):
                        wait(dve, ring_full, (2 * b + u) * NR + j * KC + c + 1)
                        if j == 0 and c == 0:
                            wait(dve, ring_full, (2 * b + u) * NR)
                        if c == 0:
                            wait(dve, exp_done, (2 * b + u - 1) * NE + (j + 1 if j < 3 else NE))
                        nc.vector.tensor_scalar(pr[:, j, c * CH:(c + 1) * CH], ring[0:TP, c, 0:CH], -1.0, 3.0e38,
                                                ALU.mult, ALU.min, accum_out=mn[:, j, c:c + 1]).then_inc(ring_free, 1)
                    wait(dve, ring_free, (2 * b + u) * NR + (j + 1) * KC)
                    nc.vector.tensor_reduce(nmx[:, j:j + 1], mn[:, j, :], AX, ALU.min).then_inc(nmx_done, 1)
                if before:
                    split_sums(*before)

            def unit(b, u, keys, pieces, before):
                if keys:
                    key_step(*keys, *SEQ[0])
                for t in range(KT):
                    wait(dve, pT_hi, (2 * b + u) * KT + t + 1)
                    nc.vector.tensor_tensor(pT[1][:, t % 3, :], ring[0:KP, t % 3, 0:QU],
                                            pT[0][:, t % 3, :].bitcast(F32), ALU.subtract).then_inc(ring_free, 1)
                    if t == 0 and before:
                        output(*before)
                    if keys and t >= 1:
                        key_step(*keys, *SEQ[t])
                    if pieces is not None and t in SPLIT_AT:
                        split_t(pieces, SPLIT_AT[t])
                    if u == 1 and keys and t in (2, 6):
                        split_q(keys[0], (2, 6).index(t))
                    if u == 1 and keys and t >= 3:
                        split_n(keys[0], t - 3)
                    if u == 1 and t == 2:
                        wait(dve, exp_done, (2 * b + 2) * NE)
                        nc.vector.tensor_reduce(zsum[:], z[:], AX, ALU.add).then_inc(zsum_done, 1)
                        wait(dve, zsum_done, b + 1)
                        x = bass.ds(b * NJ, NJ) if not isinstance(b, int) else slice(b * NJ, (b + 1) * NJ)
                        nc.vector.reciprocal(rz[:, x], zsum[:]).then_inc(rz_done, 1)
                if u == 1 and keys:
                    for t in range(KT - 3, KT):
                        split_n(keys[0], t)

            def batch(b, first, last):
                before = None if first else (b - 1, 1)
                scores(b, 0, before)
                unit(b, 0, (b, 1), None if last else b + 1, before)
                scores(b, 1, (b, 0))
                unit(b, 1, None if last else (b + 1, 0), None, (b, 0))

            nc.vector.memset(eps[:, 0:1], RMS_EPS).then_inc(eps_set, 1)
            nc.vector.memset(eps[:, 1:2], 0.0).then_inc(eps_set, 1)
            nc.vector.memset(mean_mat[:].bitcast(F32), 1.0 / HD).then_inc(eps_set, 1)
            nc.vector.memset(z[:], 0.0).then_inc(eps_set, 1)
            for n in range(PIECES):
                split_t(0, n)
            split_q(0, 0)
            split_q(0, 1)
            for t in range(KT):
                split_n(0, t)
            for part, i in SEQ:
                key_step(0, 0, part, i)
            batch(0, True, False)
            with dve.Fori(1, B - 1) as b:
                batch(b, False, False)
            batch(B - 1, False, True)
            split_sums(B - 1, 1)
            output(B - 1, 1)
            dve.wait_ge(out_free, 2 * B)
            dve.wait_ge(rz_done, B)

        @block.gpsimd
        def _(pool):
            def key_step(b, u, part, i):
                n = (2 * b + u) * NS + i
                c, gi = i // 2, i % 2
                if part == 0:
                    wait(pool, sq_hi, n + 1)
                    nc.gpsimd.tensor_tensor(sq[1][:, i % 2, :], work[:, i % 2, :], sq[0][:, i % 2, :].bitcast(F32),
                                            ALU.subtract).then_inc(sq_lo, 1)
                else:
                    wait(pool, k_hi, n + 1)
                    x = (slice(None), gi, slice(c * CH, (c + 1) * CH))
                    nc.gpsimd.tensor_tensor(k[1][x], work[:, i % 2, :], k[0][x].bitcast(F32),
                                            ALU.subtract).then_inc(k_lo, 1)

            N_AFTER = {3: (0,), 6: (1, 2), 7: (3, 4), 11: range(5, KT)}

            def split_n(b, t):
                half, j = divmod(t, KT // 2)
                wait(pool, n_hi, b * KT + t + 1)
                nc.gpsimd.tensor_tensor(cn[1][:, t, :], raw_n[:, half, j, :], cn[0][:, t, :].bitcast(F32),
                                        ALU.subtract).then_inc(n_lo, 1)

            def batch(b, last):
                for part, i in SEQ:
                    key_step(b, 1, part, i)
                if not last:
                    for s, (part, i) in enumerate(SEQ):
                        key_step(b + 1, 0, part, i)
                        for t in N_AFTER.get(s, ()):
                            split_n(b + 1, t)

            for part, i in SEQ:
                key_step(0, 0, part, i)
            for t in range(KT):
                split_n(0, t)
            batch(0, False)
            with pool.Fori(1, B - 1) as b:
                batch(b, False)
            batch(B - 1, True)


def attention_output(nc, x, oT, rz, wo_dram, ident, load_next):
    with ExitStack() as ctx:
        p = Phase(nc, ctx, "wo")
        wo = p.sb("wo", [128, NH, D])
        ones_mat = p.sb("ones_mat", [TP, 128])
        diag = p.sb("diag", [TP, 2, NJ, TP])
        spread = p.ps("spread", [128, 2, 2, 512])
        out = p.ps("out", [128, 2, 512])
        ones_set, loaded, diag_done, spread_done, scaled, out_done, added = (p.sem(s) for s in (
            "ones_set", "loaded", "diag_done", "spread_done", "scaled", "out_done", "added"))
        block = ctx.enter_context(nc.Block())

        @block.sync
        def _(sp):
            sp.dma_start(wo[:], wo_dram.rearrange("(h p) n -> p h n", p=128)).then_inc(loaded, 16)
            load_next(sp)

        @block.vector
        def _(dve):
            def scale(b):
                for i in range(2):
                    dve.wait_ge(spread_done, b + 1)
                    y = oT[:, 8 * i:8 * i + 8, b * S:(b + 1) * S]
                    nc.vector.tensor_tensor(y, y, spread[:, b % 2, i, 0:QU].rearrange("p (h t) -> p h t", t=S),
                                            ALU.mult).then_inc(scaled, 1)

            for b in range(B):
                wait(dve, spread_done, b - 1)
                nc.vector.tensor_tensor(diag[:, b % 2], ident[0:TP, None, 0:TP].to_broadcast([TP, NJ, TP]),
                                        rz[:, b * NJ:(b + 1) * NJ].unsqueeze(2).to_broadcast([TP, NJ, TP]),
                                        ALU.mult).then_inc(diag_done, 1)
                if b >= 1:
                    scale(b - 1)
            scale(B - 1)
            for t in range(TT):
                dve.wait_ge(out_done, t + 1)
                nc.vector.tensor_tensor(x[:, t, :], x[:, t, :], out[0:TP, t % 2, 0:D], ALU.add).then_inc(added, 1)
            dve.wait_ge(added, TT)

        @block.gpsimd
        def _(pool):
            nc.gpsimd.memset(ones_mat[:], 1.0).then_inc(ones_set, 1)

        @block.tensor
        def _(pe):
            pe.wait_ge(ones_set, 1)
            for b in range(B):
                pe.wait_ge(diag_done, b + 1)
                wait(pe, scaled, 2 * (b - 1))
                for i in range(2):
                    last = nc.tensor.matmul(spread[:, b % 2, i, 0:QU], ones_mat[:],
                                            diag[:, b % 2, 4 * i:4 * i + 4, :], start=True, stop=True)
                last.then_inc(spread_done, 1)
            pe.wait_ge(loaded, 16)
            for t in range(TT):
                pe.wait_ge(scaled, 2 * (2 * t + 2))
                wait(pe, added, t - 1)
                for h in range(NH):
                    last = nc.tensor.matmul(out[0:TP, t % 2, 0:D], oT[:, h, t * TP:(t + 1) * TP], wo[:, h, :],
                                            start=(h == 0), stop=(h == NH - 1))
                last.then_inc(out_done, 1)


class Weights:

    def __init__(self, nc, ctx, name, drams, shared_blocks, logits):
        p = Phase(nc, ctx, name)
        self.drams, self.shared_blocks, self.logits = drams, shared_blocks, logits
        self.blocks = E * EB + shared_blocks
        self.gate = p.sb("gate", [128, DC, self.blocks * HB])
        self.up = p.sb("up", [128, DC, self.blocks * HB])
        self.down = p.sb("down", [HB, self.blocks, D])
        self.router = p.sb("router", [128, DC, E + 1])
        self.router_loaded, self.loaded = p.sem("router_loaded"), p.sem("loaded")

    def load(self, sp):
        gate, up, down, router = self.drams
        sp.dma_start(self.router[:, :, 0:self.logits], router.rearrange("(c p) n -> p c n", p=128))\
            .then_inc(self.router_loaded, 16)
        sp.dma_start(self.gate[:], gate.rearrange("(c p) n -> p c n", p=128)).then_inc(self.loaded, 16)
        sp.dma_start(self.up[:], up.rearrange("(c p) n -> p c n", p=128)).then_inc(self.loaded, 16)
        sp.dma_start(self.down[:], down.rearrange("(m p) n -> p m n", p=HB)).then_inc(self.loaded, 16)


def mixture(nc, name, x, xnT, xn, weights, before, normalise, shared_gate=False):
    with ExitStack() as ctx:
        p = Phase(nc, ctx, name)
        wide = [p.sb(f"wide{i}", [128, 3, 2, DC, 2 * HB], F32R) for i in range(2)]
        wd = [p.sb(f"wd{i}", [HB, 3, 2, D], F32R) for i in range(2)]
        hid = [p.sb(f"hid{i}", [HB, 4, NTOK], F32R) for i in range(2)]
        silu = p.sb("silu", [HB, 2, NTOK])
        full = p.sb("full", [HB, 2, NTOK])
        logit = p.sb("logit", [TP, TT, E + 1])
        mx = p.sb("mx", [TP, TT])
        prob = p.sb("prob", [TP, TT, E])
        tot = p.sb("tot", [TP, TT])
        rank = p.sb("rank", [TP, TT, E, E])
        same = p.sb("same", [TP, TT, E, E])
        place = p.sb("place", [TP, TT, E])
        share = p.sb("share", [TP, TT])
        comb = p.sb("comb", [TP, TT, E + 1])
        zero = p.sb("zero", [128, 1])
        gate = p.ps("gate", [128, 2, 512])
        up = p.ps("up", [128, 2, 512])
        down = p.ps("down", [128, 2, 512])
        lg = p.ps("lg", [128, 512])

        lg_done, r, gates_done, silu_done, hid_done, down_done, added, act_r = (p.sem(s) for s in (
            "lg_done", "route_step", "gates_done", "silu_done", "hid_done", "down_done", "added", "act_step"))
        hid_hi, hid_lo, w_hi, w_lo = (p.sem(s) for s in ("hid_hi", "hid_lo", "w_hi", "w_lo"))
        block = ctx.enter_context(nc.Block())

        pairs = weights.blocks // 2
        nl = weights.logits
        NW = 3

        @block.tensor
        def _(pe):
            pe.wait_ge(weights.router_loaded, 16)
            for t in range(TT):
                for c in range(DC):
                    last = nc.tensor.matmul(lg[0:TP, t * 16:t * 16 + nl], xnT[:, c, t * TP:(t + 1) * TP],
                                            weights.router[:, c, 0:nl], start=(c == 0), stop=(c == DC - 1))
            last.then_inc(lg_done, 1)

            def widen(n):
                y = slice(n % 2 * HB, (n % 2 + 1) * HB)
                pe.wait_ge(w_lo, NW * (n // 2 + 1))
                wait(pe, hid_done, n - 1)
                for i, out in enumerate((gate, up)):
                    for c in range(DC):
                        w = [half[:, n // 2 % 3, i, c, y] for half in wide]
                        last = mm3(nc, out[0:HB, n % 2, 0:NTOK], *w, xn[0][:, c, :], xn[1][:, c, :],
                                   c == 0, c == DC - 1)
                last.then_inc(gates_done, 1)

            def narrow(i):
                for half in range(2):
                    wait(pe, added, 4 * i + 2 * half - 2)
                    for t in (2 * half, 2 * half + 1):
                        for n in (2 * i, 2 * i + 1):
                            wait(pe, hid_lo, n + 1)
                            h = [part[:, n % 4, t * TP:(t + 1) * TP] for part in hid]
                            last = mm3(nc, down[0:TP, half, (t % 2) * D:(t % 2 + 1) * D], *h,
                                       wd[0][:, i % 3, n % 2, :], wd[1][:, i % 3, n % 2, :],
                                       n % 2 == 0, n % 2 == 1)
                    last.then_inc(down_done, 1)

            for i in range(pairs + 1):
                if i < pairs:
                    widen(2 * i)
                    widen(2 * i + 1)
                if i >= 1:
                    narrow(i - 1)

        @block.scalar
        def _(act):
            def split(i):
                if i == 0:
                    act.wait_ge(weights.loaded, 48)
                wait(act, down_done, 2 * (i - 2))
                y = slice(2 * i * HB, 2 * (i + 1) * HB)
                nc.scalar.activation(wide[0][:, i % 3, 0], weights.gate[:, :, y], ACT.Copy).then_inc(w_hi, 1)
                nc.scalar.activation(wide[0][:, i % 3, 1], weights.up[:, :, y], ACT.Copy).then_inc(w_hi, 1)
                nc.scalar.activation(wd[0][:, i % 3], weights.down[:, 2 * i:2 * i + 2, :], ACT.Copy).then_inc(w_hi, 1)

            split(0)
            act.wait_ge(r, 4)
            nc.scalar.activation(prob[:], prob[:], ACT.Exp, bias=zero[0:TP, 0:1]).then_inc(act_r, 1)
            if shared_gate:
                nc.scalar.activation(share[:], logit[:, :, E], ACT.Exp, scale=-1.0, bias=zero[0:TP, 0:1]).then_inc(act_r, 1)
            split(1)
            for i in range(pairs):
                for n in (2 * i, 2 * i + 1):
                    act.wait_ge(gates_done, n + 1)
                    wait(act, hid_done, n - 1)
                    nc.scalar.activation(silu[:, n % 2, :], gate[0:HB, n % 2, 0:NTOK], ACT.Silu,
                                         bias=zero[0:HB, 0:1]).then_inc(silu_done, 1)
                for n in (2 * i, 2 * i + 1):
                    act.wait_ge(hid_done, n + 1)
                    wait(act, down_done, 2 * (i - 1))
                    nc.scalar.activation(hid[0][:, n % 4, :], full[:, n % 2, :], ACT.Copy).then_inc(hid_hi, 1)
                if i + 2 < pairs:
                    split(i + 2)

        @block.gpsimd
        def _(pool):
            for i in range(pairs):
                y = slice(2 * i * HB, 2 * (i + 1) * HB)
                for k, (hi, lo, raw) in enumerate((
                        (wide[0][:, i % 3, 0], wide[1][:, i % 3, 0], weights.gate[:, :, y]),
                        (wide[0][:, i % 3, 1], wide[1][:, i % 3, 1], weights.up[:, :, y]),
                        (wd[0][:, i % 3], wd[1][:, i % 3], weights.down[:, 2 * i:2 * i + 2, :]))):
                    pool.wait_ge(w_hi, NW * i + k + 1)
                    nc.gpsimd.tensor_tensor(lo, raw, hi.bitcast(F32), ALU.subtract).then_inc(w_lo, 1)

        @block.vector
        def _(dve):
            step = [0]

            def then(ins):
                step[0] += 1
                ins.then_inc(r, 1)
                dve.wait_ge(r, step[0])

            then(nc.vector.memset(zero[:], 0.0))
            dve.wait_ge(lg_done, 1)
            then(nc.vector.tensor_copy(logit[:, :, 0:nl], lg[0:TP, 0:TT * 16].rearrange("p (t n) -> p t n", n=16)[:, :, 0:nl]))
            then(nc.vector.tensor_reduce(mx[:], logit[:, :, 0:E], AX, ALU.max))
            then(nc.vector.tensor_tensor(prob[:], logit[:, :, 0:E], mx[:].unsqueeze(2).to_broadcast([TP, TT, E]),
                                         ALU.subtract))
            dve.wait_ge(act_r, 1)
            then(nc.vector.tensor_reduce(tot[:], prob[:], AX, ALU.add))
            then(nc.vector.reciprocal(tot[:], tot[:]))
            then(nc.vector.tensor_tensor(prob[:], prob[:], tot[:].unsqueeze(2).to_broadcast([TP, TT, E]), ALU.mult))
            for t in range(TT):
                mine = prob[:, t, :].unsqueeze(2).to_broadcast([TP, E, E])
                other = prob[:, t, :].unsqueeze(1).to_broadcast([TP, E, E])
                then(nc.vector.tensor_tensor(rank[:, t], other, mine, ALU.is_gt))
                then(nc.vector.tensor_tensor(same[:, t], other, mine, ALU.is_equal))
                then(nc.vector.tensor_tensor(same[:, t], same[:, t], before[0:TP], ALU.mult))
            then(nc.vector.tensor_tensor(rank[:], rank[:], same[:], ALU.add))
            then(nc.vector.tensor_reduce(place[:], rank[:], AX, ALU.add))
            then(nc.vector.tensor_scalar(place[:], place[:], 1.5, None, ALU.is_lt))
            then(nc.vector.tensor_tensor(comb[:, :, 0:E], place[:], prob[:], ALU.mult))
            if normalise:
                then(nc.vector.tensor_reduce(tot[:], comb[:, :, 0:E], AX, ALU.add))
                then(nc.vector.reciprocal(tot[:], tot[:]))
                then(nc.vector.tensor_tensor(comb[:, :, 0:E], comb[:, :, 0:E],
                                             tot[:].unsqueeze(2).to_broadcast([TP, TT, E]), ALU.mult))
            if shared_gate:
                dve.wait_ge(act_r, 2)
                then(nc.vector.tensor_scalar(share[:], share[:], 1.0, None, ALU.add))
                then(nc.vector.reciprocal(comb[:, :, E], share[:]))
            else:
                then(nc.vector.memset(comb[:, :, E:E + 1], 1.0))

            def hidden(n):
                dve.wait_ge(silu_done, n + 1)
                wait(dve, hid_lo, n - 1)
                nc.vector.tensor_tensor(full[:, n % 2, :], silu[:, n % 2, :], up[0:HB, n % 2, 0:NTOK],
                                        ALU.mult).then_inc(hid_done, 1)

            def split(n):
                dve.wait_ge(hid_hi, n + 1)
                nc.vector.tensor_tensor(hid[1][:, n % 4, :], full[:, n % 2, :], hid[0][:, n % 4, :].bitcast(F32),
                                        ALU.subtract).then_inc(hid_lo, 1)

            def add(i):
                e = min(i, E)
                for t in range(TT):
                    dve.wait_ge(down_done, 2 * i + t // 2 + 1)
                    wait(dve, added, 4 * (i - 1) + t + 1)
                    nc.vector.scalar_tensor_tensor(x[:, t, :], down[0:TP, t // 2, (t % 2) * D:(t % 2 + 1) * D],
                                                   comb[:, t, e:e + 1], x[:, t, :], ALU.mult, ALU.add)\
                        .then_inc(added, 1)

            for i in range(pairs):
                hidden(2 * i)
                hidden(2 * i + 1)
                split(2 * i)
                split(2 * i + 1)
                if i >= 1:
                    add(i - 1)
            add(pairs - 1)
            dve.wait_ge(added, 4 * pairs)


def key_value_sums(nc, kv, ctxT_dram, mask_dram, wk_dram, bk_dram, wv_dram, bv_dram, wf_dram, load_next):
    with ExitStack() as ctx:
        p = Phase(nc, ctx, "kvs")
        wk = [p.sb(f"wk{i}", [128, DC, D], F32R) for i in range(2)]
        wv = [p.sb(f"wv{i}", [128, DC, D], F32R) for i in range(2)]
        split_weights(nc, "kvsw", [(w.rearrange("(c p) n -> p c n", p=128), *halves)
                                   for w, halves in ((wk_dram, wk), (wv_dram, wv))])
        fmap = p.sb("fmap", [128, D])
        f2 = p.sb("f2", [128, 2, D], F32R)
        bk = p.sb("bk", [128, DC])
        bv = p.sb("bv", [KP, D])
        zero = p.sb("zero", [128, 1])
        masks = p.sb("masks", [KP, B * KT])
        mask2 = p.sb("mask2", [KP, B * KT, 2], F32R)
        raw = p.sb("raw", [128, KC, DC, CH])
        ct = [p.sb(f"ct{i}", [128, KC, DC, CH], F32R) for i in range(2)]
        ks = p.sb("ks", [128, KC, 4, CH], F32R)
        vb = p.sb("vb", [KP, 2, KG * GV])
        vs = p.sb("vs", [KP, 2, KG, VW], F32R)
        kp = [p.sb(f"kp{i}", [KP, 2, FEAT], F32R) for i in range(2)]
        keys_ps = p.ps("keys_ps", [128, DC, 512])
        vals_ps = p.ps("vals_ps", [128, 512])
        feat = p.ps("feat", [128, 2, 512])
        sums = p.ps("sums", [128, 3, 512])

        zeros = p.sb("zeros", [KP, KG, 2])
        zeros_set = p.sem("zeros_set")
        const_loaded, fmap_set, f_loaded, f_hi_done, f_split, m_loaded, m_hi, m_lo, vb_set = (p.sem(s) for s in (
            "const_loaded", "fmap_set", "f_loaded", "f_hi_done", "f_split", "m_loaded", "m_hi", "m_lo", "vb_set"))
        loaded = [p.sem(f"loaded{c}") for c in range(KC)]
        t_hi, t_lo, k_done, ks_hi, ks_lo = (p.sem(s) for s in ("t_hi", "t_lo", "k_done", "ks_hi", "ks_lo"))
        v_done, vb_done, v_hi, v_lo, v_mask = (p.sem(s) for s in ("v_done", "vb_done", "v_hi", "v_lo", "v_mask"))
        feat_done, f_hi, f_lo, sums_done, kv_done = (p.sem(s) for s in ("feat_done", "f_hi", "f_lo", "sums_done", "kv_done"))
        block = ctx.enter_context(nc.Block())
        NB = len(SUMS)

        def at_batch(b, t):
            return slice(b * KT + t, b * KT + t + 1) if isinstance(b, int) else bass.ds(b * KT + t, 1)

        def chunk_after(b, t):
            if t % TPC != 1:
                return None
            c = t // TPC + 1
            return (b, c) if c < KC else (b + 1, 0)

        def chunk_to_split(b, t):
            if t % TPC != TPC - 1:
                return None
            c = t // TPC + 2
            return (b, c) if c < KC else (b + 1, c - KC)

        def passes(b, last):
            for t in range(KT):
                project, split = chunk_after(b, t), chunk_to_split(b, t)
                wraps = t // TPC + 1 >= KC, t // TPC + 2 >= KC
                yield (t, None if last and wraps[0] else project, None if last and wraps[1] else split)

        def run_peeled(eng, batch):
            batch(0, False)
            with eng.Fori(1, B - 1) as b:
                batch(b, False)
            batch(B - 1, True)

        @block.sync
        def _(sp):
            sp.dma_start(bk[:], bk_dram).then_inc(const_loaded, 16)
            sp.dma_start(bv[:], bv_dram.partition_broadcast(KP)).then_inc(const_loaded, 16)
            sp.dma_start(masks[:], mask_dram).then_inc(m_loaded, 16)
            sp.wait_ge(fmap_set, 1)
            for h in range(8):
                i = h % 4
                sp.dma_start(fmap[16 * h:16 * h + 16, FD * i:FD * (i + 1)], wf_dram).then_inc(f_loaded, 16)

            def load(b, c):
                wait(sp, t_lo, (b - 1) * KC + c + 1)
                src = ctxT_dram[bass.ds(b, 1), :, c * CH:(c + 1) * CH] if not isinstance(b, int) else \
                    ctxT_dram[b:b + 1, :, c * CH:(c + 1) * CH]
                sp.dma_start(raw[:, c], src.rearrange("a (k p) n -> p (a k) n", p=128)).then_inc(loaded[c], 16)

            for c in range(KC):
                load(0, c)
            load_next(sp)
            with sp.Fori(1, B) as b:
                for c in range(KC):
                    load(b, c)

        @block.tensor
        def _(pe):
            def keys(b, c):
                wait(pe, t_lo, b * KC + c + 1)
                for m in range(DC):
                    wait(pe, ks_lo, 4 * (b * KC + c - 1) + 2 * (m + 1))
                    for i in range(DC):
                        last = mm3(nc, keys_ps[:, m, 0:CH], wk[0][:, i, m * 128:(m + 1) * 128],
                                   wk[1][:, i, m * 128:(m + 1) * 128], ct[0][:, c, i, :], ct[1][:, c, i, :],
                                   i == 0, i == DC - 1)
                    last.then_inc(k_done, 1)

            def values(b, t):
                c, i = divmod(t, TPC)
                x = slice(i * KP, (i + 1) * KP)
                wait(pe, vb_done, b * KT + t)
                for k in range(DC):
                    last = mm3(nc, vals_ps[0:KP, 0:D], ct[0][:, c, k, x], ct[1][:, c, k, x],
                               wv[0][:, k, :], wv[1][:, k, :], k == 0, k == DC - 1)
                last.then_inc(v_done, 1)

            def features(b, t):
                c, i = divmod(t, TPC)
                x = slice(i * KP, (i + 1) * KP)
                wait(pe, ks_lo, 4 * (b * KC + c + 1))
                for half in range(2):
                    wait(pe, f_lo, 2 * (b * KT + t - 1) + half + 1)
                    for g in range(2):
                        y = slice(g * D, (g + 1) * D)
                        for w in (1, 0):
                            last = nc.tensor.matmul(feat[0:KP, half, y], ks[:, c, 2 * half + g, x], f2[:, w, :],
                                                    start=(w == 1), stop=(w == 0), skip_group_check=True)
                    last.then_inc(feat_done, 1)

            def add(b, t):
                n = b * KT + t
                wait(pe, v_lo, n + 1)
                wait(pe, v_mask, n + 1)
                wait(pe, f_lo, 2 * n + 2)
                if t == 0:
                    wait(pe, kv_done, NB * b)
                for g in range(KG):
                    w = min(GF, FEAT - g * GF)
                    for half in (1, 0):
                        last = nc.tensor.matmul(sums[0:VW, g // 2, (g % 2) * GF:(g % 2) * GF + w],
                                                vs[:, t % 2, g, :], kp[half][:, t % 2, g * GF:g * GF + w],
                                                start=(t == 0 and g % 2 == 0 and half == 1),
                                                stop=(t == KT - 1 and g % 2 == 1 and half == 0),
                                                skip_group_check=True)
                last.then_inc(sums_done, 1)

            def batch(b, last):
                for t, project, _ in passes(b, last):
                    values(b, t)
                    features(b, t)
                    if t >= 1:
                        add(b, t - 1)
                    if project is not None:
                        keys(*project)
                add(b, KT - 1)

            pe.wait_ge(f_split, 2)
            keys(0, 0)
            run_peeled(pe, batch)

        @block.scalar
        def _(act):
            def split(b, c):
                wait(act, loaded[c], 16 * (b + 1))
                wait(act, v_done, (b - 1) * KT + TPC * (c + 1))
                nc.scalar.activation(ct[0][:, c], raw[:, c], ACT.Copy).then_inc(t_hi, 1)

            def keys(b, c):
                for m in range(DC):
                    wait(act, k_done, 2 * (b * KC + c) + m + 1)
                    wait(act, feat_done, 2 * ((b - 1) * KT + TPC * (c + 1)))
                    for h in range(2):
                        x = slice(64 * h, 64 * (h + 1))
                        nc.scalar.activation(ks[0:64, c, 2 * m + h, :], keys_ps[x, m, 0:CH], ACT.Identity,
                                             bias=bk[x, m:m + 1]).then_inc(ks_hi, 1)

            def batch(b, last):
                for t, project, to_split in passes(b, last):
                    n = b * KT + t
                    wait(act, sums_done, n - 1)
                    for half in range(2):
                        wait(act, feat_done, 2 * n + half + 1)
                        nc.scalar.activation(kp[0][:, t % 2, half * 512:(half + 1) * 512], feat[0:KP, half, :],
                                             ACT.Relu, bias=zero[0:KP, 0:1]).then_inc(f_hi, 1)
                    wait(act, vb_done, n + 1)
                    nc.scalar.activation(vs[:, t % 2, :, 0:GV], vb[:, t % 2, :].rearrange("p (g v) -> p g v", v=GV),
                                         ACT.Copy, scale=masks[:, at_batch(b, t)]).then_inc(v_hi, 1)
                    if project is not None:
                        keys(*project)
                    if to_split is not None:
                        split(*to_split)
                wait(act, sums_done, (b + 1) * KT)
                for i, (lo, hi) in enumerate(SUMS):
                    dst = kv[:, b, lo:hi] if isinstance(b, int) else kv[:, bass.ds(b, 1), lo:hi]
                    src = sums[0:VW, i, 0:hi - lo] if isinstance(b, int) else sums[0:VW, i:i + 1, 0:hi - lo]
                    nc.scalar.activation(dst, src, ACT.Copy).then_inc(kv_done, 1)

            act.wait_ge(m_loaded, 16)
            act.wait_ge(const_loaded, 32)
            act.wait_ge(vb_set, 2)
            act.wait_ge(f_loaded, 16 * 8)
            nc.scalar.activation(f2[:, 0, :], fmap[:], ACT.Copy).then_inc(f_hi_done, 1)
            split(0, 0)
            split(0, 1)
            keys(0, 0)
            run_peeled(act, batch)
            act.wait_ge(kv_done, NB * B)

        @block.vector
        def _(dve):
            def keys(b, c):
                for m in range(DC):
                    for h in range(2):
                        x = slice(64 * h, 64 * (h + 1))
                        wait(dve, ks_hi, 4 * (b * KC + c) + 2 * m + h + 1)
                        nc.vector.scalar_tensor_tensor(ks[64:128, c, 2 * m + h, :], keys_ps[x, m, 0:CH],
                                                       bk[x, m:m + 1], ks[0:64, c, 2 * m + h, :].bitcast(F32),
                                                       ALU.add, ALU.subtract).then_inc(ks_lo, 1)

            def batch(b, last):
                for t, project, to_split in passes(b, last):
                    n = b * KT + t
                    wait(dve, v_done, n + 1)
                    wait(dve, v_lo, n - 1)
                    nc.vector.tensor_tensor(vb[:, t % 2, 0:D], vals_ps[0:KP, 0:D], bv[:], ALU.add).then_inc(vb_done, 1)
                    for half in range(2):
                        wait(dve, f_hi, 2 * n + half + 1)
                        y = slice(half * 512, (half + 1) * 512)
                        nc.vector.scalar_tensor_tensor(kp[1][:, t % 2, y], feat[0:KP, half, :], 0.0,
                                                       kp[0][:, t % 2, y].bitcast(F32), ALU.max,
                                                       ALU.subtract).then_inc(f_lo, 1)
                    wait(dve, v_hi, n + 1)
                    nc.vector.scalar_tensor_tensor(vs[:, t % 2, :, GV:2 * GV],
                                                   vb[:, t % 2, :].rearrange("p (g v) -> p g v", v=GV),
                                                   masks[:, at_batch(b, t)], vs[:, t % 2, :, 0:GV].bitcast(F32),
                                                   ALU.mult, ALU.subtract).then_inc(v_lo, 1)
                    if project is not None:
                        keys(*project)

            dve.wait_ge(m_lo, 1)
            nc.vector.memset(vb[:], 0.0).then_inc(vb_set, 1)
            nc.vector.memset(zero[:], 0.0).then_inc(vb_set, 1)
            dve.wait_ge(vb_set, 2)
            nc.vector.memset(f2[64:128, 1, :].bitcast(F32), 0.0).then_inc(f_split, 1)
            dve.wait_ge(f_hi_done, 1)
            nc.vector.tensor_tensor(f2[0:64, 1, :], fmap[0:64, :], f2[0:64, 0, :].bitcast(F32),
                                    ALU.subtract).then_inc(f_split, 1)
            keys(0, 0)
            run_peeled(dve, batch)

        @block.gpsimd
        def _(pool):
            nc.gpsimd.memset(fmap[:], 0.0).then_inc(fmap_set, 1)
            pool.wait_ge(m_loaded, 16)
            nc.gpsimd.tensor_copy(mask2[:, :, 0], masks[:]).then_inc(m_hi, 1)
            pool.wait_ge(m_hi, 1)
            nc.gpsimd.tensor_tensor(mask2[:, :, 1], masks[:], mask2[:, :, 0].bitcast(F32), ALU.subtract).then_inc(m_lo, 1)
            nc.gpsimd.memset(zeros[:], 0.0).then_inc(zeros_set, 1)
            pool.wait_ge(zeros_set, 1)
            pool.wait_ge(m_lo, 1)

            def split(b, c):
                wait(pool, t_hi, b * KC + c + 1)
                nc.gpsimd.tensor_tensor(ct[1][:, c], raw[:, c], ct[0][:, c].bitcast(F32), ALU.subtract).then_inc(t_lo, 1)

            def batch(b, last):
                for t, _, to_split in passes(b, last):
                    wait(pool, sums_done, b * KT + t - 1)
                    nc.gpsimd.tensor_tensor(vs[:, t % 2, :, 2 * GV:VW],
                                            mask2[:, at_batch(b, t), :].bitcast(F32).to_broadcast([KP, KG, 2]),
                                            zeros[:], ALU.add).then_inc(v_mask, 1)
                    if to_split is not None:
                        split(*to_split)

            split(0, 0)
            split(0, 1)
            run_peeled(pool, batch)


def linear_readout(nc, x, xnT, kv, wq_dram, bq_dram, wf_dram, wo_dram, bo_dram, ident):
    with ExitStack() as ctx:
        p = Phase(nc, ctx, "lin")
        wq = p.sb("wq", [128, DC, D])
        wo = p.sb("wo", [128, DC, D])
        fmap = p.sb("fmap", [128, 4, 128])
        bq = p.sb("bq", [128, DC])
        bo = p.sb("bo", [TP, D])
        qT = p.sb("qT", [128, DC, NTOK])
        qf = p.sb("qf", [128, NH // 2, NTOK])
        sel = p.sb("sel", [VW, GH, RV])
        kvd = p.sb("kvd", [128, 2, NH // 2, 2 * RV])
        den = p.sb("den", [S, B, NH])
        att = p.sb("att", [S, B, D])
        attT = p.sb("attT", [128, DC, NTOK])
        zero = p.sb("zero", [128, 1])
        q_ps = p.ps("q_ps", [128, 2, 512])
        kv_ps = p.ps("kv_ps", [128, 2, 512])
        out_ps = p.ps("out_ps", [128, 2, 512])
        t_ps = p.ps("t_ps", [128, 2, 512])

        set0, loaded, f_loaded, sel_done = p.sem("set0"), p.sem("loaded"), p.sem("f_loaded"), p.sem("sel_done")
        q_done, qT_done, qf_ps, qf_done, kv_full, kvd_done = (p.sem(s) for s in (
            "q_done", "qT_done", "qf_ps", "qf_done", "kv_full", "kvd_done"))
        read_done, den_done, att_done, t_done, attT_done, y_done, added = (p.sem(s) for s in (
            "read_done", "den_done", "att_done", "t_done", "attT_done", "y_done", "added"))
        block = ctx.enter_context(nc.Block())

        @block.sync
        def _(sp):
            sp.dma_start(wq[:], wq_dram.rearrange("(c p) n -> p c n", p=128)).then_inc(loaded, 16)
            sp.dma_start(wo[:], wo_dram.rearrange("(c p) n -> p c n", p=128)).then_inc(loaded, 16)
            sp.dma_start(bq[:], bq_dram).then_inc(loaded, 16)
            sp.dma_start(bo[:], bo_dram.partition_broadcast(TP)).then_inc(loaded, 16)
            sp.wait_ge(set0, 3)
            for h in range(8):
                sp.dma_start(fmap[16 * h:16 * h + 16, h // 2, FD * (h % 2):FD * (h % 2 + 1)], wf_dram)\
                    .then_inc(f_loaded, 16)

        @block.gpsimd
        def _(pool):
            nc.gpsimd.memset(fmap[:], 0.0).then_inc(set0, 1)
            nc.gpsimd.memset(kvd[:], 0.0).then_inc(set0, 1)
            nc.gpsimd.memset(zero[:], 0.0).then_inc(set0, 1)
            for i in range(GH):
                x = slice(HE * i, HE * (i + 1))
                y = slice(GV + HE * i, GV + HE * (i + 1))
                nc.gpsimd.tensor_tensor(sel[:, i, 0:HE], ident[0:VW, x], ident[0:VW, y], ALU.add).then_inc(sel_done, 1)
                nc.gpsimd.tensor_tensor(sel[:, i, HE:RV], ident[0:VW, 2 * GV:2 * GV + 1],
                                        ident[0:VW, 2 * GV + 1:2 * GV + 2], ALU.add).then_inc(sel_done, 1)

        @block.tensor
        def _(pe):
            pe.wait_ge(loaded, 64)
            for m in range(DC):
                for c in range(DC):
                    last = nc.tensor.matmul(q_ps[:, m, 0:NTOK], wq[:, c, m * 128:(m + 1) * 128], xnT[:, c, :],
                                            start=(c == 0), stop=(c == DC - 1))
                last.then_inc(q_done, 1)
            pe.wait_ge(f_loaded, 16 * 8)
            pe.wait_ge(qT_done, DC)
            for j in range(NH // 2):
                wait(pe, qf_done, j - 1)
                nc.tensor.matmul(q_ps[:, j % 2, 0:NTOK], fmap[:, j % 4, :], qT[:, j // 4, :],
                                 start=True, stop=True).then_inc(qf_ps, 1)
            pe.wait_ge(sel_done, 2 * GH)

            def gather(b):
                wait(pe, kvd_done, 2 * (b - 1))
                for h in range(NH):
                    r = slice(64 * (h % 2), 64 * (h % 2 + 1))
                    c0 = h // 2 * 2 * RV + (h % 2) * RV
                    last = nc.tensor.matmul(kv_ps[r, b % 2, c0:c0 + RV], kv[:, b, h * FD:(h + 1) * FD],
                                            sel[:, h % GH, :], start=True, stop=True, skip_group_check=True)
                last.then_inc(kv_full, 1)

            def read(b):
                wait(pe, kvd_done, 2 * (b + 1))
                wait(pe, qf_done, NH // 2)
                wait(pe, att_done, b - 1)
                for j in range(NH // 2):
                    last = nc.tensor.matmul(out_ps[0:S, b % 2, j * 2 * RV:(j + 1) * 2 * RV],
                                            qf[:, j, b * S:(b + 1) * S], kvd[:, b % 2, j, :], start=True, stop=True)
                last.then_inc(read_done, 1)

            def turn(b):
                wait(pe, att_done, b + 1)
                for c in range(DC):
                    last = nc.tensor.transpose(t_ps[:, c, b * S:(b + 1) * S], att[:, b, c * 128:(c + 1) * 128],
                                               ident[0:S, 0:S])
                last.then_inc(t_done, 1)

            for b in range(B + 2):
                if b < B:
                    gather(b)
                if 1 <= b <= B:
                    read(b - 1)
                if b >= 2:
                    turn(b - 2)
            pe.wait_ge(attT_done, DC)
            for t in range(TT):
                wait(pe, added, 2 * (t - 1))
                for c in range(DC):
                    last = nc.tensor.matmul(q_ps[0:TP, t % 2, 0:D], attT[:, c, t * TP:(t + 1) * TP], wo[:, c, :],
                                            start=(c == 0), stop=(c == DC - 1))
                last.then_inc(y_done, 1)

        @block.scalar
        def _(act):
            act.wait_ge(set0, 3)
            act.wait_ge(loaded, 64)
            for m in range(DC):
                act.wait_ge(q_done, m + 1)
                nc.scalar.activation(qT[:, m, :], q_ps[:, m, 0:NTOK], ACT.Identity, bias=bq[:, m:m + 1]).then_inc(qT_done, 1)
            for j in range(NH // 2):
                act.wait_ge(qf_ps, j + 1)
                nc.scalar.activation(qf[:, j, :], q_ps[:, j % 2, 0:NTOK], ACT.Relu, bias=zero[:, 0:1]).then_inc(qf_done, 1)

        @block.vector
        def _(dve):
            dve.wait_ge(set0, 3)

            def diagonal(b):
                dve.wait_ge(kv_full, b + 1)
                wait(dve, read_done, b - 1)
                src = kv_ps[:, b % 2, 0:NH * RV].rearrange("p (j n) -> p j n", n=2 * RV)
                for i in range(2):
                    r, c = slice(64 * i, 64 * (i + 1)), slice(RV * i, RV * (i + 1))
                    nc.vector.tensor_copy(kvd[r, b % 2, :, c], src[r, :, c]).then_inc(kvd_done, 1)

            def divide(b):
                dve.wait_ge(read_done, b + 1)
                o = out_ps[0:S, b % 2, 0:NH * RV].rearrange("p (h n) -> p h n", n=RV)
                nc.vector.tensor_scalar(den[:, b, :], o[:, :, HE], 1e-8, None, ALU.add).then_inc(den_done, 1)
                dve.wait_ge(den_done, 2 * b + 1)
                nc.vector.reciprocal(den[:, b, :], den[:, b, :]).then_inc(den_done, 1)
                dve.wait_ge(den_done, 2 * b + 2)
                nc.vector.tensor_tensor(att[:, b, :].rearrange("p (h n) -> p h n", n=HE), o[:, :, 0:HE],
                                        den[:, b, :].unsqueeze(2).to_broadcast([S, NH, HE]), ALU.mult).then_inc(att_done, 1)

            for b in range(B + 1):
                if b < B:
                    diagonal(b)
                if b >= 1:
                    divide(b - 1)
            dve.wait_ge(t_done, B)
            for c in range(DC):
                nc.vector.tensor_copy(attT[:, c, :], t_ps[:, c, 0:NTOK]).then_inc(attT_done, 1)
            dve.wait_ge(loaded, 64)
            for t in range(TT):
                dve.wait_ge(y_done, t + 1)
                nc.vector.tensor_tensor(x[:, t, :], x[:, t, :], q_ps[0:TP, t % 2, 0:D], ALU.add).then_inc(added, 1)
                dve.wait_ge(added, 2 * t + 1)
                nc.vector.tensor_tensor(x[:, t, :], x[:, t, :], bo[:], ALU.add).then_inc(added, 1)
            dve.wait_ge(added, 2 * TT)


def build(nc, a, out):
    with ExitStack() as ctx:
        p = Phase(nc, ctx, "all")
        x = p.sb("x", [TP, TT, D])
        xnT = p.sb("xnT", [128, DC, NTOK])
        ident = p.sb("ident", [128, 128])
        before = p.sb("before", [128, E, E])
        x_loaded, zeroed, consts, stored = p.sem("x_loaded"), p.sem("zeroed"), p.sem("consts"), p.sem("stored")

        with nc.Block() as block:
            @block.gpsimd
            def _(pool):
                identity(nc, pool, ident[:], 128, zeroed, consts)
                nc.gpsimd.memset(before[:], 1.0).then_inc(zeroed, 1)
                pool.wait_ge(zeroed, 2)
                nc.gpsimd.affine_select(out=before[:], in_=before[:], compare_op=ALU.is_gt, fill=0.0, base=0,
                                        pattern=[[1, E], [-1, E]], channel_multiplier=0).then_inc(consts, 1)
                pool.wait_ge(consts, 2)

            @block.sync
            def _(sp):
                sp.dma_start(x[:], a["x"].rearrange("(t p) d -> p t d", p=TP)).then_inc(x_loaded, 16)
                sp.wait_ge(x_loaded, 16)

        with ExitStack() as heads:
            h = Phase(nc, heads, "heads")
            qT = h.sb("qT", [128, NH, NTOK])
            rz = h.sb("rz", [TP, B * NJ])
            layernorm_transposed(nc, "ln0", x, xnT, ident)
            queries(nc, xnT, qT, a["wq0"], a["qnorm"], a["knorm"])
            softmax_attention(nc, qT, rz, a["ctx"], a["ctxT"], a["wk0"], a["wv0"], ident)
            w0 = Weights(nc, heads, "w0", (a["gate0"], a["up0"], a["down0"], a["router0"]), SHARED0, E)
            attention_output(nc, x, qT, rz, a["wo0"], ident, w0.load)
            xn = [h.sb(f"xn{i}", [128, DC, NTOK], F32R) for i in range(2)]
            layernorm_transposed(nc, "ln1", x, xnT, ident, xn)
            mixture(nc, "moe0", x, xnT, xn, w0, before, False)

        with ExitStack() as linear:
            w1 = Weights(nc, linear, "w1", (a["gate1"], a["up1"], a["down1"], a["router1"]), SHARED1, E + 1)
            h = Phase(nc, linear, "linear")
            kv = h.sb("kv", [VW, B, FEAT])
            key_value_sums(nc, kv, a["ctxT"], a["mask"], a["wk1"], a["bk1"], a["wv1"], a["bv1"], a["wkf"], w1.load)
            layernorm_transposed(nc, "ln2", x, xnT, ident)
            linear_readout(nc, x, xnT, kv, a["wq1"], a["bq1"], a["wqf"], a["wo1"], a["bo1"], ident)
            xn = [h.sb(f"xn{i}", [128, DC, NTOK], F32R) for i in range(2)]
            layernorm_transposed(nc, "ln3", x, xnT, ident, xn)
            mixture(nc, "moe1", x, xnT, xn, w1, before, True, shared_gate=True)

        with nc.Block() as block:
            @block.sync
            def _(sp):
                sp.dma_start(out.rearrange("(t p) d -> p t d", p=TP), x[:]).then_inc(stored, 16)
                sp.wait_ge(stored, 16)


def kernel(**inputs):
    import numpy as np
    from concourse import bacc
    from concourse.bass_utils import run_bass_kernel_spmd

    g = {k: np.asarray(v) for k, v in inputs.items()}
    moe1 = g["L1_ffn_gate_up_proj"].transpose(0, 2, 1)
    hidden = moe1.shape[2] // 2

    def columns(w, shared):
        return np.concatenate([w.transpose(1, 0, 2).reshape(D, -1), shared], axis=1)

    arrays = {
        "x": g["x"].reshape(NTOK, D),
        "ctx": g["ctx_2048"],
        "ctxT": g["ctx_2048"].transpose(0, 2, 1),
        "mask": g["mask_BxS2_ff1"].reshape(B, KT, KP).transpose(2, 0, 1).reshape(KP, B * KT),
        "wq0": g["L0_xattn_Wq"], "wk0": g["L0_xattn_Wk"], "wv0": g["L0_xattn_Wv"], "wo0": g["L0_xattn_Wo"],
        "qnorm": g["L0_xattn_q_norm_w"].reshape(HD, 1), "knorm": g["L0_xattn_k_norm_w"].reshape(HD, 1),
        "router0": g["L0_ffn_gate_w"],
        "gate0": columns(g["L0_ffn_w_gate"], g["L0_ffn_sw_gate"]),
        "up0": columns(g["L0_ffn_w_up"], g["L0_ffn_sw_up"]),
        "down0": np.concatenate([g["L0_ffn_w_down"].reshape(-1, D), g["L0_ffn_sw_down"]]),
        "wq1": g["L1_xattn_Wq"].T, "wk1": g["L1_xattn_Wk"].T, "wv1": g["L1_xattn_Wv"].T, "wo1": g["L1_xattn_Wo"].T,
        "bq1": g["L1_xattn_bq"].reshape(DC, 128).T, "bk1": g["L1_xattn_bk"].reshape(DC, 128).T,
        "bv1": g["L1_xattn_bv"].reshape(1, D), "bo1": g["L1_xattn_bo"].reshape(1, D),
        "wqf": g["L1_xattn_Wqf"].T, "wkf": g["L1_xattn_Wkf"].T,
        "router1": np.concatenate([g["L1_ffn_router_weight"], g["L1_ffn_shared_gate_w"]]).T,
        "gate1": columns(moe1[:, :, :hidden], g["L1_ffn_sh_gate_w"].T),
        "up1": columns(moe1[:, :, hidden:], g["L1_ffn_sh_up_w"].T),
        "down1": np.concatenate([g["L1_ffn_down_proj"].transpose(0, 2, 1).reshape(-1, D), g["L1_ffn_sh_down_w"].T]),
    }
    nc = bacc.Bacc("TRN2", target_bir_lowering=False, num_devices=1)
    drams, feed = {}, {}
    for name, value in arrays.items():
        value = np.ascontiguousarray(value)
        feed[f"in_{name}"] = value
        drams[name] = nc.dram_tensor(f"in_{name}", value.shape, mybir.dt.from_np(value.dtype), kind="ExternalInput").ap()
    out = nc.dram_tensor("out", (NTOK, D), F32, kind="ExternalOutput").ap()
    build(nc, drams, out)
    got = run_bass_kernel_spmd(nc, [feed], core_ids=[0]).results[0]["out"]
    return got.reshape(B, S, D)
```

```python
from contextlib import ExitStack

import concourse.bass as bass
from concourse import mybir

F32 = mybir.dt.float32
F32R = mybir.dt.float32r
ALU = mybir.AluOpType
ACT = mybir.ActivationFunctionType
AX = mybir.AxisListType.X

B = 8
S = 56
D = 256
DC = D // 128
NTOK = B * S
TT = 4
TP = NTOK // TT
SK = 1500
KC = 3
CH = SK // KC
KT = 12
KP = SK // KT
TPC = KT // KC

NH = 16
HD = 128
G = 4
HG = NH // G
QG = HG * S
U = 2
QU = 2 * QG
NJ = NH * S // TP

HE = 16
FD = 64
FEAT = NH * FD
KG = 6
GH = 3
GF = GH * FD
GV = GH * HE
VW = 2 * GV + 2
SUMS = [(i * 2 * GF, min((i + 1) * 2 * GF, FEAT)) for i in range(KG // 2)]
RV = HE + 1

E = 8
EU = 176
SHARED0 = 352
SHARED1 = 704

LN_EXP = "natural_log_exp_and_others"

LN_EPS = 1e-5
RMS_EPS = 1e-6


def wait(eng, sem, value):
    if isinstance(value, int) and value <= 0:
        return
    eng.wait_ge(sem, value)


def identity(nc, pool, tile, n, memset_done, ident_done):
    nc.gpsimd.memset(tile, 0.0).then_inc(memset_done, 1)
    pool.wait_ge(memset_done, 1)
    nc.gpsimd.affine_select(out=tile, in_=tile, compare_op=ALU.not_equal, fill=1.0, base=0,
                            pattern=[[-1, n]], channel_multiplier=1).then_inc(ident_done, 1)


class Phase:

    def __init__(self, nc, ctx, name):
        self.nc, self.ctx, self.name, self.sems = nc, ctx, name, []
        ctx.callback(self.clear)

    def clear(self):
        if self.sems:
            self.nc.clear_and_free_semaphores(self.sems)
            self.nc.all_engine_barrier()

    def sb(self, name, shape, dt=F32):
        return self.ctx.enter_context(self.nc.sbuf_tensor(f"{self.name}_{name}", shape, dt))

    def ps(self, name, shape):
        return self.ctx.enter_context(self.nc.psum_tensor(f"{self.name}_{name}", shape, F32))

    def sem(self, name):
        self.sems.append(self.nc.alloc_semaphore(f"{self.name}_{name}"))
        return self.sems[-1]


def mm3(nc, out, w_hi, w_lo, x_hi, x_lo, start, stop):
    nc.tensor.matmul(out, w_lo, x_hi, start=start, stop=False, skip_group_check=True)
    nc.tensor.matmul(out, w_hi, x_lo, start=False, stop=False, skip_group_check=True)
    return nc.tensor.matmul(out, w_hi, x_hi, start=False, stop=stop, skip_group_check=True)


def layernorm_transposed(nc, name, x, xnT, ident, halves=None):
    with ExitStack() as ctx:
        p = Phase(nc, ctx, name)
        stats = p.sb("stats", [TP, TT, 6])
        mv = p.sb("mv", [TP, TT, 2])
        var = p.sb("var", [TP, TT])
        rstd = p.sb("rstd", [TP, TT])
        tmp = p.sb("tmp", [TP, TT])
        xn = p.sb("xn", [TP, TT, D])
        eps = p.sb("eps", [128, 1])
        turned = p.ps("turned", [128, 2, 512])
        stats_done, mv_done, var_done, guess_done = (p.sem(s) for s in (
            "stats_done", "mv_done", "var_done", "guess_done"))
        newton, xn_done, turned_done, copied = (p.sem(s) for s in ("newton", "xn_done", "turned_done", "copied"))
        hi_done = p.sem("hi_done")
        block = ctx.enter_context(nc.Block())

        @block.vector
        def _(dve):
            nc.vector.memset(eps[:], 0.0).then_inc(var_done, 1)
            for t in range(TT):
                nc.vector.bn_stats(stats[:, t, :], x[:, t, :]).then_inc(stats_done, 1)
            for t in range(TT):
                dve.wait_ge(stats_done, t + 1)
                nc.vector.bn_aggr(mv[:, t, :], stats[:, t, :]).then_inc(mv_done, 1)
            dve.wait_ge(mv_done, TT)
            nc.vector.tensor_scalar(var[:], mv[:, :, 1], LN_EPS, None, ALU.add).then_inc(var_done, 1)
            dve.wait_ge(guess_done, 2)
            nc.vector.tensor_tensor(tmp[:], rstd[:], rstd[:], ALU.mult).then_inc(newton, 1)
            dve.wait_ge(newton, 1)
            nc.vector.tensor_tensor(tmp[:], tmp[:], var[:], ALU.mult).then_inc(newton, 1)
            dve.wait_ge(newton, 2)
            nc.vector.tensor_scalar(tmp[:], tmp[:], -0.5, 1.5, ALU.mult, ALU.add).then_inc(newton, 1)
            dve.wait_ge(newton, 3)
            nc.vector.tensor_tensor(rstd[:], rstd[:], tmp[:], ALU.mult).then_inc(newton, 1)
            dve.wait_ge(newton, 4)
            for t in range(TT):
                nc.vector.tensor_scalar(xn[:, t, :], x[:, t, :], mv[:, t, 0:1], rstd[:, t:t + 1],
                                        ALU.subtract, ALU.mult).then_inc(xn_done, 1)
            for c in range(DC):
                dve.wait_ge(turned_done, c + 1)
                nc.vector.tensor_copy(xnT[:, c, :], turned[:, c, 0:NTOK]).then_inc(copied, 1)
            if halves:
                for c in range(DC):
                    dve.wait_ge(hi_done, c + 1)
                    nc.vector.tensor_tensor(halves[1][:, c, :], xnT[:, c, :], halves[0][:, c, :].bitcast(F32),
                                            ALU.subtract).then_inc(copied, 1)
            dve.wait_ge(copied, 2 * DC if halves else DC)

        @block.scalar
        def _(act):
            nc.scalar.preload_act_table_set(LN_EXP)
            act.wait_ge(var_done, 2)
            nc.scalar.activation(rstd[:], var[:], ACT.Ln, bias=eps[0:TP, 0:1]).then_inc(guess_done, 1)
            act.wait_ge(guess_done, 1)
            nc.scalar.activation(rstd[:], rstd[:], ACT.Exp, scale=-0.5, bias=eps[0:TP, 0:1]).then_inc(guess_done, 1)
            if halves:
                for c in range(DC):
                    act.wait_ge(copied, c + 1)
                    nc.scalar.activation(halves[0][:, c, :], xnT[:, c, :], ACT.Copy).then_inc(hi_done, 1)

        @block.tensor
        def _(pe):
            for c in range(DC):
                for t in range(TT):
                    if c == 0:
                        pe.wait_ge(xn_done, t + 1)
                    last = nc.tensor.transpose(turned[:, c, t * TP:(t + 1) * TP],
                                               xn[:, t, c * 128:(c + 1) * 128], ident[0:TP, 0:TP])
                last.then_inc(turned_done, 1)


def queries(nc, xn, qT, wq_dram, qw_dram, kw_dram, splits):
    with ExitStack() as ctx:
        p = Phase(nc, ctx, "qry")
        raw = p.sb("raw", [128, DC, NH * HD])
        wq = [p.sb(f"wq{i}", [128, DC, NH * HD], F32R) for i in range(2)]
        nw = p.sb("nw", [128, 4])
        eps = p.sb("eps", [128, 2])
        mean_mat = p.sb("mean_mat", [128, 128], F32R)
        work = p.sb("work", [128, 4, NTOK])
        sq = [p.sb(f"sq{i}", [128, 3, NTOK], F32R) for i in range(2)]
        proj = p.ps("proj", [128, 4, 512])
        mean = p.ps("mean", [128, 2, 512])
        loaded = [p.sem(f"loaded{i}") for i in range(4)]
        next_loaded = [p.sem(f"next_loaded{i}") for i in range(len(splits))]
        w_hi, w_lo, next_hi, next_lo = (p.sem(s) for s in ("w_hi", "w_lo", "next_hi", "next_lo"))
        nw_loaded, eps_set, nw_done, proj_done, sq_done, sq_hi, sq_lo, mean_done = (p.sem(s) for s in (
            "nw_loaded", "eps_set", "nw_done", "proj_done", "sq_done", "sq_hi", "sq_lo", "mean_done"))
        ln_done, rs_done, q_done = (p.sem(s) for s in ("ln_done", "rs_done", "q_done"))
        block = ctx.enter_context(nc.Block())
        QUARTER = NH // 4
        NEXT_AT = {3 + 2 * i: i for i in range(len(splits))}

        def head(h):
            return slice(h * HD, (h + 1) * HD)

        @block.sync
        def _(sp):
            src = wq_dram.rearrange("(c p) n -> p c n", p=128)
            for i in range(4):
                y = slice(i * QUARTER * HD, (i + 1) * QUARTER * HD)
                sp.dma_start(raw[:, :, y], src[:, :, y]).then_inc(loaded[i], 16)
                if i == 0:
                    sp.dma_start(nw[:, 0:1], qw_dram).then_inc(nw_loaded, 16)
                    sp.dma_start(nw[:, 1:2], kw_dram).then_inc(nw_loaded, 16)
            for i, (dram, tile, _, _) in enumerate(splits):
                sp.dma_start(tile, dram).then_inc(next_loaded[i], 16)

        @block.tensor
        def _(pe):
            pe.wait_ge(eps_set, 3)

            def mean_square(h):
                pe.wait_ge(sq_lo, h + 1)
                wait(pe, ln_done, h - 1)
                for half in (1, 0):
                    last = nc.tensor.matmul(mean[:, h % 2, 0:NTOK], mean_mat[:], sq[half][:, h % 3, :],
                                            start=(half == 1), stop=(half == 0))
                last.then_inc(mean_done, 1)

            for h in range(NH):
                pe.wait_ge(w_lo, h + 1)
                wait(pe, q_done, h - 3)
                for c in range(DC):
                    last = mm3(nc, proj[:, h % 4, 0:NTOK], wq[0][:, c, head(h)], wq[1][:, c, head(h)],
                               xn[0][:, c, :], xn[1][:, c, :], c == 0, c == DC - 1)
                last.then_inc(proj_done, 1)
                if h >= 2:
                    mean_square(h - 2)
            mean_square(NH - 2)
            mean_square(NH - 1)

        @block.scalar
        def _(act):
            nc.scalar.preload_act_table_set(LN_EXP)
            act.wait_ge(eps_set, 3)

            def rstd(h):
                act.wait_ge(mean_done, h + 1)
                nc.scalar.activation(work[:, h % 4, :], mean[:, h % 2, 0:NTOK], ACT.Ln,
                                     bias=eps[:, 0:1]).then_inc(ln_done, 1)
                act.wait_ge(ln_done, h + 1)
                nc.scalar.activation(work[:, h % 4, :], work[:, h % 4, :], ACT.Exp, scale=-0.5,
                                     bias=eps[:, 1:2]).then_inc(rs_done, 1)

            for h in range(NH):
                act.wait_ge(proj_done, h + 1)
                wait(act, q_done, h - 3)
                nc.scalar.activation(work[:, h % 4, :], proj[:, h % 4, 0:NTOK], ACT.Square,
                                     bias=eps[:, 1:2]).then_inc(sq_done, 1)
                if h >= 2:
                    rstd(h - 2)
                if h in NEXT_AT:
                    i = NEXT_AT[h]
                    act.wait_ge(next_loaded[i], 16)
                    nc.scalar.activation(splits[i][2], splits[i][1], ACT.Copy).then_inc(next_hi, 1)
            rstd(NH - 2)
            rstd(NH - 1)

        @block.vector
        def _(dve):
            nc.vector.memset(eps[:, 0:1], RMS_EPS).then_inc(eps_set, 1)
            nc.vector.memset(eps[:, 1:2], 0.0).then_inc(eps_set, 1)
            nc.vector.memset(mean_mat[:].bitcast(F32), 1.0 / HD).then_inc(eps_set, 1)

            def split_w(h):
                if h % QUARTER == 0:
                    dve.wait_ge(loaded[h // QUARTER], 16)
                nc.vector.tensor_copy(wq[0][:, :, head(h)], raw[:, :, head(h)]).then_inc(w_hi, 1)
                dve.wait_ge(w_hi, h + 1)
                nc.vector.tensor_tensor(wq[1][:, :, head(h)], raw[:, :, head(h)],
                                        wq[0][:, :, head(h)].bitcast(F32), ALU.subtract).then_inc(w_lo, 1)

            def normalise(h):
                dve.wait_ge(rs_done, h + 1)
                nc.vector.scalar_tensor_tensor(qT[:, h, :], proj[:, h % 4, 0:NTOK], nw[:, 2:3],
                                               work[:, h % 4, :], ALU.mult, ALU.mult).then_inc(q_done, 1)

            split_w(0)
            split_w(1)
            dve.wait_ge(nw_loaded, 32)
            nc.vector.scalar_tensor_tensor(nw[:, 2:3], nw[:, 0:1], HD ** -0.5, nw[:, 1:2],
                                           ALU.mult, ALU.mult).then_inc(nw_done, 1)
            dve.wait_ge(nw_done, 1)
            for h in range(NH):
                if h + 2 < NH:
                    split_w(h + 2)
                dve.wait_ge(sq_done, h + 1)
                wait(dve, mean_done, h - 2)
                nc.vector.tensor_copy(sq[0][:, h % 3, :], work[:, h % 4, :]).then_inc(sq_hi, 1)
                if h >= 2:
                    normalise(h - 2)
            normalise(NH - 2)
            normalise(NH - 1)
            dve.wait_ge(q_done, NH)

        @block.gpsimd
        def _(pool):
            for h in range(NH):
                pool.wait_ge(sq_hi, h + 1)
                nc.gpsimd.tensor_tensor(sq[1][:, h % 3, :], work[:, h % 4, :], sq[0][:, h % 3, :].bitcast(F32),
                                        ALU.subtract).then_inc(sq_lo, 1)
                if h in NEXT_AT:
                    i = NEXT_AT[h]
                    pool.wait_ge(next_hi, i + 1)
                    nc.gpsimd.tensor_tensor(splits[i][3], splits[i][1], splits[i][2].bitcast(F32),
                                            ALU.subtract).then_inc(next_lo, 1)
            pool.wait_ge(next_lo, len(splits))


def softmax_attention(nc, qT, rz, ctx_dram, ctxT_dram, wk, wv, raw_t, ct, ident):
    with ExitStack() as ctx:
        p = Phase(nc, ctx, "att")
        raw_n = p.sb("raw_n", [KP, 2, KT // 2, D])
        cn = [p.sb(f"cn{i}", [KP, KT, D], F32R) for i in range(2)]
        q = [p.sb(f"q{i}", [128, NH, S], F32R) for i in range(2)]
        work = p.sb("work", [128, 2, CH])
        sq = [p.sb(f"sq{i}", [128, 2, CH], F32R) for i in range(2)]
        mean_mat = p.sb("mean_mat", [128, 128], F32R)
        k = [p.sb(f"k{i}", [128, 2, SK], F32R) for i in range(2)]
        pr = p.sb("pr", [TP, 4, SK])
        mn = p.sb("mn", [TP, 4, KC])
        nmx = p.sb("nmx", [TP, 4])
        z = p.sb("z", [TP, NJ, KC])
        zsum = p.sb("zsum", [TP, NJ])
        pT = [p.sb(f"pT{i}", [KP, 3, QU], F32R) for i in range(2)]
        cs = [p.sb(f"cs{i}", [128, DC, QU], F32R) for i in range(2)]
        eps = p.sb("eps", [128, 2])
        proj = p.ps("proj", [128, 2, 512])
        mean = p.ps("mean", [128, 512])
        ring = p.ps("ring", [128, 3, 512])
        csum = p.ps("csum", [128, 2, 512])

        eps_set = p.sem("eps_set")
        t_loaded = p.sem("t_loaded")
        n_loaded = [p.sem(f"n_loaded{i}") for i in range(2)]
        t_hi, t_lo, n_hi, n_lo, q_hi, q_lo = (p.sem(s) for s in ("t_hi", "t_lo", "n_hi", "n_lo", "q_hi", "q_lo"))
        proj_done, sq_done, sq_hi, sq_lo, mean_done, ln_done, rs_done = (p.sem(s) for s in (
            "proj_done", "sq_done", "sq_hi", "sq_lo", "mean_done", "ln_done", "rs_done"))
        k_full, k_hi, k_lo = (p.sem(s) for s in ("k_full", "k_hi", "k_lo"))
        ring_full, ring_free = p.sem("ring_full"), p.sem("ring_free")
        nmx_done, exp_done, rz_done = (p.sem(s) for s in ("nmx_done", "exp_done", "rz_done"))
        pT_hi, pv_done, cs_hi, cs_lo = (p.sem(s) for s in ("pT_hi", "pv_done", "cs_hi", "cs_lo"))
        out_full, out_free, zsum_done = p.sem("out_full"), p.sem("out_free"), p.sem("zsum_done")
        block = ctx.enter_context(nc.Block())

        NE = 3 + KC
        NS = 2 * KC
        NSC = 4 * KC
        NR = NSC + KT
        PIECES = DC * KC
        SEQ = [(0, 0), (0, 1), (1, 0), (1, 1), (0, 2), (0, 3), (1, 2), (1, 3), (0, 4), (0, 5), (1, 4), (1, 5)]
        SPLIT_AT = {2: 0, 4: 1, 5: 2, 8: 3, 9: 4, 11: 5}

        @block.sync
        def _(sp):
            def load_t(b):
                wait(sp, t_lo, (b - 1) * PIECES)
                src = ctxT_dram[bass.ds(b, 1), :, :] if not isinstance(b, int) else ctxT_dram[b:b + 1, :, :]
                sp.dma_start(raw_t[:], src.rearrange("a (c p) n -> p (a c) n", p=128)).then_inc(t_loaded, 16)

            def load_n(b):
                for half in range(2):
                    wait(sp, n_lo, (b - 1) * KT + (half + 1) * (KT // 2))
                    rows = slice(half * (SK // 2), (half + 1) * (SK // 2))
                    src = ctx_dram[bass.ds(b, 1), rows, :] if not isinstance(b, int) else ctx_dram[b:b + 1, rows, :]
                    sp.dma_start(raw_n[:, half], src.rearrange("a (j p) c -> p (a j) c", p=KP))\
                        .then_inc(n_loaded[half], 16)

            load_n(0)
            load_t(1)
            load_n(1)
            with sp.Fori(2, B) as b:
                load_t(b)
                load_n(b)

        @block.tensor
        def _(pe):
            def key_step(b, u, part, i):
                n = (2 * b + u) * NS + i
                c, g = i // 2, 2 * u + i % 2
                if part == 0:
                    if u == 0 and i % 2 == 0:
                        wait(pe, t_lo, (b - 1) * PIECES + DC * (c + 1))
                    wait(pe, k_full, n - 1)
                    for d in range(DC):
                        last = mm3(nc, proj[:, i % 2, 0:CH], wk[0][:, d, g * HD:(g + 1) * HD],
                                   wk[1][:, d, g * HD:(g + 1) * HD], ct[0][:, d, c * CH:(c + 1) * CH],
                                   ct[1][:, d, c * CH:(c + 1) * CH], d == 0, d == DC - 1)
                    last.then_inc(proj_done, 1)
                else:
                    wait(pe, sq_lo, n + 1)
                    wait(pe, ln_done, n)
                    if i == 0:
                        wait(pe, out_free, 2 * b + u - 1)
                    for half in (1, 0):
                        last = nc.tensor.matmul(mean[:, 0:CH], mean_mat[:], sq[half][:, i % 2, :],
                                                start=(half == 1), stop=(half == 0))
                    last.then_inc(mean_done, 1)

            def output(b, u, ahead=NS):
                wait(pe, cs_lo, (2 * b + u + 1) * DC)
                wait(pe, ln_done, (2 * b + u + 1) * NS + ahead)
                wait(pe, out_free, 2 * b + u)
                for gi in range(2):
                    w = slice((2 * u + gi) * HD, (2 * u + gi + 1) * HD)
                    x = slice(gi * QG, (gi + 1) * QG)
                    for i in range(DC):
                        last = mm3(nc, mean[:, x], wv[0][:, i, w], wv[1][:, i, w],
                                   cs[0][:, i, x], cs[1][:, i, x], i == 0, i == DC - 1)
                last.then_inc(out_full, 1)

            def scores(b, u):
                for j in range(4):
                    gi = j // 2
                    for c in range(KC):
                        r = (2 * b + u) * NR + j * KC + c
                        if j % 2 == 0:
                            wait(pe, k_lo, (2 * b + u) * NS + 2 * c + gi + 1)
                        if u == 0 and j == 0 and c == 0:
                            wait(pe, q_lo, 2 * (b + 1))
                        wait(pe, ring_free, r - 2)
                        h = 8 * u + 2 * j
                        mm3(nc, ring[0:TP, c, 0:CH], q[0][:, h:h + 2, :], q[1][:, h:h + 2, :],
                            k[0][:, gi, c * CH:(c + 1) * CH], k[1][:, gi, c * CH:(c + 1) * CH],
                            True, True).then_inc(ring_full, 1)

            def unit(b, u, keys, before):
                def turn(t):
                    if t % TPC == 0:
                        wait(pe, exp_done, (2 * b + u) * NE + 3 + t // TPC + 1)
                    wait(pe, ring_free, (2 * b + u) * NR + NSC + t - 2)
                    for j in range(4):
                        last = nc.tensor.transpose(ring[0:KP, t % 3, j * TP:(j + 1) * TP],
                                                   pr[:, j, t * KP:(t + 1) * KP], ident[0:TP, 0:TP])
                    last.then_inc(ring_full, 1)

                if keys:
                    key_step(*keys, *SEQ[0])
                    key_step(*keys, *SEQ[1])
                turn(0)
                turn(1)
                if before:
                    output(*before)
                for t in range(KT):
                    if t + 2 < KT:
                        turn(t + 2)
                    wait(pe, ring_free, (2 * b + u) * NR + NSC + t + 1)
                    if u == 0:
                        wait(pe, n_lo, b * KT + t + 1)
                    if t == 0:
                        wait(pe, cs_lo, (2 * b + u) * DC)
                    for i in range(DC):
                        last = mm3(nc, csum[:, i, 0:QU], cn[0][:, t, i * 128:(i + 1) * 128],
                                   cn[1][:, t, i * 128:(i + 1) * 128], pT[0][:, t % 3, :], pT[1][:, t % 3, :],
                                   t == 0, t == KT - 1)
                    last.then_inc(pv_done, 1)
                    if keys and t + 2 < len(SEQ):
                        key_step(*keys, *SEQ[t + 2])

            def batch(b, first, last):
                scores(b, 0)
                unit(b, 0, (b, 1), None if first else (b - 1, 1))
                scores(b, 1)
                unit(b, 1, None if last else (b + 1, 0), (b, 0))

            pe.wait_ge(eps_set, 4)
            for part, i in SEQ:
                key_step(0, 0, part, i)
            batch(0, True, False)
            with pe.Fori(1, B - 1) as b:
                batch(b, False, False)
            batch(B - 1, False, True)
            output(B - 1, 1, 0)

        @block.scalar
        def _(act):
            def split_t(b, n):
                c, d = n // DC, n % DC
                wait(act, t_loaded, 16 * b)
                wait(act, proj_done, (2 * b - 1) * NS + 2 * (c + 1))
                nc.scalar.activation(ct[0][:, d, c * CH:(c + 1) * CH], raw_t[:, d, c * CH:(c + 1) * CH],
                                     ACT.Copy).then_inc(t_hi, 1)

            def key_step(b, u, part, i):
                n = (2 * b + u) * NS + i
                if part == 0:
                    wait(act, proj_done, n + 1)
                    wait(act, k_lo, n - 1)
                    nc.scalar.activation(work[:, i % 2, :], proj[:, i % 2, 0:CH], ACT.Square,
                                         bias=eps[:, 1:2]).then_inc(sq_done, 1)
                else:
                    wait(act, mean_done, n + 1)
                    nc.scalar.activation(work[:, i % 2, :], mean[:, 0:CH], ACT.Ln, bias=eps[:, 0:1]).then_inc(ln_done, 1)
                    wait(act, ln_done, n + 1)
                    nc.scalar.activation(work[:, i % 2, :], work[:, i % 2, :], ACT.Exp, scale=-0.5,
                                         bias=eps[:, 1:2]).then_inc(rs_done, 1)

            def exponential(u, j, c, keys):
                nc.scalar.activation(pr[:, j, keys], pr[:, j, keys], ACT.Exp, scale=-1.0, bias=nmx[:, j:j + 1],
                                     accum_out=z[:, 4 * u + j, c:c + 1]).then_inc(exp_done, 1)

            def exponentials(b, u):
                for j in range(4):
                    wait(act, nmx_done, b * NJ + 4 * u + j + 1)
                    if u == 0 and j == 0:
                        wait(act, rz_done, b)
                    exponential(u, j, 0, slice(0, CH if j == 3 else SK))

            def unit(b, u, keys, pieces):
                if keys:
                    key_step(*keys, *SEQ[0])
                for t in range(KT):
                    wait(act, ring_full, (2 * b + u) * NR + NSC + t + 1)
                    wait(act, pv_done, (2 * b + u) * KT + t - 2)
                    nc.scalar.activation(pT[0][:, t % 3, :], ring[0:KP, t % 3, 0:QU], ACT.Copy).then_inc(pT_hi, 1)
                    if t + 1 < KC:
                        exponential(u, 3, t + 1, slice((t + 1) * CH, (t + 2) * CH))
                    if keys and t >= 1:
                        key_step(*keys, *SEQ[t])
                    if pieces is not None and t in SPLIT_AT:
                        split_t(pieces, SPLIT_AT[t])
                wait(act, pv_done, (2 * b + u + 1) * KT)
                wait(act, out_full, 2 * b + u)
                for i in range(DC):
                    nc.scalar.activation(cs[0][:, i, :], csum[:, i, 0:QU], ACT.Copy).then_inc(cs_hi, 1)

            def batch(b, last):
                exponentials(b, 0)
                unit(b, 0, (b, 1), None if last else b + 1)
                exponentials(b, 1)
                unit(b, 1, None if last else (b + 1, 0), None)

            nc.scalar.preload_act_table_set(LN_EXP)
            act.wait_ge(eps_set, 4)
            for part, i in SEQ:
                key_step(0, 0, part, i)
            batch(0, False)
            with act.Fori(1, B - 1) as b:
                batch(b, False)
            batch(B - 1, True)

        @block.vector
        def _(dve):
            def split_t(b, n):
                wait(dve, t_hi, (b - 1) * PIECES + n + 1)
                x = (slice(None), n % DC, slice(n // DC * CH, (n // DC + 1) * CH))
                nc.vector.tensor_tensor(ct[1][x], raw_t[x], ct[0][x].bitcast(F32), ALU.subtract).then_inc(t_lo, 1)

            def split_n(b, t):
                half, j = divmod(t, KT // 2)
                wait(dve, n_loaded[half], 16 * (b + 1))
                wait(dve, pv_done, (2 * b - 1) * KT + t + 1)
                nc.vector.tensor_copy(cn[0][:, t, :], raw_n[:, half, j, :]).then_inc(n_hi, 1)

            def split_q(b, half):
                wait(dve, ring_full, (2 * b - 1) * NR + NSC)
                for y in (slice(0, NH // 2), slice(NH // 2, NH)):
                    src = qT[:, y, bass.ds(b * S, S)] if not isinstance(b, int) else qT[:, y, b * S:(b + 1) * S]
                    if half == 0:
                        nc.vector.tensor_scalar(q[0][:, y], src, 1.0, None, ALU.mult).then_inc(q_hi, 1)
                    else:
                        wait(dve, q_hi, 2 * (b + 1))
                        nc.vector.tensor_tensor(q[1][:, y], src, q[0][:, y].bitcast(F32), ALU.subtract).then_inc(q_lo, 1)

            def key_step(b, u, part, i):
                n = (2 * b + u) * NS + i
                c, gi = i // 2, i % 2
                if part == 0:
                    wait(dve, sq_done, n + 1)
                    wait(dve, mean_done, n - 1)
                    nc.vector.tensor_copy(sq[0][:, i % 2, :], work[:, i % 2, :]).then_inc(sq_hi, 1)
                else:
                    wait(dve, rs_done, n + 1)
                    nc.vector.tensor_tensor(work[:, i % 2, :], proj[:, i % 2, 0:CH], work[:, i % 2, :],
                                            ALU.mult).then_inc(k_full, 1)
                    wait(dve, k_full, n + 1)
                    if i == 0:
                        wait(dve, ring_full, (2 * b + u - 1) * NR + NSC)
                    nc.vector.tensor_copy(k[0][:, gi, c * CH:(c + 1) * CH], work[:, i % 2, :]).then_inc(k_hi, 1)

            def split_sums(b, u):
                for i in range(DC):
                    wait(dve, cs_hi, (2 * b + u) * DC + i + 1)
                    nc.vector.tensor_tensor(cs[1][:, i, :], csum[:, i, 0:QU], cs[0][:, i, :].bitcast(F32),
                                            ALU.subtract).then_inc(cs_lo, 1)

            def output(b, u):
                wait(dve, out_full, 2 * b + u + 1)
                x = bass.ds(b * S, S) if not isinstance(b, int) else slice(b * S, (b + 1) * S)
                nc.vector.tensor_scalar(qT[:, 8 * u:8 * u + 8, x],
                                        mean[:, 0:QU].rearrange("p (h t) -> p h t", t=S), 1.0, None,
                                        ALU.mult).then_inc(out_free, 1)

            def scores(b, u, before):
                for j in range(4):
                    for c in range(KC):
                        wait(dve, ring_full, (2 * b + u) * NR + j * KC + c + 1)
                        if j == 0 and c == 0:
                            wait(dve, ring_full, (2 * b + u) * NR)
                        if c == 0:
                            wait(dve, exp_done, (2 * b + u - 1) * NE + (j + 1 if j < 3 else NE))
                        nc.vector.tensor_scalar(pr[:, j, c * CH:(c + 1) * CH], ring[0:TP, c, 0:CH], -1.0, 3.0e38,
                                                ALU.mult, ALU.min, accum_out=mn[:, j, c:c + 1]).then_inc(ring_free, 1)
                    wait(dve, ring_free, (2 * b + u) * NR + (j + 1) * KC)
                    nc.vector.tensor_reduce(nmx[:, j:j + 1], mn[:, j, :], AX, ALU.min).then_inc(nmx_done, 1)
                if before:
                    split_sums(*before)

            def unit(b, u, keys, pieces, before):
                if keys:
                    key_step(*keys, *SEQ[0])
                for t in range(KT):
                    wait(dve, pT_hi, (2 * b + u) * KT + t + 1)
                    nc.vector.tensor_tensor(pT[1][:, t % 3, :], ring[0:KP, t % 3, 0:QU],
                                            pT[0][:, t % 3, :].bitcast(F32), ALU.subtract).then_inc(ring_free, 1)
                    if t == 0 and before:
                        output(*before)
                    if keys and t >= 1:
                        key_step(*keys, *SEQ[t])
                    if pieces is not None and t in SPLIT_AT:
                        split_t(pieces, SPLIT_AT[t])
                    if u == 1 and keys and t in (2, 6):
                        split_q(keys[0], (2, 6).index(t))
                    if u == 1 and keys and t >= 3:
                        split_n(keys[0], t - 3)
                    if u == 1 and t == 2:
                        wait(dve, exp_done, (2 * b + 2) * NE)
                        nc.vector.tensor_reduce(zsum[:], z[:], AX, ALU.add).then_inc(zsum_done, 1)
                        wait(dve, zsum_done, b + 1)
                        x = bass.ds(b * NJ, NJ) if not isinstance(b, int) else slice(b * NJ, (b + 1) * NJ)
                        nc.vector.reciprocal(rz[:, x], zsum[:]).then_inc(rz_done, 1)
                if u == 1 and keys:
                    for t in range(KT - 3, KT):
                        split_n(keys[0], t)

            def batch(b, first, last):
                before = None if first else (b - 1, 1)
                scores(b, 0, before)
                unit(b, 0, (b, 1), None if last else b + 1, before)
                scores(b, 1, (b, 0))
                unit(b, 1, None if last else (b + 1, 0), None, (b, 0))

            nc.vector.memset(eps[:, 0:1], RMS_EPS).then_inc(eps_set, 1)
            nc.vector.memset(eps[:, 1:2], 0.0).then_inc(eps_set, 1)
            nc.vector.memset(mean_mat[:].bitcast(F32), 1.0 / HD).then_inc(eps_set, 1)
            nc.vector.memset(z[:], 0.0).then_inc(eps_set, 1)
            for step, (part, i) in enumerate(SEQ):
                key_step(0, 0, part, i)
                split_n(0, step)
                if step in (3, 6):
                    split_q(0, (3, 6).index(step))
            batch(0, True, False)
            with dve.Fori(1, B - 1) as b:
                batch(b, False, False)
            batch(B - 1, False, True)
            split_sums(B - 1, 1)
            output(B - 1, 1)
            dve.wait_ge(out_free, 2 * B)
            dve.wait_ge(rz_done, B)

        @block.gpsimd
        def _(pool):
            def key_step(b, u, part, i):
                n = (2 * b + u) * NS + i
                c, gi = i // 2, i % 2
                if part == 0:
                    wait(pool, sq_hi, n + 1)
                    nc.gpsimd.tensor_tensor(sq[1][:, i % 2, :], work[:, i % 2, :], sq[0][:, i % 2, :].bitcast(F32),
                                            ALU.subtract).then_inc(sq_lo, 1)
                else:
                    wait(pool, k_hi, n + 1)
                    x = (slice(None), gi, slice(c * CH, (c + 1) * CH))
                    nc.gpsimd.tensor_tensor(k[1][x], work[:, i % 2, :], k[0][x].bitcast(F32),
                                            ALU.subtract).then_inc(k_lo, 1)

            N_AFTER = {11: range(KT)}

            def split_n(b, t):
                half, j = divmod(t, KT // 2)
                wait(pool, n_hi, b * KT + t + 1)
                nc.gpsimd.tensor_tensor(cn[1][:, t, :], raw_n[:, half, j, :], cn[0][:, t, :].bitcast(F32),
                                        ALU.subtract).then_inc(n_lo, 1)

            def batch(b, last):
                for part, i in SEQ:
                    key_step(b, 1, part, i)
                if not last:
                    for s, (part, i) in enumerate(SEQ):
                        key_step(b + 1, 0, part, i)
                        for t in N_AFTER.get(s, ()):
                            split_n(b + 1, t)

            for part, i in SEQ:
                key_step(0, 0, part, i)
            for t in range(KT):
                split_n(0, t)
            batch(0, False)
            with pool.Fori(1, B - 1) as b:
                batch(b, False)
            batch(B - 1, True)


def attention_output(nc, x, oT, rz, wo_dram, ident, following):
    with ExitStack() as ctx:
        p = Phase(nc, ctx, "wo")
        raw = p.sb("raw", [128, NH, D])
        wo = [p.sb(f"wo{i}", [128, NH, D], F32R) for i in range(2)]
        ones_mat = p.sb("ones_mat", [TP, 128], F32R)
        rz_r = p.sb("rz_r", [TP, B * NJ], F32R)
        rz2 = [p.sb(f"rz{i}", [TP, B * NJ]) for i in range(2)]
        diag = [p.sb(f"diag{i}", [TP, 2, NJ, TP], F32R) for i in range(2)]
        o = [p.sb(f"o{i}", [128, 2, NH, TP], F32R) for i in range(2)]
        spread = p.ps("spread", [128, 2, 2, 512])
        out = p.ps("out", [128, 2, 512])
        ones_set, rz_hi, rz_lo, diag_hi, diag_lo, spread_done, scaled, o_hi, o_lo = (p.sem(s) for s in (
            "ones_set", "rz_hi", "rz_lo", "diag_hi", "diag_lo", "spread_done", "scaled", "o_hi", "o_lo"))
        w_hi, w_lo, out_done, added = (p.sem(s) for s in ("w_hi", "w_lo", "out_done", "added"))
        loaded = [p.sem(f"loaded{i}") for i in range(4)]
        block = ctx.enter_context(nc.Block())
        QUARTER = NH // 4

        def heads(i):
            return slice(i * QUARTER, (i + 1) * QUARTER)

        def tokens(b):
            return slice(b % 2 * S, (b % 2 + 1) * S)

        def diagonal(engine, b, half):
            return engine.tensor_tensor(diag[half][:, b % 2], ident[0:TP, None, 0:TP].to_broadcast([TP, NJ, TP]),
                                        rz2[half][:, b * NJ:(b + 1) * NJ].unsqueeze(2).to_broadcast([TP, NJ, TP]),
                                        ALU.mult)

        @block.sync
        def _(sp):
            for i in range(4):
                y = slice(i * QUARTER * HD, (i + 1) * QUARTER * HD)
                sp.dma_start(raw[:, heads(i), :], wo_dram[y, :].rearrange("(h p) n -> p h n", p=128))\
                    .then_inc(loaded[i], 16)
            following.load(sp)

        @block.vector
        def _(dve):
            nc.vector.memset(ones_mat[:].bitcast(F32), 1.0).then_inc(ones_set, 1)
            nc.vector.tensor_copy(rz_r[:], rz[:]).then_inc(rz_hi, 1)
            dve.wait_ge(rz_hi, 1)
            nc.vector.tensor_copy(rz2[0][:], rz_r[:].bitcast(F32)).then_inc(rz_hi, 1)
            nc.vector.tensor_tensor(rz2[1][:], rz[:], rz_r[:].bitcast(F32), ALU.subtract).then_inc(rz_lo, 1)
            dve.wait_ge(rz_hi, 2)

            def scale(b):
                for i in range(2):
                    dve.wait_ge(spread_done, b + 1)
                    y = oT[:, 8 * i:8 * i + 8, b * S:(b + 1) * S]
                    nc.vector.tensor_tensor(y, y, spread[:, b % 2, i, 0:QU].rearrange("p (h t) -> p h t", t=S),
                                            ALU.mult).then_inc(scaled, 1)

            def split(b):
                dve.wait_ge(o_hi, b + 1)
                nc.vector.tensor_tensor(o[1][:, b // 2 % 2, :, tokens(b)], oT[:, :, b * S:(b + 1) * S],
                                        o[0][:, b // 2 % 2, :, tokens(b)].bitcast(F32), ALU.subtract).then_inc(o_lo, 1)

            def add(t):
                dve.wait_ge(out_done, t + 1)
                nc.vector.tensor_tensor(x[:, t, :], x[:, t, :], out[0:TP, t % 2, 0:D], ALU.add).then_inc(added, 1)

            def set_diagonal(b):
                wait(dve, spread_done, b - 1)
                diagonal(nc.vector, b, 0).then_inc(diag_hi, 1)

            set_diagonal(0)
            set_diagonal(1)
            for b in range(B):
                scale(b)
                if b < 4:
                    dve.wait_ge(w_hi, b + 1)
                    nc.vector.tensor_tensor(wo[1][:, heads(b), :], raw[:, heads(b), :],
                                            wo[0][:, heads(b), :].bitcast(F32), ALU.subtract).then_inc(w_lo, 1)
                if b + 2 < B:
                    set_diagonal(b + 2)
                split(b)
                if b == 6:
                    add(0)
            for t in range(1, TT):
                add(t)
            dve.wait_ge(added, TT)

        @block.gpsimd
        def _(pool):
            pool.wait_ge(rz_lo, 1)
            for b in range(B):
                wait(pool, spread_done, b - 1)
                diagonal(nc.gpsimd, b, 1).then_inc(diag_lo, 1)
            following.set_member(pool)

        @block.scalar
        def _(act):
            def split_w(i):
                act.wait_ge(loaded[i], 16)
                nc.scalar.activation(wo[0][:, heads(i), :], raw[:, heads(i), :], ACT.Copy).then_inc(w_hi, 1)

            for b in range(B):
                if b < 4:
                    split_w(b)
                act.wait_ge(scaled, 2 * (b + 1))
                if b >= 4:
                    act.wait_ge(out_done, b // 2 - 1)
                nc.scalar.activation(o[0][:, b // 2 % 2, :, tokens(b)], oT[:, :, b * S:(b + 1) * S], ACT.Copy)\
                    .then_inc(o_hi, 1)

        @block.tensor
        def _(pe):
            pe.wait_ge(ones_set, 1)

            def spread_out(b):
                pe.wait_ge(diag_hi, b + 1)
                pe.wait_ge(diag_lo, b + 1)
                wait(pe, scaled, 2 * (b - 1))
                for i in range(2):
                    for half in (1, 0):
                        last = nc.tensor.matmul(spread[:, b % 2, i, 0:QU], ones_mat[:],
                                                diag[half][:, b % 2, 4 * i:4 * i + 4, :],
                                                start=(half == 1), stop=(half == 0))
                last.then_inc(spread_done, 1)

            def project(t, i):
                if t == 0:
                    pe.wait_ge(w_lo, i + 1)
                if i == 0:
                    pe.wait_ge(o_lo, 2 * (t + 1))
                    wait(pe, added, t - 1)
                for h in range(NH)[heads(i)]:
                    last = mm3(nc, out[0:TP, t % 2, 0:D], o[0][:, t % 2, h, :], o[1][:, t % 2, h, :],
                               wo[0][:, h, :], wo[1][:, h, :], h == 0, h == NH - 1)
                if i == 3:
                    last.then_inc(out_done, 1)

            steps = iter([(t, i) for t in range(TT) for i in range(4)])

            for b in range(B):
                spread_out(b)
                if b >= 3:
                    for _ in range(2):
                        project(*next(steps))
            for step in steps:
                project(*step)


class Weights:

    def __init__(self, nc, ctx, name, drams, shared, logits):
        p = Phase(nc, ctx, name)
        self.nc, self.drams, self.logits = nc, drams, logits
        self.units = E * EU + shared
        self.blocks = -(-self.units // 128)
        self.gate = p.sb("gate", [128, DC, self.units])
        self.up = p.sb("up", [128, DC, self.units])
        self.down = p.sb("down", [128, self.blocks, D])
        self.router = p.sb("router", [128, DC, E + 1])
        self.member = p.sb("member", [E + 1, self.units])
        self.router_loaded, self.loaded, self.member_done = (p.sem(s) for s in (
            "router_loaded", "loaded", "member_done"))

    def size(self, n):
        return min(128, self.units - 128 * n)

    def load(self, sp):
        gate, up, down, router = self.drams
        sp.dma_start(self.router[:, :, 0:self.logits], router.rearrange("(c p) n -> p c n", p=128))\
            .then_inc(self.router_loaded, 16)
        sp.dma_start(self.gate[:], gate.rearrange("(c p) n -> p c n", p=128)).then_inc(self.loaded, 16)
        sp.dma_start(self.up[:], up.rearrange("(c p) n -> p c n", p=128)).then_inc(self.loaded, 16)
        whole = self.units // 128
        sp.dma_start(self.down[:, 0:whole, :], down[0:whole * 128, :].rearrange("(m p) n -> p m n", p=128))\
            .then_inc(self.loaded, 16)
        sp.dma_start(self.down[0:self.units - whole * 128, whole, :], down[whole * 128:, :]).then_inc(self.loaded, 16)

    def set_member(self, pool):
        member = self.member
        self.nc.gpsimd.memset(member[:], 1.0).then_inc(self.member_done, 1)
        pool.wait_ge(self.member_done, 1)
        self.nc.gpsimd.affine_select(out=member[:], in_=member[:], compare_op=ALU.is_ge, fill=0.0, base=0,
                                     pattern=[[1, self.units]], channel_multiplier=-EU).then_inc(self.member_done, 1)
        pool.wait_ge(self.member_done, 2)
        self.nc.gpsimd.affine_select(out=member[0:E], in_=member[0:E], compare_op=ALU.is_ge, fill=0.0, base=EU - 1,
                                     pattern=[[-1, self.units]], channel_multiplier=EU).then_inc(self.member_done, 1)


def mixture(nc, name, x, xnT, xn, weights, before, ident, normalise, shared_gate=False):
    with ExitStack() as ctx:
        p = Phase(nc, ctx, name)
        wide = [p.sb(f"wide{i}", [128, 3, 2, DC, 128], F32R) for i in range(2)]
        wd = [p.sb(f"wd{i}", [128, 6, D], F32R) for i in range(2)]
        silu = p.sb("silu", [128, 2, NTOK])
        full = p.sb("full", [128, 4, NTOK])
        hid = [p.sb(f"hid{i}", [128, 3, NTOK], F32R) for i in range(2)]
        member = p.sb("member", [E + 1, weights.units], F32R)
        combT = [p.sb(f"combT{i}", [E + 1, NTOK], F32R) for i in range(2)]
        logit = p.sb("logit", [TP, TT, E + 1])
        mx = p.sb("mx", [TP, TT])
        prob = p.sb("prob", [TP, TT, E])
        tot = p.sb("tot", [TP, TT])
        rank = p.sb("rank", [TP, TT, E, E])
        same = p.sb("same", [TP, TT, E, E])
        place = p.sb("place", [TP, TT, E])
        share = p.sb("share", [TP, TT])
        comb = p.sb("comb", [TP, TT, E + 1])
        zero = p.sb("zero", [128, 1])
        gate = p.ps("gate", [128, 2, 512])
        up = p.ps("up", [128, 2, 512])
        down = p.ps("down", [128, 2, 512])
        scale = p.ps("scale", [128, 2, 512])

        lg_done, r, gates_done, silu_done, hid_done, down_done, added, act_r = (p.sem(s) for s in (
            "lg_done", "route_step", "gates_done", "silu_done", "hid_done", "down_done", "added", "act_step"))
        member_r, comb_turned, comb_hi, comb_lo = (p.sem(s) for s in (
            "member_rounded", "comb_turned", "comb_hi", "comb_lo"))
        scale_done, scaled, hid_hi, hid_lo, w_hi, w_lo = (p.sem(s) for s in (
            "scale_done", "scaled", "hid_hi", "hid_lo", "w_hi", "w_lo"))
        block = ctx.enter_context(nc.Block())

        blocks, size = weights.blocks, weights.size
        nl = weights.logits
        route_steps = 7 + 3 * TT + 4 + (3 if normalise else 0) + (2 if shared_gate else 1)
        NW = 3
        LAG = 2

        @block.tensor
        def _(pe):
            pe.wait_ge(weights.router_loaded, 16)
            for t in range(TT):
                for c in range(DC):
                    last = nc.tensor.matmul(scale[0:TP, 0, t * 16:t * 16 + nl], xnT[:, c, t * TP:(t + 1) * TP],
                                            weights.router[:, c, 0:nl], start=(c == 0), stop=(c == DC - 1))
            last.then_inc(lg_done, 1)

            def widen(n):
                pe.wait_ge(w_lo, NW * n + 2)
                wait(pe, hid_done, n - 1)
                for i, out in enumerate((gate, up)):
                    for c in range(DC):
                        w = [half[:, n % 3, i, c, 0:size(n)] for half in wide]
                        last = mm3(nc, out[0:size(n), n % 2, 0:NTOK], *w, xn[0][:, c, :], xn[1][:, c, :],
                                   c == 0, c == DC - 1)
                last.then_inc(gates_done, 1)

            def turn_weights():
                pe.wait_ge(r, route_steps)
                for t in range(TT):
                    last = nc.tensor.transpose(scale[0:E + 1, 1, t * TP:(t + 1) * TP], comb[:, t, :], ident[0:TP, 0:TP])
                last.then_inc(comb_turned, 1)

            def spread(n):
                if n == 0:
                    pe.wait_ge(comb_lo, 1)
                    pe.wait_ge(member_r, 1)
                wait(pe, scaled, n - 1)
                for half in (1, 0):
                    last = nc.tensor.matmul(scale[0:size(n), n % 2, 0:NTOK], member[:, n * 128:n * 128 + size(n)],
                                            combT[half][:], start=(half == 1), stop=(half == 0))
                last.then_inc(scale_done, 1)

            def narrow(n):
                pe.wait_ge(w_lo, NW * (n + 1))
                pe.wait_ge(hid_lo, n + 1)
                for t in range(TT):
                    h = [part[0:size(n), n % 3, t * TP:(t + 1) * TP] for part in hid]
                    last = mm3(nc, down[0:TP, t // 2, (t % 2) * D:(t % 2 + 1) * D], *h,
                               wd[0][0:size(n), n % 6, :], wd[1][0:size(n), n % 6, :],
                               n == 0 and t % 2 == 0, n == blocks - 1 and t % 2 == 1)
                last.then_inc(down_done, 1)

            for n in range(blocks + LAG + 1):
                if n < blocks:
                    widen(n)
                if n == 1:
                    turn_weights()
                if LAG <= n < blocks + LAG:
                    spread(n - LAG)
                if n > LAG:
                    narrow(n - LAG - 1)

        @block.scalar
        def _(act):
            def split(n):
                if n == 0:
                    act.wait_ge(weights.loaded, 64)
                wait(act, gates_done, n - 2)
                wait(act, down_done, n - 5)
                y = slice(n * 128, n * 128 + size(n))
                nc.scalar.activation(wide[0][:, n % 3, 0, :, 0:size(n)], weights.gate[:, :, y], ACT.Copy).then_inc(w_hi, 1)
                nc.scalar.activation(wide[0][:, n % 3, 1, :, 0:size(n)], weights.up[:, :, y], ACT.Copy).then_inc(w_hi, 1)
                nc.scalar.activation(wd[0][0:size(n), n % 6], weights.down[0:size(n), n, :], ACT.Copy).then_inc(w_hi, 1)

            split(0)
            act.wait_ge(r, 4)
            nc.scalar.activation(prob[:], prob[:], ACT.Exp, bias=zero[0:TP, 0:1]).then_inc(act_r, 1)
            if shared_gate:
                nc.scalar.activation(share[:], logit[:, :, E], ACT.Exp, scale=-1.0, bias=zero[0:TP, 0:1]).then_inc(act_r, 1)
            split(1)
            act.wait_ge(weights.member_done, 3)
            nc.scalar.activation(member[:], weights.member[:], ACT.Copy).then_inc(member_r, 1)
            for n in range(blocks + LAG):
                if n < blocks:
                    act.wait_ge(gates_done, n + 1)
                    wait(act, hid_done, n - 1)
                    nc.scalar.activation(silu[0:size(n), n % 2, :], gate[0:size(n), n % 2, 0:NTOK], ACT.Silu,
                                         bias=zero[0:size(n), 0:1]).then_inc(silu_done, 1)
                if n == 1:
                    act.wait_ge(comb_turned, 1)
                    nc.scalar.activation(combT[0][:], scale[0:E + 1, 1, 0:NTOK], ACT.Copy).then_inc(comb_hi, 1)
                if n >= LAG:
                    m = n - LAG
                    act.wait_ge(scaled, m + 1)
                    wait(act, down_done, m - 2)
                    nc.scalar.activation(hid[0][0:size(m), m % 3, :], full[0:size(m), m % 4, :], ACT.Copy)\
                        .then_inc(hid_hi, 1)
                if n + 2 < blocks:
                    split(n + 2)

        @block.gpsimd
        def _(pool):
            for n in range(blocks):
                y = slice(n * 128, n * 128 + size(n))
                for k, (hi, lo, raw) in enumerate((
                        (wide[0][:, n % 3, 0, :, 0:size(n)], wide[1][:, n % 3, 0, :, 0:size(n)], weights.gate[:, :, y]),
                        (wide[0][:, n % 3, 1, :, 0:size(n)], wide[1][:, n % 3, 1, :, 0:size(n)], weights.up[:, :, y]),
                        (wd[0][0:size(n), n % 6], wd[1][0:size(n), n % 6], weights.down[0:size(n), n, :]))):
                    pool.wait_ge(w_hi, NW * n + k + 1)
                    nc.gpsimd.tensor_tensor(lo, raw, hi.bitcast(F32), ALU.subtract).then_inc(w_lo, 1)

        @block.vector
        def _(dve):
            step = [0]

            def then(ins):
                step[0] += 1
                ins.then_inc(r, 1)
                dve.wait_ge(r, step[0])

            then(nc.vector.memset(zero[:], 0.0))
            dve.wait_ge(lg_done, 1)
            then(nc.vector.tensor_copy(logit[:, :, 0:nl], scale[0:TP, 0, 0:TT * 16].rearrange("p (t n) -> p t n", n=16)[:, :, 0:nl]))
            then(nc.vector.tensor_reduce(mx[:], logit[:, :, 0:E], AX, ALU.max))
            then(nc.vector.tensor_tensor(prob[:], logit[:, :, 0:E], mx[:].unsqueeze(2).to_broadcast([TP, TT, E]),
                                         ALU.subtract))
            dve.wait_ge(act_r, 1)
            then(nc.vector.tensor_reduce(tot[:], prob[:], AX, ALU.add))
            then(nc.vector.reciprocal(tot[:], tot[:]))
            then(nc.vector.tensor_tensor(prob[:], prob[:], tot[:].unsqueeze(2).to_broadcast([TP, TT, E]), ALU.mult))
            for t in range(TT):
                mine = prob[:, t, :].unsqueeze(2).to_broadcast([TP, E, E])
                other = prob[:, t, :].unsqueeze(1).to_broadcast([TP, E, E])
                then(nc.vector.tensor_tensor(rank[:, t], other, mine, ALU.is_gt))
                then(nc.vector.tensor_tensor(same[:, t], other, mine, ALU.is_equal))
                then(nc.vector.tensor_tensor(same[:, t], same[:, t], before[0:TP], ALU.mult))
            then(nc.vector.tensor_tensor(rank[:], rank[:], same[:], ALU.add))
            then(nc.vector.tensor_reduce(place[:], rank[:], AX, ALU.add))
            then(nc.vector.tensor_scalar(place[:], place[:], 1.5, None, ALU.is_lt))
            then(nc.vector.tensor_tensor(comb[:, :, 0:E], place[:], prob[:], ALU.mult))
            if normalise:
                then(nc.vector.tensor_reduce(tot[:], comb[:, :, 0:E], AX, ALU.add))
                then(nc.vector.reciprocal(tot[:], tot[:]))
                then(nc.vector.tensor_tensor(comb[:, :, 0:E], comb[:, :, 0:E],
                                             tot[:].unsqueeze(2).to_broadcast([TP, TT, E]), ALU.mult))
            if shared_gate:
                dve.wait_ge(act_r, 2)
                then(nc.vector.tensor_scalar(share[:], share[:], 1.0, None, ALU.add))
                then(nc.vector.reciprocal(comb[:, :, E], share[:]))
            else:
                then(nc.vector.memset(comb[:, :, E:E + 1], 1.0))

            assert step[0] == route_steps

            def hidden(n):
                dve.wait_ge(silu_done, n + 1)
                wait(dve, hid_lo, n - 3)
                nc.vector.tensor_tensor(full[0:size(n), n % 4, :], silu[0:size(n), n % 2, :],
                                        up[0:size(n), n % 2, 0:NTOK], ALU.mult).then_inc(hid_done, 1)

            for n in range(blocks + LAG):
                if n < blocks:
                    hidden(n)
                if n == 1:
                    dve.wait_ge(comb_hi, 1)
                    nc.vector.tensor_tensor(combT[1][:], scale[0:E + 1, 1, 0:NTOK], combT[0][:].bitcast(F32),
                                            ALU.subtract).then_inc(comb_lo, 1)
                if n >= LAG:
                    m = n - LAG
                    y = full[0:size(m), m % 4, :]
                    dve.wait_ge(scale_done, m + 1)
                    nc.vector.tensor_tensor(y, y, scale[0:size(m), m % 2, 0:NTOK], ALU.mult).then_inc(scaled, 1)
                    dve.wait_ge(hid_hi, m + 1)
                    nc.vector.tensor_tensor(hid[1][0:size(m), m % 3, :], y, hid[0][0:size(m), m % 3, :].bitcast(F32),
                                            ALU.subtract).then_inc(hid_lo, 1)
            dve.wait_ge(down_done, blocks)
            for t in range(TT):
                nc.vector.tensor_tensor(x[:, t, :], x[:, t, :], down[0:TP, t // 2, (t % 2) * D:(t % 2 + 1) * D],
                                        ALU.add).then_inc(added, 1)
            dve.wait_ge(added, TT)


def key_value_sums(nc, kv, ctxT_dram, mask_dram, wk_dram, bk_dram, wv_dram, bv_dram, wf_dram):
    with ExitStack() as ctx:
        p = Phase(nc, ctx, "kvs")
        wk = [p.sb(f"wk{i}", [128, DC, D], F32R) for i in range(2)]
        wv = [p.sb(f"wv{i}", [128, DC, D], F32R) for i in range(2)]
        raw_w = p.sb("raw_w", [128, 2, DC, D])
        fmap = p.sb("fmap", [128, D])
        f2 = p.sb("f2", [128, 2, D], F32R)
        bk = p.sb("bk", [128, DC])
        bv = p.sb("bv", [KP, D])
        zero = p.sb("zero", [128, 1])
        masks = p.sb("masks", [KP, B * KT])
        mask2 = p.sb("mask2", [KP, B * KT, 2], F32R)
        raw = p.sb("raw", [128, KC, DC, CH])
        ct = [p.sb(f"ct{i}", [128, KC, DC, CH], F32R) for i in range(2)]
        ks = p.sb("ks", [128, KC, 4, CH], F32R)
        vb = p.sb("vb", [KP, 2, KG * GV])
        vs = p.sb("vs", [KP, 2, KG, VW], F32R)
        kp = [p.sb(f"kp{i}", [KP, 2, FEAT], F32R) for i in range(2)]
        keys_ps = p.ps("keys_ps", [128, DC, 512])
        vals_ps = p.ps("vals_ps", [128, 512])
        feat = p.ps("feat", [128, 2, 512])
        sums = p.ps("sums", [128, 3, 512])

        zeros = p.sb("zeros", [KP, KG, 2])
        w_loaded, w_hi, w_lo = p.sem("w_loaded"), p.sem("w_hi"), p.sem("w_lo")
        zeros_set = p.sem("zeros_set")
        const_loaded, fmap_set, f_loaded, f_hi_done, f_split, m_loaded, m_hi, m_lo, vb_set = (p.sem(s) for s in (
            "const_loaded", "fmap_set", "f_loaded", "f_hi_done", "f_split", "m_loaded", "m_hi", "m_lo", "vb_set"))
        loaded = [p.sem(f"loaded{c}") for c in range(KC)]
        t_hi, t_lo, k_done, ks_hi, ks_lo = (p.sem(s) for s in ("t_hi", "t_lo", "k_done", "ks_hi", "ks_lo"))
        v_done, vb_done, v_hi, v_lo, v_mask = (p.sem(s) for s in ("v_done", "vb_done", "v_hi", "v_lo", "v_mask"))
        feat_done, f_hi, f_lo, sums_done, kv_done = (p.sem(s) for s in (
            "feat_done", "f_hi", "f_lo", "sums_done", "kv_done"))
        block = ctx.enter_context(nc.Block())
        NB = len(SUMS)

        def at_batch(b, t):
            return slice(b * KT + t, b * KT + t + 1) if isinstance(b, int) else bass.ds(b * KT + t, 1)

        def chunk_after(b, t):
            if t % TPC not in (1, 2):
                return None
            c = t // TPC + 1
            return (b, c, t % TPC - 1) if c < KC else (b + 1, 0, t % TPC - 1)

        def chunk_to_split(b, t):
            if t % TPC != TPC - 1:
                return None
            c = t // TPC + 2
            return (b, c) if c < KC else (b + 1, c - KC)

        def passes(b, last):
            for t in range(KT):
                project, split = chunk_after(b, t), chunk_to_split(b, t)
                wraps = t // TPC + 1 >= KC, t // TPC + 2 >= KC
                yield (t, None if last and wraps[0] else project, None if last and wraps[1] else split)

        def run_peeled(eng, batch):
            batch(0, True, False)
            with eng.Fori(1, B - 1) as b:
                batch(b, False, False)
            batch(B - 1, False, True)

        def sums_of(b, i):
            lo, hi = SUMS[i]
            if isinstance(b, int):
                return kv[:, b, lo:hi], sums[0:VW, i, 0:hi - lo]
            return kv[:, bass.ds(b, 1), lo:hi], sums[0:VW, i:i + 1, 0:hi - lo]

        @block.sync
        def _(sp):
            def load(b, c):
                wait(sp, t_lo, (b - 1) * KC + c + 1)
                src = ctxT_dram[bass.ds(b, 1), :, c * CH:(c + 1) * CH] if not isinstance(b, int) else \
                    ctxT_dram[b:b + 1, :, c * CH:(c + 1) * CH]
                sp.dma_start(raw[:, c], src.rearrange("a (k p) n -> p (a k) n", p=128)).then_inc(loaded[c], 16)

            load(0, 0)
            sp.dma_start(raw_w[:, 0], wk_dram.rearrange("(c p) n -> p c n", p=128)).then_inc(w_loaded, 16)
            sp.dma_start(raw_w[:, 1], wv_dram.rearrange("(c p) n -> p c n", p=128)).then_inc(w_loaded, 16)
            sp.dma_start(bk[:], bk_dram).then_inc(const_loaded, 16)
            sp.dma_start(bv[:], bv_dram.partition_broadcast(KP)).then_inc(const_loaded, 16)
            sp.dma_start(masks[:], mask_dram).then_inc(m_loaded, 16)
            sp.wait_ge(fmap_set, 1)
            for h in range(8):
                i = h % 4
                sp.dma_start(fmap[16 * h:16 * h + 16, FD * i:FD * (i + 1)], wf_dram).then_inc(f_loaded, 16)
            for c in range(1, KC):
                load(0, c)
            with sp.Fori(1, B) as b:
                for c in range(KC):
                    load(b, c)

        @block.tensor
        def _(pe):
            def keys(b, c, m):
                wait(pe, t_lo, b * KC + c + 1)
                wait(pe, ks_lo, 4 * (b * KC + c - 1) + 2 * (m + 1))
                for i in range(DC):
                    last = mm3(nc, keys_ps[:, m, 0:CH], wk[0][:, i, m * 128:(m + 1) * 128],
                               wk[1][:, i, m * 128:(m + 1) * 128], ct[0][:, c, i, :], ct[1][:, c, i, :],
                               i == 0, i == DC - 1)
                last.then_inc(k_done, 1)

            def values(b, t):
                c, i = divmod(t, TPC)
                x = slice(i * KP, (i + 1) * KP)
                wait(pe, vb_done, b * KT + t)
                for k in range(DC):
                    last = mm3(nc, vals_ps[0:KP, 0:D], ct[0][:, c, k, x], ct[1][:, c, k, x],
                               wv[0][:, k, :], wv[1][:, k, :], k == 0, k == DC - 1)
                last.then_inc(v_done, 1)

            def features(b, t):
                c, i = divmod(t, TPC)
                x = slice(i * KP, (i + 1) * KP)
                wait(pe, ks_lo, 4 * (b * KC + c + 1))
                for half in range(2):
                    wait(pe, f_lo, 2 * (b * KT + t - 1) + half + 1)
                    for g in range(2):
                        y = slice(g * D, (g + 1) * D)
                        for w in (1, 0):
                            last = nc.tensor.matmul(feat[0:KP, half, y], ks[:, c, 2 * half + g, x], f2[:, w, :],
                                                    start=(w == 1), stop=(w == 0), skip_group_check=True)
                    last.then_inc(feat_done, 1)

            def add(b, t):
                n = b * KT + t
                wait(pe, v_lo, n + 1)
                wait(pe, v_mask, n + 1)
                wait(pe, f_lo, 2 * n + 2)
                for g in range(KG):
                    if t == 0 and g % 2 == 0:
                        wait(pe, kv_done, NB * (b - 1) + g // 2 + 1)
                    w = min(GF, FEAT - g * GF)
                    for half in (1, 0):
                        last = nc.tensor.matmul(sums[0:VW, g // 2, (g % 2) * GF:(g % 2) * GF + w],
                                                vs[:, t % 2, g, :], kp[half][:, t % 2, g * GF:g * GF + w],
                                                start=(t == 0 and g % 2 == 0 and half == 1),
                                                stop=(t == KT - 1 and g % 2 == 1 and half == 0),
                                                skip_group_check=True)
                last.then_inc(sums_done, 1)

            def batch(b, first, last):
                for t, project, _ in passes(b, last):
                    values(b, t)
                    features(b, t)
                    if t >= 1:
                        add(b, t - 1)
                    elif not first:
                        add(b - 1, KT - 1)
                    if project is not None:
                        keys(*project)

            pe.wait_ge(w_lo, 2)
            for m in range(DC):
                keys(0, 0, m)
            pe.wait_ge(f_split, 2)
            run_peeled(pe, batch)
            add(B - 1, KT - 1)

        @block.scalar
        def _(act):
            def split(b, c):
                wait(act, loaded[c], 16 * (b + 1))
                wait(act, v_done, (b - 1) * KT + TPC * (c + 1))
                nc.scalar.activation(ct[0][:, c], raw[:, c], ACT.Copy).then_inc(t_hi, 1)

            def keys(b, c, m):
                wait(act, k_done, 2 * (b * KC + c) + m + 1)
                wait(act, feat_done, 2 * ((b - 1) * KT + TPC * (c + 1)))
                for h in range(2):
                    x = slice(64 * h, 64 * (h + 1))
                    nc.scalar.activation(ks[0:64, c, 2 * m + h, :], keys_ps[x, m, 0:CH], ACT.Identity,
                                         bias=bk[x, m:m + 1]).then_inc(ks_hi, 1)

            def take_sums(b):
                wait(act, sums_done, (b + 1) * KT)
                for i in range(NB):
                    nc.scalar.activation(*sums_of(b, i), ACT.Copy).then_inc(kv_done, 1)

            def batch(b, first, last):
                for t, project, to_split in passes(b, last):
                    n = b * KT + t
                    wait(act, sums_done, n - 1)
                    for half in range(2):
                        wait(act, feat_done, 2 * n + half + 1)
                        nc.scalar.activation(kp[0][:, t % 2, half * 512:(half + 1) * 512], feat[0:KP, half, :],
                                             ACT.Relu, bias=zero[0:KP, 0:1]).then_inc(f_hi, 1)
                    wait(act, vb_done, n + 1)
                    nc.scalar.activation(vs[:, t % 2, :, 0:GV], vb[:, t % 2, :].rearrange("p (g v) -> p g v", v=GV),
                                         ACT.Copy, scale=masks[:, at_batch(b, t)]).then_inc(v_hi, 1)
                    if t == 0 and not first:
                        take_sums(b - 1)
                    if project is not None:
                        keys(*project)
                    if to_split is not None:
                        split(*to_split)

            split(0, 0)
            act.wait_ge(w_loaded, 32)
            for i, w in enumerate((wk, wv)):
                nc.scalar.activation(w[0][:], raw_w[:, i], ACT.Copy).then_inc(w_hi, 1)
            act.wait_ge(f_loaded, 16 * 8)
            nc.scalar.activation(f2[:, 0, :], fmap[:], ACT.Copy).then_inc(f_hi_done, 1)
            act.wait_ge(m_loaded, 16)
            act.wait_ge(const_loaded, 32)
            act.wait_ge(vb_set, 2)
            for m in range(DC):
                keys(0, 0, m)
            split(0, 1)
            run_peeled(act, batch)
            take_sums(B - 1)
            act.wait_ge(kv_done, NB * B)

        @block.vector
        def _(dve):
            def keys(b, c, m):
                for h in range(2):
                    x = slice(64 * h, 64 * (h + 1))
                    wait(dve, ks_hi, 4 * (b * KC + c) + 2 * m + h + 1)
                    nc.vector.scalar_tensor_tensor(ks[64:128, c, 2 * m + h, :], keys_ps[x, m, 0:CH],
                                                   bk[x, m:m + 1], ks[0:64, c, 2 * m + h, :].bitcast(F32),
                                                   ALU.add, ALU.subtract).then_inc(ks_lo, 1)

            def batch(b, first, last):
                for t, project, to_split in passes(b, last):
                    n = b * KT + t
                    wait(dve, v_done, n + 1)
                    wait(dve, v_lo, n - 1)
                    nc.vector.tensor_tensor(vb[:, t % 2, 0:D], vals_ps[0:KP, 0:D], bv[:], ALU.add).then_inc(vb_done, 1)
                    for half in range(2):
                        wait(dve, f_hi, 2 * n + half + 1)
                        y = slice(half * 512, (half + 1) * 512)
                        nc.vector.scalar_tensor_tensor(kp[1][:, t % 2, y], feat[0:KP, half, :], 0.0,
                                                       kp[0][:, t % 2, y].bitcast(F32), ALU.max,
                                                       ALU.subtract).then_inc(f_lo, 1)
                    wait(dve, v_hi, n + 1)
                    nc.vector.scalar_tensor_tensor(vs[:, t % 2, :, GV:2 * GV],
                                                   vb[:, t % 2, :].rearrange("p (g v) -> p g v", v=GV),
                                                   masks[:, at_batch(b, t)], vs[:, t % 2, :, 0:GV].bitcast(F32),
                                                   ALU.mult, ALU.subtract).then_inc(v_lo, 1)
                    if project is not None:
                        keys(*project)

            nc.vector.memset(vb[:], 0.0).then_inc(vb_set, 1)
            nc.vector.memset(zero[:], 0.0).then_inc(vb_set, 1)
            dve.wait_ge(vb_set, 2)
            for i, w in enumerate((wk, wv)):
                dve.wait_ge(w_hi, i + 1)
                nc.vector.tensor_tensor(w[1][:], raw_w[:, i], w[0][:].bitcast(F32), ALU.subtract).then_inc(w_lo, 1)
            nc.vector.memset(f2[64:128, 1, :].bitcast(F32), 0.0).then_inc(f_split, 1)
            dve.wait_ge(f_hi_done, 1)
            nc.vector.tensor_tensor(f2[0:64, 1, :], fmap[0:64, :], f2[0:64, 0, :].bitcast(F32),
                                    ALU.subtract).then_inc(f_split, 1)
            for m in range(DC):
                keys(0, 0, m)
            run_peeled(dve, batch)

        @block.gpsimd
        def _(pool):
            nc.gpsimd.memset(fmap[:], 0.0).then_inc(fmap_set, 1)
            def split(b, c):
                wait(pool, t_hi, b * KC + c + 1)
                nc.gpsimd.tensor_tensor(ct[1][:, c], raw[:, c], ct[0][:, c].bitcast(F32), ALU.subtract).then_inc(t_lo, 1)

            split(0, 0)
            pool.wait_ge(m_loaded, 16)
            nc.gpsimd.tensor_copy(mask2[:, :, 0], masks[:]).then_inc(m_hi, 1)
            pool.wait_ge(m_hi, 1)
            nc.gpsimd.tensor_tensor(mask2[:, :, 1], masks[:], mask2[:, :, 0].bitcast(F32), ALU.subtract).then_inc(m_lo, 1)
            nc.gpsimd.memset(zeros[:], 0.0).then_inc(zeros_set, 1)
            pool.wait_ge(zeros_set, 1)
            pool.wait_ge(m_lo, 1)

            def batch(b, first, last):
                for t, _, to_split in passes(b, last):
                    wait(pool, sums_done, b * KT + t - 1)
                    nc.gpsimd.tensor_tensor(vs[:, t % 2, :, 2 * GV:VW],
                                            mask2[:, at_batch(b, t), :].bitcast(F32).to_broadcast([KP, KG, 2]),
                                            zeros[:], ALU.add).then_inc(v_mask, 1)
                    if to_split is not None:
                        split(*to_split)

            split(0, 1)
            run_peeled(pool, batch)


def linear_readout(nc, x, xnT, kv, wq_dram, bq_dram, wf_dram, wo_dram, bo_dram, ident, following):
    with ExitStack() as ctx:
        p = Phase(nc, ctx, "lin")
        wq = p.sb("wq", [128, DC, D])
        wo = p.sb("wo", [128, DC, D])
        fmap = p.sb("fmap", [128, 4, 128])
        bq = p.sb("bq", [128, DC])
        bo = p.sb("bo", [TP, D])
        qT = p.sb("qT", [128, DC, NTOK])
        qf = p.sb("qf", [128, NH // 2, NTOK])
        low = p.sb("low", [128, 2, NH // 2, GV + 2])
        kvd = p.sb("kvd", [128, 2, NH // 2, 2 * RV])
        den = p.sb("den", [S, B, NH])
        att = p.sb("att", [S, B, D])
        attT = p.sb("attT", [128, DC, NTOK])
        zero = p.sb("zero", [128, 1])
        q_ps = p.ps("q_ps", [128, 2, 512])
        kv_ps = p.ps("kv_ps", [128, 2, 2, 4, 128])
        out_ps = p.ps("out_ps", [128, 2, 512])

        set0, loaded, f_loaded, out_loaded = (p.sem(s) for s in ("set0", "loaded", "f_loaded", "out_loaded"))
        q_done, qT_done, qf_ps, qf_done, kv_full, low_done, kvd_done = (p.sem(s) for s in (
            "q_done", "qT_done", "qf_ps", "qf_done", "kv_full", "low_done", "kvd_done"))
        ND = 2 * (GH + 1)
        read_done, den_done, att_done, t_done, attT_done, y_done, added = (p.sem(s) for s in (
            "read_done", "den_done", "att_done", "t_done", "attT_done", "y_done", "added"))
        block = ctx.enter_context(nc.Block())

        @block.sync
        def _(sp):
            sp.dma_start(wq[:], wq_dram.rearrange("(c p) n -> p c n", p=128)).then_inc(loaded, 16)
            sp.dma_start(bq[:], bq_dram).then_inc(loaded, 16)
            sp.wait_ge(set0, 3)
            for h in range(8):
                sp.dma_start(fmap[16 * h:16 * h + 16, h // 2, FD * (h % 2):FD * (h % 2 + 1)], wf_dram)\
                    .then_inc(f_loaded, 16)
            sp.dma_start(wo[:], wo_dram.rearrange("(c p) n -> p c n", p=128)).then_inc(out_loaded, 16)
            sp.dma_start(bo[:], bo_dram.partition_broadcast(TP)).then_inc(out_loaded, 16)
            following.load(sp)

        @block.gpsimd
        def _(pool):
            nc.gpsimd.memset(fmap[:], 0.0).then_inc(set0, 1)
            nc.gpsimd.memset(kvd[:], 0.0).then_inc(set0, 1)
            nc.gpsimd.memset(zero[:], 0.0).then_inc(set0, 1)
            following.set_member(pool)

        @block.tensor
        def _(pe):
            def turn_sums(b):
                wait(pe, kvd_done, ND * (b - 1))
                for j in range(NH // 2):
                    last = nc.tensor.transpose(kv_ps[:, b % 2, j // 4, j % 4, 0:VW],
                                               kv[:, b, j * 2 * FD:(j + 1) * 2 * FD], ident[0:VW, 0:VW])
                last.then_inc(kv_full, 1)

            turn_sums(0)
            turn_sums(1)
            pe.wait_ge(loaded, 32)
            for m in range(DC):
                for c in range(DC):
                    last = nc.tensor.matmul(q_ps[:, m, 0:NTOK], wq[:, c, m * 128:(m + 1) * 128], xnT[:, c, :],
                                            start=(c == 0), stop=(c == DC - 1))
                last.then_inc(q_done, 1)
            pe.wait_ge(f_loaded, 16 * 8)
            pe.wait_ge(qT_done, DC)
            for j in range(NH // 2):
                wait(pe, qf_done, j - 1)
                nc.tensor.matmul(q_ps[:, j % 2, 0:NTOK], fmap[:, j % 4, :], qT[:, j // 4, :],
                                 start=True, stop=True).then_inc(qf_ps, 1)
            def read(b):
                wait(pe, kvd_done, ND * (b + 1))
                wait(pe, qf_done, NH // 2)
                wait(pe, att_done, b - 1)
                for j in range(NH // 2):
                    last = nc.tensor.matmul(out_ps[0:S, b % 2, j * 2 * RV:(j + 1) * 2 * RV],
                                            qf[:, j, b * S:(b + 1) * S], kvd[:, b % 2, j, :], start=True, stop=True)
                last.then_inc(read_done, 1)

            def turn(b):
                wait(pe, att_done, b + 1)
                for c in range(DC):
                    last = nc.tensor.transpose(q_ps[:, c, b * S:(b + 1) * S], att[:, b, c * 128:(c + 1) * 128],
                                               ident[0:S, 0:S])
                last.then_inc(t_done, 1)

            for b in range(B + 2):
                if 2 <= b < B:
                    turn_sums(b)
                if 1 <= b <= B:
                    read(b - 1)
                if b >= 2:
                    turn(b - 2)
            pe.wait_ge(attT_done, DC)
            pe.wait_ge(out_loaded, 32)
            for t in range(TT):
                wait(pe, added, 2 * (t - 1))
                for c in range(DC):
                    last = nc.tensor.matmul(out_ps[0:TP, t % 2, 0:D], attT[:, c, t * TP:(t + 1) * TP], wo[:, c, :],
                                            start=(c == 0), stop=(c == DC - 1))
                last.then_inc(y_done, 1)

        @block.scalar
        def _(act):
            def take_low(b):
                act.wait_ge(kv_full, b + 1)
                wait(act, kvd_done, ND * (b - 1))
                nc.scalar.activation(low[:, b % 2], kv_ps[:, b % 2].rearrange("p a j n -> p (a j) n")[:, :, GV:VW],
                                     ACT.Copy).then_inc(low_done, 1)

            act.wait_ge(set0, 3)
            take_low(0)
            take_low(1)
            act.wait_ge(loaded, 32)
            for m in range(DC):
                act.wait_ge(q_done, m + 1)
                nc.scalar.activation(qT[:, m, :], q_ps[:, m, 0:NTOK], ACT.Identity, bias=bq[:, m:m + 1]).then_inc(qT_done, 1)
            for j in range(NH // 2):
                act.wait_ge(qf_ps, j + 1)
                nc.scalar.activation(qf[:, j, :], q_ps[:, j % 2, 0:NTOK], ACT.Relu, bias=zero[:, 0:1]).then_inc(qf_done, 1)
            for b in range(2, B):
                take_low(b)

        @block.vector
        def _(dve):
            dve.wait_ge(set0, 3)

            def diagonal(b):
                dve.wait_ge(low_done, b + 1)
                wait(dve, read_done, b - 1)
                src = kv_ps[:, b % 2].rearrange("p a j n -> p (a j) n")
                for i in range(2):
                    r = slice(64 * i, 64 * (i + 1))
                    for m in range(GH):
                        v = (2 * m + i) % GH * HE
                        nc.vector.tensor_tensor(kvd[r, b % 2, m::GH, RV * i:RV * i + HE],
                                                low[r, b % 2, m::GH, v:v + HE], src[r, m::GH, v:v + HE],
                                                ALU.add).then_inc(kvd_done, 1)
                    nc.vector.tensor_tensor(kvd[r, b % 2, :, RV * i + HE:RV * (i + 1)], low[r, b % 2, :, GV + 1:GV + 2],
                                            src[r, :, 2 * GV:2 * GV + 1], ALU.add).then_inc(kvd_done, 1)

            def divide(b):
                dve.wait_ge(read_done, b + 1)
                o = out_ps[0:S, b % 2, 0:NH * RV].rearrange("p (h n) -> p h n", n=RV)
                nc.vector.tensor_scalar(den[:, b, :], o[:, :, HE], 1e-8, None, ALU.add).then_inc(den_done, 1)
                dve.wait_ge(den_done, 2 * b + 1)
                nc.vector.reciprocal(den[:, b, :], den[:, b, :]).then_inc(den_done, 1)
                dve.wait_ge(den_done, 2 * b + 2)
                nc.vector.tensor_tensor(att[:, b, :].rearrange("p (h n) -> p h n", n=HE), o[:, :, 0:HE],
                                        den[:, b, :].unsqueeze(2).to_broadcast([S, NH, HE]), ALU.mult).then_inc(att_done, 1)

            for b in range(B + 1):
                if b < B:
                    diagonal(b)
                if b >= 1:
                    divide(b - 1)
            dve.wait_ge(t_done, B)
            for c in range(DC):
                nc.vector.tensor_copy(attT[:, c, :], q_ps[:, c, 0:NTOK]).then_inc(attT_done, 1)
            dve.wait_ge(out_loaded, 32)
            for t in range(TT):
                dve.wait_ge(y_done, t + 1)
                nc.vector.tensor_tensor(x[:, t, :], x[:, t, :], out_ps[0:TP, t % 2, 0:D], ALU.add).then_inc(added, 1)
                dve.wait_ge(added, 2 * t + 1)
                nc.vector.tensor_tensor(x[:, t, :], x[:, t, :], bo[:], ALU.add).then_inc(added, 1)
            dve.wait_ge(added, 2 * TT)


def build(nc, a, out):
    with ExitStack() as ctx:
        p = Phase(nc, ctx, "all")
        x = p.sb("x", [TP, TT, D])
        xnT = p.sb("xnT", [128, DC, NTOK])
        ident = p.sb("ident", [128, 128])
        before = p.sb("before", [128, E, E])
        x_loaded, zeroed, consts, stored = p.sem("x_loaded"), p.sem("zeroed"), p.sem("consts"), p.sem("stored")

        with nc.Block() as block:
            @block.gpsimd
            def _(pool):
                identity(nc, pool, ident[:], 128, zeroed, consts)
                nc.gpsimd.memset(before[:], 1.0).then_inc(zeroed, 1)
                pool.wait_ge(zeroed, 2)
                nc.gpsimd.affine_select(out=before[:], in_=before[:], compare_op=ALU.is_gt, fill=0.0, base=0,
                                        pattern=[[1, E], [-1, E]], channel_multiplier=0).then_inc(consts, 1)
                pool.wait_ge(consts, 2)

            @block.sync
            def _(sp):
                sp.dma_start(x[:], a["x"].rearrange("(t p) d -> p t d", p=TP)).then_inc(x_loaded, 16)
                sp.wait_ge(x_loaded, 16)

        with ExitStack() as heads:
            h = Phase(nc, heads, "heads")
            qT = h.sb("qT", [128, NH, NTOK])
            rz = h.sb("rz", [TP, B * NJ])
            with ExitStack() as attention:
                h = Phase(nc, attention, "attention")
                wk = [h.sb(f"wk{i}", [128, DC, G * HD], F32R) for i in range(2)]
                wv = [h.sb(f"wv{i}", [128, DC, G * HD], F32R) for i in range(2)]
                ct = [h.sb(f"ct{i}", [128, DC, SK], F32R) for i in range(2)]
                raw_t = h.sb("raw_t", [128, DC, SK])
                with ExitStack() as before_attention:
                    h = Phase(nc, before_attention, "q")
                    xn = [h.sb(f"xn{i}", [128, DC, NTOK], F32R) for i in range(2)]
                    raw_w = [h.sb(f"raw_w{i}", [128, DC, G * HD]) for i in range(2)]
                    splits = [(dram.rearrange("(c p) n -> p c n", p=128), raw[:], w[0][:], w[1][:])
                              for dram, raw, w in ((a["wk0"], raw_w[0], wk), (a["wv0"], raw_w[1], wv))]
                    for c in range(KC):
                        y = slice(c * CH, (c + 1) * CH)
                        splits.append((a["ctxT"][0, :, y].rearrange("(c p) n -> p c n", p=128), raw_t[:, :, y],
                                       ct[0][:, :, y], ct[1][:, :, y]))
                    layernorm_transposed(nc, "ln0", x, xnT, ident, xn)
                    queries(nc, xn, qT, a["wq0"], a["qnorm"], a["knorm"], splits)
                softmax_attention(nc, qT, rz, a["ctx"], a["ctxT"], wk, wv, raw_t, ct, ident)
            w0 = Weights(nc, heads, "w0", (a["gate0"], a["up0"], a["down0"], a["router0"]), SHARED0, E)
            attention_output(nc, x, qT, rz, a["wo0"], ident, w0)
            xn = [Phase(nc, heads, "m0").sb(f"xn{i}", [128, DC, NTOK], F32R) for i in range(2)]
            layernorm_transposed(nc, "ln1", x, xnT, ident, xn)
            mixture(nc, "moe0", x, xnT, xn, w0, before, ident, False)

        with ExitStack() as linear:
            h = Phase(nc, linear, "linear")
            kv = h.sb("kv", [VW, B, FEAT])
            key_value_sums(nc, kv, a["ctxT"], a["mask"], a["wk1"], a["bk1"], a["wv1"], a["bv1"], a["wkf"])
            w1 = Weights(nc, linear, "w1", (a["gate1"], a["up1"], a["down1"], a["router1"]), SHARED1, E + 1)
            layernorm_transposed(nc, "ln2", x, xnT, ident)
            linear_readout(nc, x, xnT, kv, a["wq1"], a["bq1"], a["wqf"], a["wo1"], a["bo1"], ident, w1)
            xn = [h.sb(f"xn{i}", [128, DC, NTOK], F32R) for i in range(2)]
            layernorm_transposed(nc, "ln3", x, xnT, ident, xn)
            mixture(nc, "moe1", x, xnT, xn, w1, before, ident, True, shared_gate=True)

        with nc.Block() as block:
            @block.sync
            def _(sp):
                sp.dma_start(out.rearrange("(t p) d -> p t d", p=TP), x[:]).then_inc(stored, 16)
                sp.wait_ge(stored, 16)


def kernel(**inputs):
    import numpy as np
    from concourse import bacc
    from concourse.bass_utils import run_bass_kernel_spmd

    g = {k: np.asarray(v) for k, v in inputs.items()}
    moe1 = g["L1_ffn_gate_up_proj"].transpose(0, 2, 1)
    hidden = moe1.shape[2] // 2

    def columns(w, shared):
        return np.concatenate([w.transpose(1, 0, 2).reshape(D, -1), shared], axis=1)

    arrays = {
        "x": g["x"].reshape(NTOK, D),
        "ctx": g["ctx_2048"],
        "ctxT": g["ctx_2048"].transpose(0, 2, 1),
        "mask": g["mask_BxS2_ff1"].reshape(B, KT, KP).transpose(2, 0, 1).reshape(KP, B * KT),
        "wq0": g["L0_xattn_Wq"], "wk0": g["L0_xattn_Wk"], "wv0": g["L0_xattn_Wv"], "wo0": g["L0_xattn_Wo"],
        "qnorm": g["L0_xattn_q_norm_w"].reshape(HD, 1), "knorm": g["L0_xattn_k_norm_w"].reshape(HD, 1),
        "router0": g["L0_ffn_gate_w"],
        "gate0": columns(g["L0_ffn_w_gate"], g["L0_ffn_sw_gate"]),
        "up0": columns(g["L0_ffn_w_up"], g["L0_ffn_sw_up"]),
        "down0": np.concatenate([g["L0_ffn_w_down"].reshape(-1, D), g["L0_ffn_sw_down"]]),
        "wq1": g["L1_xattn_Wq"].T, "wk1": g["L1_xattn_Wk"].T, "wv1": g["L1_xattn_Wv"].T, "wo1": g["L1_xattn_Wo"].T,
        "bq1": g["L1_xattn_bq"].reshape(DC, 128).T, "bk1": g["L1_xattn_bk"].reshape(DC, 128).T,
        "bv1": g["L1_xattn_bv"].reshape(1, D), "bo1": g["L1_xattn_bo"].reshape(1, D),
        "wqf": g["L1_xattn_Wqf"].T, "wkf": g["L1_xattn_Wkf"].T,
        "router1": np.concatenate([g["L1_ffn_router_weight"], g["L1_ffn_shared_gate_w"]]).T,
        "gate1": columns(moe1[:, :, :hidden], g["L1_ffn_sh_gate_w"].T),
        "up1": columns(moe1[:, :, hidden:], g["L1_ffn_sh_up_w"].T),
        "down1": np.concatenate([g["L1_ffn_down_proj"].transpose(0, 2, 1).reshape(-1, D), g["L1_ffn_sh_down_w"].T]),
    }
    nc = bacc.Bacc("TRN2", target_bir_lowering=False, num_devices=1)
    drams, feed = {}, {}
    for name, value in arrays.items():
        value = np.ascontiguousarray(value)
        feed[f"in_{name}"] = value
        drams[name] = nc.dram_tensor(f"in_{name}", value.shape, mybir.dt.from_np(value.dtype), kind="ExternalInput").ap()
    out = nc.dram_tensor("out", (NTOK, D), F32, kind="ExternalOutput").ap()
    build(nc, drams, out)
    got = run_bass_kernel_spmd(nc, [feed], core_ids=[0]).results[0]["out"]
    return got.reshape(B, S, D)
```
